# Optimizing a Trainium2 kernel written in Bass

```python
import numpy as np
import jax
import jax.numpy as jnp

def _softmax(x, axis=-1):
    return jax.nn.softmax(x, axis=axis)

def _gelu(x):
    return jax.nn.gelu(x, approximate=True)

def _silu(x):
    return jax.nn.silu(x)

def _sigmoid(x):
    return jax.nn.sigmoid(x)

def _layernorm(x, axis=-1, eps=1e-05):
    m = jnp.mean(x, axis=axis, keepdims=True)
    v = jnp.var(x, axis=axis, keepdims=True)
    return (x - m) / jnp.sqrt(v + eps)

def _scatter_add(tgt, idx, src, axis=0):
    return tgt.at[idx].add(src)

def _segment_sum(src, seg, n):
    return jax.ops.segment_sum(src, seg, n)
kernel_name = 'mk_seq_postln_d1_jaxref_r4_b520e2'

def setup_inputs(seed: int=0):
    np.random.seed(seed)
    _w = jnp.asarray

    def _L0_attn_setup():
        import jax, jax.numpy as jnp
        import numpy as np
        NUM_HEADS = 16

        def _sinusoid_rel_pos(seq_len, dim):
            pos = jnp.arange(seq_len - 1, -1, -1, dtype=jnp.float32)
            inv_freq = 1.0 / 10000.0 ** (jnp.arange(0, dim, 2, dtype=jnp.float32) / dim)
            ang = pos[:, None] * inv_freq[None, :]
            return jnp.concatenate([jnp.sin(ang), jnp.cos(ang)], axis=-1)

        def _rel_shift(x):
            B, H, S, L = x.shape
            x = jnp.pad(x, ((0, 0), (0, 0), (0, 0), (1, 0)))
            x = x.reshape(B, H, L + 1, S)
            return x[:, :, 1:S + 1, :]
        key = jax.random.key(seed)
        ks = jax.random.split(key, 8)
        B, S, C = (2, 512, 256)
        Dk, Dv, H = (256, 256, NUM_HEADS)
        dk = Dk // H
        scale = 0.02
        return {'x': jax.random.normal(ks[0], (B, S, C), dtype=jnp.float32), 'Wq': jax.random.normal(ks[1], (C, Dk), dtype=jnp.float32) * scale, 'Wk': jax.random.normal(ks[2], (C, Dk), dtype=jnp.float32) * scale, 'Wv': jax.random.normal(ks[3], (C, Dv), dtype=jnp.float32) * scale, 'u': jax.random.normal(ks[4], (H, dk), dtype=jnp.float32) * scale, 'v': jax.random.normal(ks[5], (H, dk), dtype=jnp.float32) * scale, 'Wo': jax.random.normal(ks[6], (Dv, C), dtype=jnp.float32) * scale, 'bo': jnp.zeros((C,), dtype=jnp.float32)}
    _L0_attn_in = _L0_attn_setup()

    def _L0_ffn_setup():
        import jax, jax.numpy as jnp
        import numpy as np
        B, S, D, F, E, K = (4, 512, 256, 1024, 8, 2)
        key = jax.random.key(seed)
        ks = jax.random.split(key, 8)
        x = jax.random.normal(ks[0], (B, S, D), dtype=jnp.float32)
        router_w = jax.random.normal(ks[1], (E, D), dtype=jnp.float32) * 0.02
        w1_w = jax.random.normal(ks[2], (E, F, D), dtype=jnp.float32) * 0.02
        w1_b = jax.random.normal(ks[3], (E, F), dtype=jnp.float32) * 0.02
        w2_w = jax.random.normal(ks[4], (E, D, F), dtype=jnp.float32) * 0.02
        w2_b = jax.random.normal(ks[5], (E, D), dtype=jnp.float32) * 0.02
        wg_w = jax.random.normal(ks[6], (E, F, D), dtype=jnp.float32) * 0.02
        wg_b = jax.random.normal(ks[7], (E, F), dtype=jnp.float32) * 0.02
        return {'x': x, 'router_w': router_w, 'w1_w': w1_w, 'w1_b': w1_b, 'w2_w': w2_w, 'w2_b': w2_b, 'wg_w': wg_w, 'wg_b': wg_b}
    _L0_ffn_in = _L0_ffn_setup()
    _d = {'L0_attn_x': _L0_attn_in['x'], 'L0_attn_Wq': _L0_attn_in['Wq'], 'L0_attn_Wk': _L0_attn_in['Wk'], 'L0_attn_Wv': _L0_attn_in['Wv'], 'L0_attn_u': _L0_attn_in['u'], 'L0_attn_v': _L0_attn_in['v'], 'L0_attn_Wo': _L0_attn_in['Wo'], 'L0_attn_bo': _L0_attn_in['bo'], 'L0_ffn_router_w': _L0_ffn_in['router_w'], 'L0_ffn_w1_w': _L0_ffn_in['w1_w'], 'L0_ffn_w1_b': _L0_ffn_in['w1_b'], 'L0_ffn_w2_w': _L0_ffn_in['w2_w'], 'L0_ffn_w2_b': _L0_ffn_in['w2_b'], 'L0_ffn_wg_w': _L0_ffn_in['wg_w'], 'L0_ffn_wg_b': _L0_ffn_in['wg_b']}
    _x0 = _d['L0_attn_x']
    _d['L0_attn_x'] = jax.random.normal(jax.random.fold_in(jax.random.key(seed), 1), (2, 2048, 256), dtype=_x0.dtype)
    del _x0
    return _d

def reference(L0_attn_x, L0_attn_Wq, L0_attn_Wk, L0_attn_Wv, L0_attn_u, L0_attn_v, L0_attn_Wo, L0_attn_bo, L0_ffn_router_w, L0_ffn_w1_w, L0_ffn_w1_b, L0_ffn_w2_w, L0_ffn_w2_b, L0_ffn_wg_w, L0_ffn_wg_b):

    def _L0_attn_ref(x, Wq, Wk, Wv, u, v, Wo, bo):
        import jax, jax.numpy as jnp
        import numpy as np
        NUM_HEADS = 16

        def _sinusoid_rel_pos(seq_len, dim):
            pos = jnp.arange(seq_len - 1, -1, -1, dtype=jnp.float32)
            inv_freq = 1.0 / 10000.0 ** (jnp.arange(0, dim, 2, dtype=jnp.float32) / dim)
            ang = pos[:, None] * inv_freq[None, :]
            return jnp.concatenate([jnp.sin(ang), jnp.cos(ang)], axis=-1)

        def _rel_shift(x):
            B, H, S, L = x.shape
            x = jnp.pad(x, ((0, 0), (0, 0), (0, 0), (1, 0)))
            x = x.reshape(B, H, L + 1, S)
            return x[:, :, 1:S + 1, :]
        B, S, C = x.shape
        H = NUM_HEADS
        dk = Wq.shape[1] // H
        dv = Wv.shape[1] // H
        Q = (x @ Wq).reshape(B, S, H, dk).transpose(0, 2, 1, 3)
        K = (x @ Wk).reshape(B, S, H, dk).transpose(0, 2, 1, 3)
        V = (x @ Wv).reshape(B, S, H, dv).transpose(0, 2, 1, 3)
        r = _sinusoid_rel_pos(S, dk)
        term1 = jnp.einsum('bhqd,bhkd->bhqk', Q, K)
        term2 = jnp.einsum('bhqd,kd->bhqk', Q, r)
        term3 = jnp.einsum('hd,bhkd->bhk', u, K)[:, :, None, :]
        term4 = jnp.einsum('hd,kd->hk', v, r)[None, :, None, :]
        scores = (term1 + term3 + _rel_shift(term2 + term4)) / jnp.sqrt(jnp.asarray(dk, dtype=x.dtype))
        attn = jax.nn.softmax(scores, axis=-1)
        out = jnp.einsum('bhqk,bhkd->bqhd', attn, V).reshape(B, S, H * dv)
        return out @ Wo + bo

    def _L0_ffn_ref(x, router_w, w1_w, w1_b, w2_w, w2_b, wg_w, wg_b):
        import jax, jax.numpy as jnp
        import numpy as np
        B, S, D, F, E, K = (4, 512, 256, 1024, 8, 2)
        probs = jax.nn.softmax(jnp.einsum('bsd,ed->bse', x, router_w), axis=-1)
        token_probs, probs_idx = jax.lax.top_k(probs, K)
        gates = jnp.sum(token_probs[..., None] * jax.nn.one_hot(probs_idx, E, dtype=x.dtype), axis=-2)
        gates_e = jnp.moveaxis(gates, -1, 0)

        def body(acc, params):
            w1w, w1b, w2w, w2b, wgw, wgb, g = params
            y = jax.nn.gelu(jnp.einsum('bsd,fd->bsf', x, wgw) + wgb, approximate=False)
            h = y * (jnp.einsum('bsd,fd->bsf', x, w1w) + w1b)
            out = jnp.einsum('bsf,df->bsd', h, w2w) + w2b
            return (acc + out * g[..., None], None)
        acc0 = jnp.zeros_like(x)
        out, _ = jax.lax.scan(body, acc0, (w1_w, w1_b, w2_w, w2_b, wg_w, wg_b, gates_e))
        return out
    x = L0_attn_x
    x = _layernorm(x + _L0_attn_ref(x, L0_attn_Wq, L0_attn_Wk, L0_attn_Wv, L0_attn_u, L0_attn_v, L0_attn_Wo, L0_attn_bo), axis=-1)
    x = _layernorm(x + _L0_ffn_ref(x, L0_ffn_router_w, L0_ffn_w1_w, L0_ffn_w1_b, L0_ffn_w2_w, L0_ffn_w2_b, L0_ffn_wg_w, L0_ffn_wg_b), axis=-1)
    return x

_drawn_inputs = setup_inputs


def setup_inputs(seed=0):
    import zlib

    import numpy as np

    out = dict(_drawn_inputs(seed))
    spreads = {'L0_attn_bo': (0.0, 0.1)}
    factors = {'L0_attn_Wq': 8.0,
     'L0_attn_Wk': 8.0,
     'L0_attn_Wv': 8.0,
     'L0_attn_u': 8.0,
     'L0_attn_v': 8.0,
     'L0_attn_Wo': 8.0,
     'L0_ffn_router_w': 6.263,
     'L0_ffn_w1_w': 6.256,
     'L0_ffn_w1_b': 8.0,
     'L0_ffn_w2_w': 6.243,
     'L0_ffn_w2_b': 31.796,
     'L0_ffn_wg_w': 6.405,
     'L0_ffn_wg_b': 8.0}
    for name, (base, spread) in spreads.items():
        noise = np.random.default_rng([zlib.crc32(name.encode()), seed]).standard_normal(out[name].shape)
        drawn = base * np.exp(spread * noise) if base else spread * noise
        out[name] = jnp.asarray(drawn.astype(out[name].dtype))
    for name, factor in factors.items():
        out[name] = (out[name] * factor).astype(out[name].dtype)
    return out
```

```python
from contextlib import ExitStack

import numpy as np

import concourse.bass as bass
from concourse import mybir

F32 = mybir.dt.float32
F16 = mybir.dt.float16
BF16 = mybir.dt.bfloat16
I32 = mybir.dt.int32
U32 = mybir.dt.uint32
ALU = mybir.AluOpType
ACT = mybir.ActivationFunctionType
AX = mybir.AxisListType.X

P = 128
B, S, C, H = 2, 2048, 256, 16
DK = C // H
CT = C // P
E, F = 8, 1024
FT = F // P
CH = 512
NCH = S // CH
QT = CH // P
KT = S // P
QUAD = 4
NQ = H // QUAD
NIT = B * NQ
NTOK = B * S
NT = NTOK // P
W = S + 8
BLK = 256
NBLK = NTOK * 2 // BLK + E
SCALE = 1.0 / float(DK) ** 0.5
NEG = -1.0e30
EPS = 1e-5
NSPLIT = 3 * 2 * DK
ONE_ROW = NSPLIT
BIG_ROWS = NSPLIT + 1


def constants():
    half = DK // 2
    expo = np.arange(0, DK, 2, dtype=np.float32) / np.float32(DK)
    freq = (np.float32(1.0) / np.power(np.float32(10000.0), expo).astype(np.float32)).astype(np.float64)
    tok = np.arange(S, dtype=np.float64)
    rot = np.zeros((P, 4, S), np.float32)
    for r in range(P):
        d = r % DK
        w = freq[d % half]
        for k, base in ((0, 0.0), (2, float(S))):
            ang = (tok + base) * w
            own = -np.cos(ang) if d < half else np.cos(ang)
            rot[r, k] = own
            rot[r, k + 1] = np.sin(ang)
    ang = tok[None, :] * freq[:, None]
    p = np.concatenate([np.sin(ang), np.cos(ang)], 0)
    hi = p.astype(np.float16)
    lo = (p - hi.astype(np.float64)).astype(np.float16)
    pk = np.stack([hi, lo])
    r, s = np.meshgrid(np.arange(P), np.arange(P), indexing="ij")
    gt, lt, eq = ((np.where(m, 0.0, NEG)) for m in (r > s, r < s, r == s))
    mask = np.concatenate([gt] * 4 + [lt] + [eq] * 4, 1).astype(np.float32)
    ident = np.eye(P, dtype=np.float32)
    before = (r < s).astype(np.float32)
    order = np.tile(np.arange(E, 0, -1, dtype=np.float32), (P, NT))
    return {"c_rot": rot, "c_pk": pk, "c_mask": mask, "c_ident": ident, "c_before": before, "c_order": order}


def stage_project(nc, d, g):
    with ExitStack() as ctx:
        def sb(name, shape, dt):
            return ctx.enter_context(nc.sbuf_tensor(name, shape, dt))

        def sem(name):
            return ctx.enter_context(nc.semaphore(name))

        rot = sb("rot", [P, 4, S], F32)
        wq = sb("wq", [P, CT, C], F32)
        wqs = sb("wqs", [P, CT, C], F32)
        wk = sb("wk", [P, CT, C], F32)
        wv = sb("wv", [P, CT, C], F32)
        bias = sb("bias", [P, 3, CT], F32)
        xT = sb("xT", [P, 2, CT, CH], F32)
        stg = sb("stg", [P, 2, 8, CH], F16)
        vst = sb("vst", [P, 2, 2, H, 32], F32)
        prod = sb("prod", [P, 2, 4, CH], F32)
        turned = sb("turned", [P, 2, 2, CH], F32)
        zero = sb("zero", [P, 4 * C], F32)
        pq = ctx.enter_context(nc.psum_tensor("pq", [P, 2, 3, CH], F32))
        pv = ctx.enter_context(nc.psum_tensor("pv", [P, 2, 2, C], F32))

        const_in = sem("a_const_in")
        x_in = [sem(f"a_x_in{i}") for i in range(2)]
        vst_ready = sem("a_vst_ready")
        qk_ready = sem("a_qk_ready")
        v_ready = sem("a_v_ready")
        first_hi = sem("a_first_hi")
        rot_prod = sem("a_rot_prod")
        rot_sum = sem("a_rot_sum")
        rot_hi = sem("a_rot_hi")
        dve_done = sem("a_dve_done")
        pool_done = sem("a_pool_done")
        v_copied = sem("a_v_copied")
        stored = [sem(f"a_stored{i}") for i in range(2)]
        v_stored = [sem(f"a_v_stored{i}") for i in range(2)]
        zeroed = sem("a_zeroed")
        zeros_out = sem("a_zeros_out")
        misc = sem("a_misc")
        NCONST = 6
        OUT = 3 * 16
        VOUT = 2 * 16

        block = ctx.enter_context(nc.Block())

        @block.sync
        def _(sp):
            sp.dma_start(xT[:, 0], d["xT"][0]).then_inc(x_in[0], 16)
            for t, s in ((wq, "Wq"), (wqs, "Wqs"), (wk, "Wk"), (wv, "Wv")):
                sp.dma_start(t[:, :, :], d[s].rearrange("(t p) n -> p t n", p=P)).then_inc(const_in, 16)
            sp.dma_start(bias[:, :, :], d["uv"]).then_inc(const_in, 16)
            sp.dma_start(rot[:, :, :], d["c_rot"]).then_inc(const_in, 16)
            with sp.Fori(0, B) as b:
                for ch in range(NCH):
                    sp.wait_ge(v_ready, b * 8 + 2 * ch + 1)
                    nxt = b * 4 + (ch + 1) if ch < NCH - 1 else (b * 4 + 4) % 8
                    sp.dma_start(xT[:, (ch + 1) % 2], d["xT"][bass.ds(nxt, 1)].rearrange("a p t n -> p (a t) n")
                                 ).then_inc(x_in[(ch + 1) % 2], 16)
                    for ht in range(CT):
                        st = b * 8 + (2 * ch + ht)
                        row = b * C + ht * P
                        sp.wait_ge(dve_done, st + 1 + 2)
                        sp.wait_ge(pool_done, st + 1 + 2)
                        q = g["qs"].rearrange("k r n -> r k n")
                        sp.dma_start(q[bass.ds(row, P), 0:4, ch * CH + 1:(ch + 1) * CH + 1],
                                     stg[:, ht, 0:4, :]).then_inc(stored[ht], 16)
                        o = 1 if ch == 0 else 0
                        sp.dma_start(q[bass.ds(row, P), 4:6, ch * CH + o:(ch + 1) * CH],
                                     stg[:, ht, 4:6, o:]).then_inc(stored[ht], 16)
                        k = g["ks"].rearrange("k r n -> r k n")
                        sp.dma_start(k[bass.ds(row, P), :, ch * CH:(ch + 1) * CH],
                                     stg[:, ht, 6:8, :]).then_inc(stored[ht], 16)
                        sp.wait_ge(v_copied, st + 1 + 2)
                        for i in range(2):
                            tok = ch * CH + (2 * ht + i) * P
                            for_quads = g["vs"].rearrange("(a t) n -> t a n", t=S)
                            sp.dma_start(for_quads[tok:tok + P, bass.ds(b * NQ, NQ), :],
                                         vst[:, ht, i].rearrange("p (a c) n -> p a (c n)", a=NQ)
                                         ).then_inc(v_stored[ht], 16)
            for s in stored:
                sp.wait_ge(s, OUT * (B * NCH + 1))
            with nc.allow_non_contiguous_dma(reason="one column"):
                q = g["qs"]
                for dst, src in ((0, 0), (1, 1), (2, 2), (3, 3), (4, 2), (5, 3)):
                    sp.dma_start(q[dst, :, 0:1], q[src, :, S:S + 1]).then_inc(misc, 16)
            sp.wait_ge(misc, 6 * 16)
            for s in v_stored:
                sp.wait_ge(s, VOUT * (B * NCH + 1))
            sp.wait_ge(x_in[0], 16 * (B * NCH // 2 + 1))

        @block.tensor
        def _(pe):
            pe.wait_ge(const_in, 16 * NCONST)
            with pe.Fori(0, B) as b:
                for ch in range(NCH):
                    xp = ch % 2
                    pe.wait_ge(x_in[xp], b * 32 + 16 * (ch // 2 + 1))
                    for ht in range(CT):
                        st = b * 8 + (2 * ch + ht)
                        pe.wait_ge(dve_done, st - 1 + 2)
                        pe.wait_ge(first_hi, 2 * (st - 1) + 4)
                        for n, w in enumerate((wq, wqs, wk)):
                            for ct in range(CT):
                                last = nc.tensor.matmul(pq[:, ht, n, :], w[:, ct, ht * P:(ht + 1) * P],
                                                        xT[:, xp, ct, :], start=(ct == 0), stop=(ct == CT - 1))
                        last.then_inc(qk_ready, 1)
                        pe.wait_ge(v_copied, st - 1 + 2)
                        for i in range(2):
                            for ct in range(CT):
                                t = 2 * ht + i
                                last = nc.tensor.matmul(pv[:, ht, i, :], xT[:, xp, ct, t * P:(t + 1) * P],
                                                        wv[:, ct, :], start=(ct == 0), stop=(ct == CT - 1))
                        last.then_inc(v_ready, 1)

        @block.scalar
        def _(act):
            act.wait_ge(const_in, 16 * NCONST)
            act.wait_ge(vst_ready, 2)
            act.sem_inc(first_hi, 4)
            act.sem_inc(v_copied, 2)
            with act.Fori(0, B) as b:
                for ch in range(NCH):
                    for ht in range(CT):
                        st = b * 8 + (2 * ch + ht)
                        use = b * 4 + ch
                        act.wait_ge(qk_ready, st + 1)
                        act.wait_ge(stored[ht], OUT * use + OUT)
                        nc.scalar.activation(stg[:, ht, 0, :], pq[:, ht, 0, :], ACT.Identity, bias=bias[:, 0, ht:ht + 1]
                                             ).then_inc(first_hi, 1)
                        nc.scalar.activation(stg[:, ht, 6, :], pq[:, ht, 2, :], ACT.Copy).then_inc(first_hi, 1)
                        act.wait_ge(v_ready, st + 1)
                        act.wait_ge(v_stored[ht], VOUT * use + VOUT)
                        nc.scalar.activation(vst[:, ht, :, :, 0:DK],
                                             pv[:, ht].rearrange("p i (h d) -> p i h d", h=H), ACT.Copy
                                             ).then_inc(v_copied, 1)
                        for n in range(2):
                            act.wait_ge(rot_sum, 2 * st + (n + 1))
                            nc.scalar.activation(stg[:, ht, 2 + 2 * n, :], turned[:, ht, n, :], ACT.Copy
                                                 ).then_inc(rot_hi, 1)

        @block.vector
        def _(dve):
            nc.vector.memset(vst[:, :, :, :, :], 0.0).then_inc(vst_ready, 1)
            nc.vector.memset(zero[:, :], 0.0).then_inc(zeroed, 1)
            dve.wait_ge(vst_ready, 1)
            nc.vector.memset(vst[:, :, :, :, DK:DK + 1], 1.0).then_inc(vst_ready, 1)
            dve.sem_inc(dve_done, 2)
            dve.wait_ge(const_in, 16 * NCONST)
            with dve.Fori(0, B) as b:
                for ch in range(NCH):
                    for ht in range(CT):
                        st = b * 8 + (2 * ch + ht)
                        use = b * 4 + ch
                        cols = slice(ch * CH, (ch + 1) * CH)
                        dve.wait_ge(qk_ready, st + 1)
                        dve.wait_ge(pool_done, st - 1 + 2)
                        for n in (1, 3, 0, 2):
                            if n == 0:
                                dve.wait_ge(first_hi, 2 * st + 1 + 4)
                            nc.vector.scalar_tensor_tensor(
                                out=prod[:, ht, n, :], in0=pq[:, ht, n % 2, :], scalar=bias[:, 1 + n % 2, ht:ht + 1],
                                in1=rot[:, n, cols], op0=ALU.add, op1=ALU.mult).then_inc(rot_prod, 1)
                        dve.wait_ge(first_hi, 2 * st + 2 + 4)
                        dve.wait_ge(stored[ht], OUT * use + OUT)
                        nc.vector.scalar_tensor_tensor(
                            out=stg[:, ht, 1, :], in0=pq[:, ht, 0, :], scalar=bias[:, 0, ht:ht + 1],
                            in1=stg[:, ht, 0, :], op0=ALU.add, op1=ALU.subtract)
                        nc.vector.tensor_tensor(stg[:, ht, 7, :], pq[:, ht, 2, :], stg[:, ht, 6, :], ALU.subtract
                                                ).then_inc(dve_done, 1)

        @block.gpsimd
        def _(pool):
            pool.sem_inc(pool_done, 2)
            for s in stored:
                pool.sem_inc(s, OUT)
            for s in v_stored:
                pool.sem_inc(s, VOUT)
            pool.wait_ge(zeroed, 1)
            for t, r0 in ((g["xs"], 0), (g["ys"], NTOK * 2)):
                for r in range(r0, t.shape[0], P * 4):
                    pool.dma_start(t[r:r + P * 4].rearrange("(p a) n -> p (a n)", p=P), zero[:, :]).then_inc(zeros_out, 16)
            with pool.Fori(0, B) as b:
                for ch in range(NCH):
                    for ht in range(CT):
                        st = b * 8 + (2 * ch + ht)
                        for n in range(2):
                            pool.wait_ge(rot_prod, 4 * st + (n + 3))
                            nc.gpsimd.tensor_tensor(turned[:, ht, n, :], prod[:, ht, 2 * n, :],
                                                    prod[:, ht, 2 * n + 1, :], ALU.add).then_inc(rot_sum, 1)
                        for n in range(2):
                            pool.wait_ge(rot_hi, 2 * st + (n + 1))
                            last = nc.gpsimd.tensor_tensor(stg[:, ht, 3 + 2 * n, :], turned[:, ht, n, :],
                                                           stg[:, ht, 2 + 2 * n, :], ALU.subtract)
                        last.then_inc(pool_done, 1)
            pool.wait_ge(zeros_out, 16 * (((NBLK + 2) * BLK + NBLK * BLK - NTOK * 2) // (P * 4)))


def stage_attention(nc, d, g, heads_out):
    with ExitStack() as ctx:
        def sb(name, shape, dt):
            return ctx.enter_context(nc.sbuf_tensor(name, shape, dt))

        def sem(name):
            return ctx.enter_context(nc.semaphore(name))

        NMAX = QUAD * QT * 5
        SLOTS = NMAX + 2
        STEPS = KT + 2
        TILES = 2 * STEPS
        NM = 3
        LEAD, TURN_LAG, OUT_AT = 25, 5, 3
        assert len(range(NMAX)) + 2 == SLOTS and (NMAX + LEAD) % NM == (SLOTS - 1) % NM
        NP = 4

        kmax = sb("kmax", [P, QUAD, S], F16)
        kexp = sb("kexp", [P, QUAD, S], F16)
        qop = sb("qop", [P, NCH, 3, QUAD, CH], F16)
        vals = sb("vals", [P, KT, QUAD, 32], F32)
        prob = sb("prob", [P, NP, 2, CH], F32)
        ident = sb("ident", [P, P], F32)
        identb = sb("identb", [P, P], BF16)
        maskf = sb("maskf", [P, 9 * P], F32)
        mask = sb("mask", [P, 9 * P], BF16)
        part = sb("part", [P, QUAD * QT, 5], F32)
        nmax = sb("nmax", [P, QUAD * QT], F32)
        nmaxT = sb("nmaxT", [QUAD * QT, 2, P], F16)
        summed = sb("summed", [P, CH], F32)
        rsum = sb("rsum", [P, QT * QUAD], F32)
        sc_ps = ctx.enter_context(nc.psum_tensor("sc_ps", [P, 2, 2, CH], F32))
        mx_ps = ctx.enter_context(nc.psum_tensor("mx_ps", [P, NM, CH], F32))
        acc = ctx.enter_context(nc.psum_tensor("acc", [P, CH], F32))

        const_in = sem("b_const_in")
        const_cast = sem("b_const_cast")
        cleared = sem("b_cleared")
        q_in = [sem(f"b_q_in{i}") for i in range(NCH)]
        m_in = [sem(f"b_m_in{i}") for i in range(NCH)]
        kmax_in = [sem(f"b_kmax_in{i}") for i in range(QUAD)]
        kexp_in = [sem(f"b_kexp_in{i}") for i in range(4)]
        scores = sem("b_scores")
        exped = sem("b_exped")
        pv_done = sem("b_pv_done")
        evacuated = sem("b_evacuated")
        slot_full = sem("b_slot_full")
        slot_free = sem("b_slot_free")
        max_done = sem("b_max_done")
        own = sem("b_own")

        LOW, HIGH, SUP = range(3)
        NQDMA = 3 * 6 - 3
        q_total = [NQDMA + (3 if c == 0 else 0) for c in range(NCH)]

        block = ctx.enter_context(nc.Block())

        def entries(n_next, n_after):
            seq = [(1, k) for k in range(LEAD, NMAX)] if n_next else []
            if n_next:
                ahead = [(2, k) for k in range(LEAD)] if n_after else []
                seq += ahead[:TURN_LAG] + ["maxima"] + ahead[TURN_LAG:]
            seq.insert(OUT_AT if n_next else 0, "output")
            return seq

        BODY = entries(True, True)
        BEFORE = [(1, k) for k in range(NMAX)] + [(2, k) for k in range(TURN_LAG)] + ["maxima"] + [
            (2, k) for k in range(TURN_LAG, LEAD)]

        def number(n, pos, last):
            if last == "before":
                return pos
            if last and n == NIT * NCH - 1:
                return len(BEFORE) + SLOTS * (n - 1) + len(entries(True, False)) + pos
            return len(BEFORE) + SLOTS * n + pos

        def body_entries(c, last):
            return entries(not (last and c == NCH - 1), not (last and c >= NCH - 2))

        @block.sync
        def _(sp):
            def load_q(it, c):
                row = it * 4 * DK
                k = 0
                for cls in range(3):
                    for part3, half in ((0, 0), (1, 0), (2, 1)):
                        base = 32 * part3
                        src = g["qs"][half, bass.ds(row, 4 * DK), c * CH:(c + 1) * CH]
                        sp.dma_start(qop[base:base + DK, c, cls], src.rearrange("(h r) n -> r h n", h=QUAD)
                                     ).then_inc(q_in[c], 16)
                        kind = 2 * (1 if cls == LOW else 2) + half
                        if cls != SUP:
                            src = g["qs"][kind, bass.ds(row, 4 * DK), c * CH:(c + 1) * CH]
                            sp.dma_start(qop[base + DK:base + 2 * DK, c, cls], src.rearrange("(h r) n -> r h n", h=QUAD)
                                         ).then_inc(q_in[c], 16)
                        elif c == 0:
                            src = g["qs"][2 + half, bass.ds(row, 4 * DK), 0:1]
                            with nc.allow_non_contiguous_dma(reason="place 0 alone"):
                                sp.dma_start(qop[base + DK:base + 2 * DK, c, cls, :, 0:1],
                                             src.rearrange("(h r) n -> r h n", h=QUAD)).then_inc(q_in[c], 16)

            def load_kmax(it, h):
                for part3, half in ((0, 0), (1, 1), (2, 0)):
                    sp.dma_start(kmax[32 * part3:32 * part3 + DK, h], g["ks"][half, bass.ds(it * 4 * DK + h * DK, DK)]
                                 ).then_inc(kmax_in[h], 16)

            def load_kexp(it, s):
                cols = slice(s * CH, (s + 1) * CH)
                for part3, half in ((0, 0), (1, 1), (2, 0)):
                    src = g["ks"][half, bass.ds(it * 4 * DK, 4 * DK), cols]
                    sp.dma_start(kexp[32 * part3:32 * part3 + DK, :, cols], src.rearrange("(h r) n -> r h n", h=QUAD)
                                 ).then_inc(kexp_in[s], 16)
                sp.dma_start(vals[:, 4 * s:4 * s + 4].rearrange("p k h d -> p k (h d)"),
                             g["vs"][bass.ds(it * S + s * CH, CH)].rearrange("(k p) n -> p k n", p=P)
                             ).then_inc(kexp_in[s], 16)

            def send_max(c, turned):
                sp.wait_ge(slot_free, turned + 1 + NM)
                for cls in range(3):
                    sp.dma_start(qop[ONE_ROW:ONE_ROW + 1, c, cls].rearrange("o h (q n) -> o (h q) n", q=QT),
                                 nmaxT[:, c % 2, :]).then_inc(m_in[c], 16)

            sp.dma_start(ident[:, :], d["c_ident"]).then_inc(const_in, 16)
            sp.dma_start(maskf[:, :], d["c_mask"]).then_inc(const_in, 16)
            sp.wait_ge(cleared, 4)
            for t in (kmax, kexp):
                for h in range(QUAD):
                    for part3, half in ((0, 0), (1, 1), (2, 0)):
                        sp.dma_start(t[32 * part3 + DK:32 * part3 + 2 * DK, h], d["c_pk"][half]).then_inc(const_in, 16)
            load_q(0, 0)
            for h in range(QUAD):
                load_kmax(0, h)
            for s in range(4):
                load_kexp(0, s)
            load_q(0, 1)
            load_q(0, 2)
            send_max(0, BEFORE.index("maxima"))

            def turn(it, last):
                for c in range(NCH):
                    n = it * NCH + c
                    seq = body_entries(c, last)
                    if c < 1 or not last:
                        sp.wait_ge(evacuated, n + 2)
                        load_q(it + (c + 3) // NCH, (c + 3) % NCH)
                    if c == 2 and not last:
                        for h in (1, 2, 3):
                            sp.wait_ge(slot_full, number(n, seq.index((1, (h + 1) * QT * 5 - 1)), last) + 1)
                            load_kmax(it + 1, h)
                    if c == 3 and not last:
                        for s in range(3):
                            sp.wait_ge(pv_done, n * STEPS + 4 * s + 4 + 2)
                            load_kexp(it + 1, s)
                    if "maxima" in seq:
                        send_max((c + 1) % NCH, number(n, seq.index("maxima"), last))
                    if c == 1 and not last:
                        sp.wait_ge(slot_full, number(n, seq.index((2, QT * 5 - 1)), last) + 1)
                        load_kmax(it + 1, 0)
                    if c == 3 and not last:
                        sp.wait_ge(pv_done, n * STEPS + STEPS + 2)
                        load_kexp(it + 1, 3)

            with sp.Fori(0, NIT - 1) as it:
                turn(it, False)
            turn(NIT - 1, True)

        @block.tensor
        def _(pe):
            def max_tile(c, i, k, bank):
                h, qt = divmod(i, QT)
                T = c * QT + qt
                q = lambda cls: qop[0:NSPLIT, c, cls, h, qt * P:(qt + 1) * P]
                if k < 4:
                    others = [t for t in range(KT) if t != T][4 * k:4 * k + 4]
                    col = 0
                    while others:
                        cls = LOW if others[0] < T else HIGH
                        run = [others.pop(0)]
                        while others and others[0] == run[-1] + 1 and (LOW if others[0] < T else HIGH) == cls:
                            run.append(others.pop(0))
                        width = len(run) * P
                        last = nc.tensor.matmul(bank[:, col:col + width], q(cls), kmax[0:NSPLIT, h, run[0] * P:run[0] * P + width],
                                                start=True, stop=True, skip_group_check=True)
                        col += width
                else:
                    for n, cls in enumerate((LOW, HIGH, SUP)):
                        nc.tensor.matmul(bank[:, n * P:(n + 1) * P], q(cls), kmax[0:NSPLIT, h, T * P:(T + 1) * P],
                                         start=(n == 0), stop=False, skip_group_check=True)
                    last = nc.tensor.matmul(bank[:, 0:3 * P], identb[:, :], mask[:, 3 * P:6 * P],
                                            start=False, stop=True, skip_group_check=True)
                last.then_inc(slot_full, 1)

            def score_tile(c, t, pair, buf):
                for j in range(2):
                    h = 2 * pair + j
                    out = sc_ps[:, buf, j, :]
                    q = lambda cls, a, b: qop[0:BIG_ROWS, c, cls, h, a:b]
                    k = lambda kt: kexp[0:BIG_ROWS, h, kt * P:(kt + 1) * P]
                    if t < KT:
                        split = min(max(t - c * QT, 0), QT) * P
                        if t >= (c + 1) * QT:
                            split = CH
                        on_diag = c * QT <= t < (c + 1) * QT
                        if split:
                            last = nc.tensor.matmul(out[:, 0:split], k(t), q(HIGH, 0, split), start=True,
                                                    stop=True, skip_group_check=True)
                        if split < CH:
                            last = nc.tensor.matmul(out[:, split:CH], k(t), q(LOW, split, CH), start=True,
                                                    stop=not on_diag, skip_group_check=True)
                        if on_diag:
                            last = nc.tensor.matmul(out[:, split:split + P], identb[:, :], mask[:, 4 * P:5 * P],
                                                    start=False, stop=True, skip_group_check=True)
                    else:
                        cls, m = (HIGH, 0) if t == KT else (SUP, 5)
                        for n in range(QT):
                            nc.tensor.matmul(out[:, n * P:(n + 1) * P], k(c * QT + n), q(cls, n * P, (n + 1) * P),
                                             start=(n == 0), stop=False, skip_group_check=True)
                        last = nc.tensor.matmul(out[:, :], identb[:, :], mask[:, m * P:(m + 4) * P],
                                                start=False, stop=True, skip_group_check=True)
                last.then_inc(scores, 1)

            def values(c, t):
                for n in ([None] if t < KT else range(QT)):
                    for h in range(QUAD):
                        kt = t if t < KT else c * QT + n
                        cols = slice(0, CH) if t < KT else slice(n * P, (n + 1) * P)
                        last = nc.tensor.matmul(acc[32 * h:32 * h + 32, cols], vals[:, kt, h, :],
                                                prob[:, (2 * t + h // 2) % NP, h % 2, cols],
                                                start=(t == 0), stop=(t == STEPS - 1), skip_group_check=True)
                last.then_inc(pv_done, 1)

            def take_bank(n, pos, last):
                strict = pos == 0 and last != "before"
                pe.wait_ge(slot_free, number(n, pos, last) + (NM if strict else 1))
                return mx_ps[:, pos % NM, :]

            def needs_q(it, c):
                pe.wait_ge(q_in[c], (it + 1) * 16 * q_total[c])

            def emit(it, c, n, pos, entry, last):
                if entry == "maxima":
                    pe.wait_ge(max_done, n + 2)
                    bank = take_bank(n, pos, last)
                    nc.tensor.transpose(bank[0:QUAD * QT, 0:P], nmax[:, :], ident[:, :]).then_inc(slot_full, 1)
                elif entry == "output":
                    pe.wait_ge(evacuated, n + 2)
                    bank = take_bank(n, pos, last)
                    for qt in range(QT):
                        mm = nc.tensor.transpose(bank[:, qt * P:(qt + 1) * P], summed[:, qt * P:(qt + 1) * P], ident[:, :])
                    mm.then_inc(slot_full, 1)
                else:
                    off, k = entry
                    nit, nc_ = it + (c + off) // NCH, (c + off) % NCH
                    if k == 0:
                        needs_q(nit, nc_)
                    if nc_ == 0 and k % (QT * 5) == 0:
                        pe.wait_ge(kmax_in[k // (QT * 5)], (nit + 1) * 16 * 3)
                    max_tile(nc_, k // 5, k % 5, take_bank(n, pos, last))

            def first_scores(it, c, n):
                pe.wait_ge(m_in[c], (it + 1) * 16 * 3)
                pe.wait_ge(kexp_in[0], (it + 1) * 16 * 4)
                for pair in range(2):
                    pe.wait_ge(exped, n * TILES + pair + 1)
                    score_tile(c, 0, pair, pair)

            pe.wait_ge(const_in, 16 * (2 + 2 * QUAD * 3))
            pe.wait_ge(const_cast, 2)
            pe.wait_ge(cleared, 4)
            for pos, entry in enumerate(BEFORE):
                emit(-1, NCH - 1, -1, pos, entry, "before")
            first_scores(0, 0, 0)

            def turn(it, last):
                for c in range(NCH):
                    n = it * NCH + c
                    nit, nc_ = (it, c + 1) if c < NCH - 1 else (it + 1, 0)
                    more = not (last and c == NCH - 1)
                    seq = body_entries(c, last)
                    done = [0]

                    def pace(t, part):
                        due = min(len(seq), SLOTS * (3 * (t - 1) + part) // (3 * STEPS))
                        if not more:
                            due = len(seq) if t >= 2 else 0
                        while done[0] < due:
                            if seq[done[0]] == "output" and (t, part) < (1, 3):
                                return
                            emit(it, c, n, done[0], seq[done[0]], last)
                            done[0] += 1

                    for t in range(1, STEPS + 1):
                        if t < STEPS:
                            if t < KT and t % 4 == 0:
                                pe.wait_ge(kexp_in[t // 4], (it + 1) * 16 * 4)
                            for pair in range(2):
                                pe.wait_ge(exped, n * TILES + (2 * t + pair) - 2 + 1 + 2)
                                score_tile(c, t, pair, pair)
                                pace(t, pair + 1)
                        elif more:
                            first_scores(nit, nc_, n + 1)
                            pace(t, 2)
                        if t == 1:
                            pe.wait_ge(evacuated, n + 2)
                        pe.wait_ge(exped, n * TILES + 2 * t + 2)
                        values(c, t - 1)
                        pace(t, 3)

            with pe.Fori(0, NIT - 1) as it:
                turn(it, False)
            turn(NIT - 1, True)
            pe.wait_ge(evacuated, NIT * NCH + 2)
            pe.wait_ge(slot_free, number(NIT * NCH - 1, 1, True) + NM)
            for qt in range(QT):
                mm = nc.tensor.transpose(mx_ps[:, 0, qt * P:(qt + 1) * P], summed[:, qt * P:(qt + 1) * P], ident[:, :])
            mm.then_inc(slot_full, 1)

        @block.scalar
        def _(act):
            act.sem_inc(exped, 2)
            act.sem_inc(evacuated, 2)

            def exp_step(c, n, t):
                for pair in range(2):
                    act.wait_ge(scores, n * TILES + 2 * t + pair + 1)
                    if pair == 0:
                        act.wait_ge(pv_done, n * STEPS + t - 1 + 2)
                    nc.scalar.activation(prob[:, (2 * t + pair) % NP, :, :], sc_ps[:, pair, :, :], ACT.Exp, scale=SCALE
                                         ).then_inc(exped, 1)

            exp_step(0, 0, 0)

            def turn(it, last):
                for c in range(NCH):
                    n = it * NCH + c
                    for t in range(1, STEPS):
                        exp_step(c, n, t)
                    if not (last and c == NCH - 1):
                        exp_step((c + 1) % NCH, n + 1, 0)
                    act.wait_ge(pv_done, (n + 1) * STEPS + 2)
                    seq = body_entries(c, last)
                    act.wait_ge(slot_full, number(n, seq.index("output"), last) + 1)
                    nc.scalar.activation(summed[:, :], acc[:, :], ACT.Copy).then_inc(evacuated, 1)

            with act.Fori(0, NIT - 1) as it:
                turn(it, False)
            turn(NIT - 1, True)

        @block.vector
        def _(dve):
            nc.vector.memset(summed[:, :], 1.0).then_inc(cleared, 1)
            nc.vector.memset(kexp[ONE_ROW:ONE_ROW + 1], 1.0).then_inc(cleared, 1)
            dve.sem_inc(slot_free, NM)
            dve.wait_ge(const_in, 16 * (2 + 2 * QUAD * 3))
            nc.vector.tensor_copy(mask[:, :], maskf[:, :]).then_inc(const_cast, 1)
            nc.vector.tensor_copy(identb[:, :], ident[:, :]).then_inc(const_cast, 1)

            def divide_output(n, bank_no, num):
                dve.wait_ge(slot_full, num + 1)
                bank = mx_ps[:, bank_no, :].rearrange("p (a d) -> p a d", d=32)
                nc.vector.reciprocal(rsum[:, :], bank[:, :, DK]).then_inc(own, 1)
                dve.wait_ge(own, n + 1)
                nc.vector.tensor_tensor(heads_out[:, bass.ds(n, 1), :].rearrange("p o (a d) -> p (o a) d", d=DK),
                                        bank[:, :, 0:DK], rsum[:, :].unsqueeze(2).to_broadcast([P, QT * QUAD, DK]),
                                        ALU.mult).then_inc(slot_free, 1)

            def drain(c, n, seq, last):
                for pos, entry in enumerate(seq):
                    num = number(n, pos, last)
                    if entry == "output":
                        divide_output(n, pos % NM, num)
                        continue
                    dve.wait_ge(slot_full, num + 1)
                    if entry == "maxima":
                        nc.vector.tensor_copy(nmaxT[:, (c + 1) % 2, :], mx_ps[0:QUAD * QT, pos % NM, 0:P]
                                              ).then_inc(slot_free, 1)
                        continue
                    off, k = entry
                    if entry == (2, 0):
                        dve.wait_ge(max_done, n + 2)
                    width = CH if k % 5 < 3 else 3 * P
                    nc.vector.reduce_max(part[:, k // 5, k % 5:k % 5 + 1], mx_ps[:, pos % NM, 0:width], AX
                                         ).then_inc(slot_free, 1)
                    if entry == (1, NMAX - 1):
                        dve.wait_ge(slot_free, num + 1 + NM)
                        nc.vector.tensor_reduce(nmax[:, :], part[:, :, :], AX, ALU.max, negate=True).then_inc(max_done, 1)

            drain(NCH - 1, -1, BEFORE, "before")

            def turn(it, last):
                for c in range(NCH):
                    drain(c, it * NCH + c, body_entries(c, last), last)

            with dve.Fori(0, NIT - 1) as it:
                turn(it, False)
            turn(NIT - 1, True)
            divide_output(NIT * NCH, 0, number(NIT * NCH - 1, 1, True))

        @block.gpsimd
        def _(pool):
            pool.sem_inc(pv_done, 2)
            nc.gpsimd.memset(qop[0:NSPLIT, 0:2, SUP], 0.0).then_inc(cleared, 1)
            nc.gpsimd.memset(qop[0:NSPLIT, 2:4, SUP], 0.0).then_inc(cleared, 1)


def place_rows(c):
    if c:
        return [((0, P), (0, QT), c * CH - 1)]
    return [((0, 1), (0, 1), S - 1), ((1, P), (0, 1), 0), ((0, P), (1, QT), P - 1)]


def rows_of(t, run, start):
    (a, z), (q0, q1), _ = run
    n = (z - a) * (q1 - q0)
    return t[bass.ds(start, n)].rearrange("(q p) n -> p q n", q=q1 - q0)


def stage_norm(nc, d, g, heads_out, x1, logits):
    with ExitStack() as ctx:
        def sb(name, shape, dt):
            return ctx.enter_context(nc.sbuf_tensor(name, shape, dt))

        def sem(name):
            return ctx.enter_context(nc.semaphore(name))

        wo = sb("wo", [P, CT, C], F32)
        rw = sb("rw", [P, CT, E], F32)
        bo = sb("bo", [P, C], F32)
        ident = sb("identc", [P, P], F32)
        heads = sb("heads", [P, 2, QT, C], F32)
        xres = sb("xres", [P, 2, QT, C], F32)
        xbias = sb("xbias", [P, 2, QT, C], F32)
        headsT = sb("headsT", [P, 2, QT, CT, P], F32)
        res = sb("res", [P, 2, QT, C], F32)
        stats = sb("stats", [P, QT, 6], F32)
        agg = sb("agg", [P, 2, QT, 2], F32)
        dev = sb("dev", [P, 2, QT], F32)
        rstd = sb("rstd", [P, 2, QT], F32)
        xnorm = sb("xnorm", [P, 2, QT, C], F32)
        xnormT = sb("xnormT", [P, 2, QT, CT, P], F32)
        t_ps = ctx.enter_context(nc.psum_tensor("t_ps", [P, QT, CT, P], F32))
        y_ps = ctx.enter_context(nc.psum_tensor("y_ps", [P, QT, C], F32))
        n_ps = ctx.enter_context(nc.psum_tensor("n_ps", [P, QT, CT, P], F32))
        l_ps = ctx.enter_context(nc.psum_tensor("l_ps", [P, 2, CH], F32))

        const_in = sem("c_const_in")
        x_in = [sem(f"c_x_in{i}") for i in range(2)]
        gathered = sem("c_gathered")
        biased = sem("c_biased")
        kept = sem("c_kept")
        headsT_ps = sem("c_headsT_ps")
        headsT_sb = sem("c_headsT_sb")
        projected = sem("c_projected")
        residual = sem("c_residual")
        spread = sem("c_spread")
        rooted = sem("c_rooted")
        normed = sem("c_normed")
        xT_ps = sem("c_xT_ps")
        xT_sb = sem("c_xT_sb")
        routed = sem("c_routed")
        own = sem("c_own")
        passed = sem("c_passed")
        logged = sem("c_logged")

        block = ctx.enter_context(nc.Block())
        GROUPS = B * NCH
        x_dmas = [len(place_rows(c)) for c in range(NCH)]
        upto = [sum(x_dmas[k] for k in range(c + 1) if k % 2 == c % 2) for c in range(NCH)]

        @block.sync
        def _(sp):
            sp.dma_start(wo[:, :, :], d["Wo"].rearrange("(t p) n -> p t n", p=P)).then_inc(const_in, 16)
            sp.dma_start(rw[:, :, :], d["rw"].rearrange("(t p) n -> p t n", p=P)).then_inc(const_in, 16)
            sp.dma_start(bo[:, :], d["bo"].to_broadcast([P, C])).then_inc(const_in, 16)
            sp.dma_start(ident[:, :], d["c_ident"]).then_inc(const_in, 16)
            with sp.Fori(0, B) as b:
                for c in range(NCH):
                    m = b * NCH + c
                    sp.wait_ge(biased, m - 1 + 2)
                    for run in place_rows(c):
                        (a, z), (q0, q1), row = run
                        sp.dma_start(xres[a:z, c % 2, q0:q1], rows_of(d["x"], run, b * S + row)).then_inc(x_in[c % 2], 16)

        @block.gpsimd
        def _(pool):
            pool.sem_inc(biased, 2)
            pool.sem_inc(kept, 2)
            pool.wait_ge(const_in, 64)

            def keep(m, par):
                pool.wait_ge(normed, m + 1)
                nc.gpsimd.tensor_copy(x1[:, bass.ds(m * QT, QT), :], xnorm[:, par]).then_inc(kept, 1)

            with pool.Fori(0, B) as b:
                for c in range(NCH):
                    m = b * NCH + c
                    pool.wait_ge(headsT_ps, m - 1 + 2)
                    for quad in range(NQ):
                        slot = b * NQ * NCH + (quad * NCH + c + 1)
                        last = nc.gpsimd.tensor_copy(heads[:, c % 2, :, quad * 64:(quad + 1) * 64],
                                                     heads_out[:, bass.ds(slot, 1), :].rearrange("p o (q n) -> p (o q) n", q=QT))
                    last.then_inc(gathered, 1)
                    pool.wait_ge(x_in[c % 2], b * (16 * sum(x_dmas[c % 2::2])) + 16 * upto[c])
                    pool.wait_ge(residual, m - 1 + 2)
                    nc.gpsimd.tensor_tensor(xbias[:, c % 2], xres[:, c % 2],
                                            bo[:, :].unsqueeze(1).to_broadcast([P, QT, C]), ALU.add).then_inc(biased, 1)
                    keep(m, c % 2)

        @block.tensor
        def _(pe):
            pe.sem_inc(headsT_ps, 2)
            pe.wait_ge(const_in, 64)
            with pe.Fori(0, B) as b:
                for c in range(NCH):
                    m = b * NCH + c
                    par = c % 2
                    pe.wait_ge(gathered, m + 1)
                    pe.wait_ge(headsT_sb, m + 1)
                    for qt in range(QT):
                        for ct in range(CT):
                            last = nc.tensor.transpose(t_ps[:, qt, ct, :], heads[:, par, qt, ct * P:(ct + 1) * P], ident[:, :])
                    last.then_inc(headsT_ps, 1)
                    pe.wait_ge(headsT_sb, m + 2)
                    pe.wait_ge(residual, m + 2)
                    for qt in range(QT):
                        for ct in range(CT):
                            last = nc.tensor.matmul(y_ps[:, qt, :], headsT[:, par, qt, ct, :], wo[:, ct, :],
                                                    start=(ct == 0), stop=(ct == CT - 1))
                    last.then_inc(projected, 1)
                    pe.wait_ge(normed, m + 1)
                    for qt in range(QT):
                        for ct in range(CT):
                            last = nc.tensor.transpose(n_ps[:, qt, ct, :], xnorm[:, par, qt, ct * P:(ct + 1) * P], ident[:, :])
                    last.then_inc(xT_ps, 1)
                    pe.wait_ge(xT_sb, m + 1)
                    pe.wait_ge(logged, m + 1)
                    for qt in range(QT):
                        for ct in range(CT):
                            last = nc.tensor.matmul(l_ps[:, 0, qt * E:(qt + 1) * E], xnormT[:, par, qt, ct, :], rw[:, ct, :],
                                                    start=(ct == 0), stop=(ct == CT - 1))
                    last.then_inc(routed, 1)

        @block.scalar
        def _(act):
            act.sem_inc(headsT_sb, 1)
            with act.Fori(0, B) as b:
                for c in range(NCH):
                    m = b * NCH + c
                    par = c % 2
                    act.wait_ge(headsT_ps, m + 1 + 2)
                    nc.scalar.activation(headsT[:, par], t_ps[:, :, :, :], ACT.Copy).then_inc(headsT_sb, 1)
                    act.wait_ge(spread, m + 1)
                    nc.scalar.activation(dev[:, par, :], agg[:, par, :, 1], ACT.Sqrt).then_inc(rooted, 1)
                    act.wait_ge(xT_ps, m + 1)
                    nc.scalar.activation(xnormT[:, par], n_ps[:, :, :, :], ACT.Copy).then_inc(xT_sb, 1)

        @block.vector
        def _(dve):
            dve.sem_inc(residual, 2)
            dve.sem_inc(logged, 1)
            with dve.Fori(0, B) as b:
                for c in range(NCH):
                    m = b * NCH + c
                    par = c % 2
                    dve.wait_ge(projected, m + 1)
                    dve.wait_ge(biased, m + 1 + 2)
                    nc.vector.tensor_tensor(res[:, par], y_ps[:, :, :], xbias[:, par], ALU.add).then_inc(residual, 1)
                    dve.wait_ge(residual, m + 1 + 2)
                    for qt in range(QT):
                        last = nc.vector.bn_stats(stats[:, qt, :], res[:, par, qt, :])
                    last.then_inc(own, 1)
                    dve.wait_ge(own, 3 * m + 1)
                    dve.sem_inc(passed, 1)
                    for qt in range(QT):
                        last = nc.vector.bn_aggr(agg[:, par, qt, :], stats[:, qt, :])
                    last.then_inc(own, 1)
                    dve.wait_ge(own, 3 * m + 2)
                    nc.vector.tensor_scalar(agg[:, par, :, 1], agg[:, par, :, 1], EPS, None, ALU.add).then_inc(spread, 1)
                    dve.wait_ge(rooted, m + 1)
                    nc.vector.reciprocal(rstd[:, par, :], dev[:, par, :]).then_inc(own, 1)
                    dve.wait_ge(own, 3 * m + 3)
                    dve.wait_ge(kept, m - 1 + 2)
                    for qt in range(QT):
                        last = nc.vector.tensor_scalar(xnorm[:, par, qt, :], res[:, par, qt, :], agg[:, par, qt, 0:1],
                                                       rstd[:, par, qt:qt + 1], ALU.subtract, ALU.mult)
                    last.then_inc(normed, 1)
                    dve.wait_ge(routed, m + 1)
                    nc.vector.tensor_copy(logits[:, bass.ds(m * QT, QT), :],
                                          l_ps[:, 0, 0:QT * E].rearrange("p (q e) -> p q e", q=QT)).then_inc(logged, 1)


def stage_route(nc, d, g, x1, logits, gates, slots, bounds):
    with ExitStack() as ctx:
        def sb(name, shape, dt):
            return ctx.enter_context(nc.sbuf_tensor(name, shape, dt))

        def sem(name):
            return ctx.enter_context(nc.semaphore(name))

        full = [P, NT, E]
        order = sb("order", full, F32)
        before = sb("before", [P, P], F32)
        ones = sb("ones", [P, P], F32)
        probs = sb("probs", full, F32)
        expd = sb("expd", full, F32)
        work = sb("work", full, F32)
        chosen = sb("chosen", [P, 2, NT, E], F32)
        both = sb("both", full, F32)
        rank = sb("rank", full, F32)
        total = sb("total", full, F32)
        run = sb("run", [P, 2, NT, E], F32)
        row = sb("row", [P, NT], F32)
        slotf = sb("slotf", [P, NT], F32)
        need = sb("need", [P, E], F32)
        needi = sb("needi", [P, E], I32)
        upto = sb("upto", [P, 2, E], F32)
        r_ps = ctx.enter_context(nc.psum_tensor("r_ps", [P, 2, NT * E], F32))

        const_in = sem("d_const_in")
        own = sem("d_own")
        shifted = sem("d_shifted")
        exped = sem("d_exped")
        hot = sem("d_hot")
        counted = sem("d_counted")
        placed = sem("d_placed")
        sent = sem("d_sent")
        block = ctx.enter_context(nc.Block())

        @block.sync
        def _(sp):
            sp.dma_start(order[:, :, :].rearrange("p t e -> p (t e)"), d["c_order"]).then_inc(const_in, 16)
            sp.dma_start(before[:, :], d["c_before"]).then_inc(const_in, 16)

        @block.scalar
        def _(act):
            act.wait_ge(shifted, 1)
            nc.scalar.activation(expd[:, :, :], work[:, :, :], ACT.Exp).then_inc(exped, 1)

        @block.tensor
        def _(pe):
            pe.wait_ge(hot, 1)
            rhs = both[:, :, :].rearrange("p t e -> p (t e)")
            nc.tensor.matmul(r_ps[:, 0, :], before[:, :], rhs, start=True, stop=True)
            nc.tensor.matmul(r_ps[:, 1, :], ones[:, :], rhs, start=True, stop=True).then_inc(counted, 1)

        @block.vector
        def _(dve):
            links = [0]

            def link(ins):
                links[0] += 1
                ins.then_inc(own, 1)
                dve.wait_ge(own, links[0])

            def wide(ap):
                return ap.unsqueeze(2).to_broadcast(full)

            V = nc.vector
            link(V.memset(ones[:, :], 1.0))
            link(V.reduce_max(row[:, :], logits[:, :, :], AX))
            V.tensor_tensor(work[:, :, :], logits[:, :, :], wide(row[:, :]), ALU.subtract).then_inc(shifted, 1)
            dve.wait_ge(exped, 1)
            link(V.reduce_sum(row[:, :], expd[:, :, :], AX))
            link(V.reciprocal(row[:, :], row[:, :]))
            link(V.tensor_tensor(probs[:, :, :], expd[:, :, :], wide(row[:, :]), ALU.mult))
            dve.wait_ge(const_in, 32)
            for k in range(2):
                link(V.reduce_max(gates[:, k, :], probs[:, :, :], AX))
                link(V.tensor_tensor(work[:, :, :], probs[:, :, :], wide(gates[:, k, :]), ALU.is_equal))
                link(V.tensor_tensor(work[:, :, :], work[:, :, :], order[:, :, :], ALU.mult))
                link(V.reduce_max(row[:, :], work[:, :, :], AX))
                link(V.tensor_tensor(chosen[:, k], work[:, :, :], wide(row[:, :]), ALU.is_equal))
                if k == 0:
                    link(V.scalar_tensor_tensor(out=probs[:, :, :], in0=chosen[:, 0], scalar=-2.0, in1=probs[:, :, :],
                                                op0=ALU.mult, op1=ALU.add))
            V.tensor_tensor(both[:, :, :], chosen[:, 0], chosen[:, 1], ALU.add).then_inc(hot, 1)
            dve.wait_ge(counted, 1)
            link(V.tensor_copy(rank[:, :, :].rearrange("p t e -> p (t e)"), r_ps[:, 0, :]))
            link(V.tensor_copy(total[:, :, :].rearrange("p t e -> p (t e)"), r_ps[:, 1, :]))
            link(V.tensor_copy(run[:, 0], total[:, :, :]))
            a, step = 0, 1
            while step < NT:
                link(V.tensor_copy(run[:, 1 - a, 0:step], run[:, a, 0:step]))
                link(V.tensor_tensor(run[:, 1 - a, step:], run[:, a, step:], run[:, a, 0:NT - step], ALU.add))
                a, step = 1 - a, 2 * step
            link(V.tensor_scalar(need[:, :], run[:, a, NT - 1], float(BLK - 1), None, ALU.add))
            link(V.tensor_copy(needi[:, :], need[:, :]))
            link(V.tensor_single_scalar(needi[:, :], needi[:, :], BLK.bit_length() - 1, ALU.arith_shift_right))
            link(V.tensor_copy(need[:, :], needi[:, :]))
            link(V.tensor_scalar(need[:, :], need[:, :], 1.0, None, ALU.max))
            link(V.tensor_copy(upto[:, 0], need[:, :]))
            u, step = 0, 1
            while step < E:
                link(V.tensor_copy(upto[:, 1 - u, 0:step], upto[:, u, 0:step]))
                link(V.tensor_tensor(upto[:, 1 - u, step:], upto[:, u, step:], upto[:, u, 0:E - step], ALU.add))
                u, step = 1 - u, 2 * step
            link(V.tensor_tensor(need[:, :], upto[:, u], need[:, :], ALU.subtract))
            link(V.tensor_copy(bounds[:, 0:E], need[:, :]))
            link(V.tensor_copy(bounds[:, E:2 * E], upto[:, u]))
            link(V.tensor_tensor(rank[:, :, :], rank[:, :, :], total[:, :, :], ALU.subtract))
            link(V.tensor_tensor(rank[:, :, :], rank[:, :, :], run[:, a], ALU.add))
            link(V.scalar_tensor_tensor(out=rank[:, :, :], in0=need[:, :].unsqueeze(1).to_broadcast(full),
                                        scalar=float(BLK), in1=rank[:, :, :], op0=ALU.mult, op1=ALU.add))
            for k in range(2):
                link(V.tensor_tensor(work[:, :, :], rank[:, :, :], chosen[:, k], ALU.mult))
                link(V.reduce_sum(slotf[:, :], work[:, :, :], AX))
                V.tensor_copy(slots[:, k, :], slotf[:, :]).then_inc(placed, 1)
                dve.wait_ge(placed, k + 1)

        @block.gpsimd
        def _(pool):
            for k in range(2):
                pool.wait_ge(placed, k + 1)
                for t in range(NT):
                    pool.indirect_dma_start(out=g["xs"], out_offset=bass.IndirectOffsetOnAxis(ap=slots[:, k, t:t + 1], axis=0),
                                            in_=x1[:, t, :], in_offset=None).then_inc(sent, 16)
            pool.wait_ge(sent, 16 * 2 * NT)


def stage_experts(nc, d, g, bounds):
    with ExitStack() as ctx:
        def sb(name, shape, dt):
            return ctx.enter_context(nc.sbuf_tensor(name, shape, dt))

        def sem(name):
            return ctx.enter_context(nc.semaphore(name))

        raw = sb("raw", [P, 2, 3, CT * F], F32)
        wh = sb("wh", [P, 2, 3, 2, CT * F], F16)
        ball = sb("ball", [P, 2, E, FT], F32)
        bcur = sb("bcur", [P, 2, 2, FT], F32)
        b2 = sb("b2", [P, E, C], F32)
        ident = sb("idente", [P, P], F32)
        xin = sb("xin", [P, 2, C], F32)
        xh = sb("xh", [P, 2, CT, BLK], F16)
        act_out = sb("act_out", [P, 4, BLK], F32)
        hid = sb("hid", [P, 4, BLK], F32)
        hh = sb("hh", [P, FT, 2, BLK], F16)
        yout = sb("yout", [P, 2, C], F32)
        gu = ctx.enter_context(nc.psum_tensor("gu", [P, 4, 2, BLK], F32))
        y_ps = ctx.enter_context(nc.psum_tensor("ye_ps", [P, 2, C], F32))
        x_ps = ctx.enter_context(nc.psum_tensor("xe_ps", [P, CT, BLK], F32))

        const_in = sem("e_const_in")
        w_in = [sem(f"e_w_in{i}") for i in range(2)]
        w_high = sem("e_w_high")
        w_low = sem("e_w_low")
        x_in = sem("e_x_in")
        x_turned = sem("e_x_turned")
        x_high = sem("e_x_high")
        x_low = sem("e_x_low")
        gu_ready = sem("e_gu_ready")
        gated = sem("e_gated")
        hidden = sem("e_hidden")
        h_high = sem("e_h_high")
        h_low = sem("e_h_low")
        down = sem("e_down")
        y_ready = sem("e_y_ready")
        y_out = sem("e_y_out")
        biases = sem("e_biases")
        passed = sem("e_passed")
        PARTS = ((0, 0), (0, 1), (1, 0))

        block = ctx.enter_context(nc.Block())

        def span(eng, e):
            lo = eng.value_load(bounds[0:1, bass.ds(e, 1)], min_val=0, max_val=NBLK - 1)
            hi = eng.value_load(bounds[0:1, bass.ds(e + E, 1)], min_val=1, max_val=NBLK)
            return lo, hi

        @block.sync
        def _(sp):
            def load_x(blk):
                sp.dma_start(xin[:, :, :], g["xs"][bass.ds(blk * BLK, BLK)].rearrange("(i p) n -> p i n", p=P)
                             ).then_inc(x_in, 16)

            sp.dma_start(ident[:, :], d["c_ident"]).then_inc(const_in, 16)
            sp.dma_start(ball[:, 0], d["bg"]).then_inc(const_in, 16)
            sp.dma_start(ball[:, 1], d["b1"]).then_inc(const_in, 16)
            sp.dma_start(b2[:, :, :].rearrange("p e n -> p (e n)"), d["b2"].to_broadcast([P, E * C])).then_inc(const_in, 16)
            load_x(0)
            sp.wait_ge(x_turned, 1)
            load_x(1)
            with sp.Fori(0, E // 2) as pair:
                for par in range(2):
                    lo, hi = span(sp, pair * 2 + par)
                    with sp.Fori(lo, hi) as blk:
                        sp.wait_ge(x_turned, blk + 2)
                        load_x(blk + 2)
                        sp.wait_ge(y_ready, blk + 1 + 1)
                        sp.dma_start(g["ys"][bass.ds(blk * BLK, BLK)].rearrange("(i p) n -> p i n", p=P), yout[:, :, :]
                                     ).then_inc(y_out, 16)
            _, total = span(sp, E - 1)
            sp.wait_ge(y_out, total * 16 + 16)
            sp.sem_inc(passed, 1)
            sp.wait_ge(x_in, total * 16 + 32)
            sp.sem_inc(passed, 1)

        @block.tensor
        def _(pe):
            def turn_x(blk):
                pe.wait_ge(x_in, blk * 16 + 16)
                pe.wait_ge(x_low, blk + 1)
                for i in range(2):
                    for ct in range(CT):
                        last = nc.tensor.transpose(x_ps[:, ct, i * P:(i + 1) * P], xin[:, i, ct * P:(ct + 1) * P], ident[:, :])
                last.then_inc(x_turned, 1)

            def gate_up(blk, f, par):
                if f == 0:
                    pe.wait_ge(x_low, blk + 2)
                pe.wait_ge(hidden, blk * FT + f + 1)
                for n in range(2):
                    for ct in range(CT):
                        for k, (wp, xp) in enumerate(PARTS):
                            at = ct * F + f * P
                            last = nc.tensor.matmul(gu[:, f % 4, n, :], wh[:, par, n, wp, at:at + P], xh[:, xp, ct, :],
                                                    start=(ct == 0 and k == 0), stop=(ct == CT - 1 and k == 2),
                                                    skip_group_check=True)
                last.then_inc(gu_ready, 1)

            def down_product(blk, f, par):
                pe.wait_ge(h_low, blk * FT + f + 1)
                if f == 0:
                    pe.wait_ge(y_ready, blk + 1)
                for i in range(2):
                    for k, (wp, hp) in enumerate(PARTS):
                        last = nc.tensor.matmul(y_ps[:, i, :], hh[:, f, hp, i * P:(i + 1) * P],
                                                wh[:, par, 2, wp, f * C:(f + 1) * C],
                                                start=(f == 0 and i == 0 and k == 0), stop=(f == FT - 1 and k == 2),
                                                skip_group_check=True)
                last.then_inc(down, 1)

            pe.wait_ge(const_in, 64)
            turn_x(0)
            with pe.Fori(0, E // 2) as pair:
                for par in range(2):
                    lo, hi = span(pe, pair * 2 + par)
                    pe.wait_ge(w_low, pair * 2 + (par + 1))
                    pe.sem_inc(passed, 1)
                    with pe.Fori(lo, hi) as blk:
                        for f in range(FT):
                            gate_up(blk, f, par)
                            if f >= 2:
                                down_product(blk, f - 2, par)
                        turn_x(blk + 1)
                        down_product(blk, FT - 2, par)
                        down_product(blk, FT - 1, par)

        @block.scalar
        def _(act):
            def load_w(e, par):
                for n, name in enumerate(("wg", "w1")):
                    act.dma_start(raw[:, par, n].rearrange("p (t f) -> p t f", t=CT),
                                  d[name][bass.ds(e, 1)].rearrange("a (t p) f -> p (a t) f", p=P)).then_inc(w_in[par], 16)
                act.dma_start(raw[:, par, 2].rearrange("p (t n) -> p t n", t=FT),
                              d["w2"][bass.ds(e, 1)].rearrange("a (t p) n -> p (a t) n", p=P)).then_inc(w_in[par], 16)

            def high_halves(e, par, loads):
                act.wait_ge(w_in[par], loads * 48)
                for n in range(3):
                    last = nc.scalar.activation(wh[:, par, n, 0, :], raw[:, par, n, :], ACT.Copy)
                last.then_inc(w_high, 1)

            def turned_high(blk):
                act.wait_ge(x_turned, blk + 1)
                nc.scalar.activation(xh[:, 0], x_ps[:, :, :], ACT.Copy).then_inc(x_high, 1)

            load_w(0, 0)
            load_w(1, 1)
            high_halves(0, 0, 1)
            turned_high(0)
            with act.Fori(0, E // 2) as pair:
                for par in range(2):
                    e = pair * 2 + par
                    lo, hi = span(act, e)
                    act.wait_ge(down, lo * FT + 8)
                    high_halves(e + 1, 1 - par, pair + 1 + par)
                    act.wait_ge(w_low, e + 1)
                    load_w((e + 2) % E, par)
                    act.wait_ge(biases, e + 1)
                    with act.Fori(lo, hi) as blk:
                        for f in range(FT + 1):
                            if f < FT:
                                act.wait_ge(gu_ready, blk * FT + f + 1)
                                nc.scalar.activation(act_out[:, f % 4, :], gu[:, f % 4, 0, :], ACT.Gelu,
                                                     bias=bcur[:, par, 0, f:f + 1]).then_inc(gated, 1)
                            if f >= 1:
                                act.wait_ge(hidden, blk * FT + (f - 1) + 1 + 4)
                                act.wait_ge(down, blk * FT + (f - 1) + 1)
                                nc.scalar.activation(hh[:, f - 1, 0, :], hid[:, (f - 1) % 4, :], ACT.Copy).then_inc(h_high, 1)
                        turned_high(blk + 1)
            for par in range(2):
                act.wait_ge(w_in[par], 48 * (E // 2 + 1))

        @block.gpsimd
        def _(pool):
            def low_halves(par):
                for n in range(3):
                    last = nc.gpsimd.tensor_tensor(wh[:, par, n, 1, :], raw[:, par, n, :], wh[:, par, n, 0, :], ALU.subtract)
                last.then_inc(w_low, 1)

            pool.wait_ge(w_high, 1)
            low_halves(0)
            with pool.Fori(0, E // 2) as pair:
                for par in range(2):
                    pool.wait_ge(w_high, pair * 2 + (par + 2))
                    low_halves(1 - par)

        @block.vector
        def _(dve):
            def turned_low(blk):
                dve.wait_ge(x_high, blk + 1)
                nc.vector.tensor_tensor(xh[:, 1], x_ps[:, :, :], xh[:, 0], ALU.subtract).then_inc(x_low, 1)

            dve.sem_inc(x_low, 1)
            dve.sem_inc(hidden, 4)
            dve.sem_inc(down, 8)
            dve.sem_inc(y_ready, 1)
            dve.sem_inc(y_out, 16)
            dve.wait_ge(const_in, 64)
            turned_low(0)
            with dve.Fori(0, E // 2) as pair:
                for par in range(2):
                    e = pair * 2 + par
                    lo, hi = span(dve, e)
                    nc.vector.tensor_copy(bcur[:, par], ball[:, :, bass.ds(e, 1), :].rearrange("p k a f -> p k (a f)")
                                          ).then_inc(biases, 1)
                    dve.wait_ge(biases, e + 1)
                    dve.sem_inc(passed, 1)
                    with dve.Fori(lo, hi) as blk:
                        for f in range(FT + 1):
                            if f < FT:
                                dve.wait_ge(gated, blk * FT + f + 1)
                                nc.vector.scalar_tensor_tensor(
                                    out=hid[:, f % 4, :], in0=gu[:, f % 4, 1, :], scalar=bcur[:, par, 1, f:f + 1],
                                    in1=act_out[:, f % 4, :], op0=ALU.add, op1=ALU.mult).then_inc(hidden, 1)
                            if f >= 1:
                                dve.wait_ge(h_high, blk * FT + (f - 1) + 1)
                                nc.vector.tensor_tensor(hh[:, f - 1, 1, :], hid[:, (f - 1) % 4, :], hh[:, f - 1, 0, :],
                                                        ALU.subtract).then_inc(h_low, 1)
                        turned_low(blk + 1)
                        dve.wait_ge(down, blk * FT + FT + 8)
                        dve.wait_ge(y_out, blk * 16 + 16)
                        nc.vector.tensor_tensor(yout[:, :, :], y_ps[:, :, :],
                                                b2[:, bass.ds(e, 1), :].to_broadcast([P, 2, C]), ALU.add).then_inc(y_ready, 1)


def stage_combine(nc, d, g, x1, gates, slots, out):
    with ExitStack() as ctx:
        def sb(name, shape, dt):
            return ctx.enter_context(nc.sbuf_tensor(name, shape, dt))

        def sem(name):
            return ctx.enter_context(nc.semaphore(name))

        ya = sb("ya", [P, NT, C], F32)
        yb = sb("yb", [P, NT, C], F32)
        stats = sb("fstats", [P, NT, 6], F32)
        agg = sb("fagg", [P, NT, 2], F32)
        dev = sb("fdev", [P, NT], F32)
        rstd = sb("frstd", [P, NT], F32)
        got = [sem(f"f_got{i}") for i in range(B * NCH)]
        own = sem("f_own")
        spread = sem("f_spread")
        rooted = sem("f_rooted")
        normed = sem("f_normed")
        out_done = sem("f_out_done")
        block = ctx.enter_context(nc.Block())

        @block.gpsimd
        def _(pool):
            for t in range(NT):
                for k, y in enumerate((ya, yb)):
                    pool.indirect_dma_start(out=y[:, t, :], out_offset=None, in_=g["ys"],
                                            in_offset=bass.IndirectOffsetOnAxis(ap=slots[:, k, t:t + 1], axis=0)
                                            ).then_inc(got[t // QT], 16)

        @block.vector
        def _(dve):
            for m in range(B * NCH):
                tiles = range(m * QT, (m + 1) * QT)
                some = slice(m * QT, (m + 1) * QT)
                dve.wait_ge(got[m], 16 * 2 * QT)
                for k, (a, b) in enumerate(((ya, x1), (yb, ya))):
                    for t in tiles:
                        last = nc.vector.scalar_tensor_tensor(out=(ya if k == 0 else yb)[:, t, :], in0=a[:, t, :],
                                                              scalar=gates[:, k, t:t + 1], in1=b[:, t, :],
                                                              op0=ALU.mult, op1=ALU.add)
                    last.then_inc(own, 1)
                    dve.wait_ge(own, 5 * m + k + 1)
                for t in tiles:
                    last = nc.vector.bn_stats(stats[:, t, :], yb[:, t, :])
                last.then_inc(own, 1)
                dve.wait_ge(own, 5 * m + 3)
                for t in tiles:
                    last = nc.vector.bn_aggr(agg[:, t, :], stats[:, t, :])
                last.then_inc(own, 1)
                dve.wait_ge(own, 5 * m + 4)
                nc.vector.tensor_scalar(agg[:, some, 1], agg[:, some, 1], EPS, None, ALU.add).then_inc(spread, 1)
                dve.wait_ge(rooted, m + 1)
                nc.vector.reciprocal(rstd[:, some], dev[:, some]).then_inc(own, 1)
                dve.wait_ge(own, 5 * m + 5)
                for t in tiles:
                    last = nc.vector.tensor_scalar(ya[:, t, :], yb[:, t, :], agg[:, t, 0:1], rstd[:, t:t + 1],
                                                   ALU.subtract, ALU.mult)
                last.then_inc(normed, 1)

        @block.scalar
        def _(act):
            for m in range(B * NCH):
                some = slice(m * QT, (m + 1) * QT)
                act.wait_ge(spread, m + 1)
                nc.scalar.activation(dev[:, some], agg[:, some, 1], ACT.Sqrt).then_inc(rooted, 1)

        @block.sync
        def _(sp):
            n = 0
            for m in range(B * NCH):
                b, c = divmod(m, NCH)
                sp.wait_ge(normed, m + 1)
                for run in place_rows(c):
                    (a, z), (q0, q1), row = run
                    sp.dma_start(rows_of(out, run, b * S + row), ya[a:z, m * QT + q0:m * QT + q1, :]).then_inc(out_done, 16)
                    n += 1
            sp.wait_ge(out_done, 16 * n)


def build(nc, d, out):
    g = scratch(nc)
    with ExitStack() as ctx:
        def sb(name, shape, dt):
            return ctx.enter_context(nc.sbuf_tensor(name, shape, dt))

        x1 = sb("x1", [P, NT, C], F32)
        logits = sb("logits", [P, NT, E], F32)
        gates = sb("gates", [P, 2, NT], F32)
        slots = sb("slots", [P, 2, NT], U32)
        bounds = sb("bounds", [P, 2 * E], I32)
        with nc.sbuf_tensor("heads_out", [P, NIT * NCH + 1, QT * QUAD * DK], F32) as heads_out:
            stage_project(nc, d, g)
            stage_attention(nc, d, g, heads_out)
            stage_norm(nc, d, g, heads_out, x1, logits)
        stage_route(nc, d, g, x1, logits, gates, slots, bounds)
        stage_experts(nc, d, g, bounds)
        stage_combine(nc, d, g, x1, gates, slots, out)


def layouts(i):
    swap = np.arange(C).reshape(H, 2, DK // 2)[:, ::-1].reshape(C)
    x = np.ascontiguousarray(i["L0_attn_x"]).reshape(NTOK, C)
    cols = lambda a: a.reshape(CT, P).T
    u, v = i["L0_attn_u"].reshape(C), i["L0_attn_v"].reshape(C)
    out = {
        "x": x,
        "xT": x.reshape(B * NCH, CH, CT, P).transpose(0, 3, 2, 1),
        "Wq": i["L0_attn_Wq"], "Wqs": i["L0_attn_Wq"][:, swap], "Wk": i["L0_attn_Wk"], "Wv": i["L0_attn_Wv"],
        "Wo": i["L0_attn_Wo"], "bo": i["L0_attn_bo"].reshape(1, C),
        "uv": np.stack([cols(u), cols(v), cols(v[swap])], 1),
        "rw": i["L0_ffn_router_w"].T,
        "w1": i["L0_ffn_w1_w"].transpose(0, 2, 1), "wg": i["L0_ffn_wg_w"].transpose(0, 2, 1),
        "w2": i["L0_ffn_w2_w"].transpose(0, 2, 1),
        "b1": i["L0_ffn_w1_b"].reshape(E, FT, P).transpose(2, 0, 1), "bg": i["L0_ffn_wg_b"].reshape(E, FT, P).transpose(2, 0, 1),
        "b2": i["L0_ffn_w2_b"].reshape(1, E * C),
    }
    out.update(constants())
    return {k: np.ascontiguousarray(a) for k, a in out.items()}


def scratch(nc, kind="Internal"):
    shapes = {"qs": ((6, B * C, W), F16), "ks": ((2, B * C, S), F16), "vs": ((B * NQ * S, P), F32),
              "xs": (((NBLK + 2) * BLK, C), F32), "ys": ((NBLK * BLK, C), F32)}
    return {k: nc.dram_tensor(f"scratch_{k}", s, dt, kind=kind).ap() for k, (s, dt) in shapes.items()}


def kernel(**inputs):
    import concourse.bacc as bacc
    from concourse.bass_utils import run_bass_kernel_spmd

    nc = bacc.Bacc("TRN2", target_bir_lowering=False, num_devices=1)
    arrays = {f"in_{k}": a for k, a in layouts({k: np.asarray(a) for k, a in inputs.items()}).items()}
    d = {k[3:]: nc.dram_tensor(k, a.shape, mybir.dt.from_np(a.dtype), kind="ExternalInput").ap() for k, a in arrays.items()}
    out = nc.dram_tensor("out", (NTOK, C), F32, kind="ExternalOutput").ap()
    build(nc, d, out)
    r = run_bass_kernel_spmd(nc, [arrays], core_ids=[0])
    return r.results[0]["out"].reshape(B, S, C)
```

```python
from contextlib import ExitStack

import numpy as np

import concourse.bass as bass
from concourse import mybir

F32 = mybir.dt.float32
F16 = mybir.dt.float16
BF16 = mybir.dt.bfloat16
I32 = mybir.dt.int32
U32 = mybir.dt.uint32
ALU = mybir.AluOpType
ACT = mybir.ActivationFunctionType
AX = mybir.AxisListType.X

P = 128
B, S, C, H = 2, 2048, 256, 16
DK = C // H
CT = C // P
E, F = 8, 1024
FT = F // P
CH = 512
NCH = S // CH
QT = CH // P
KT = S // P
QUAD = 4
NQ = H // QUAD
NIT = B * NQ
NTOK = B * S
NT = NTOK // P
W = S + 8
BLK = 256
NBLK = NTOK * 2 // BLK + E
SCALE = 1.0 / float(DK) ** 0.5
NEG = -1.0e30
EPS = 1e-5
NSPLIT = 3 * 2 * DK
ONE_ROW = NSPLIT
BIG_ROWS = NSPLIT + 1
LOW, HIGH, SUP = range(3)


def constants():
    half = DK // 2
    expo = np.arange(0, DK, 2, dtype=np.float32) / np.float32(DK)
    freq = (np.float32(1.0) / np.power(np.float32(10000.0), expo).astype(np.float32)).astype(np.float64)
    tok = np.arange(S, dtype=np.float64)
    rot = np.zeros((P, 4, S), np.float32)
    for r in range(P):
        d = r % DK
        w = freq[d % half]
        for k, base in ((0, 0.0), (2, float(S))):
            ang = (tok + base) * w
            own = -np.cos(ang) if d < half else np.cos(ang)
            rot[r, k] = own
            rot[r, k + 1] = np.sin(ang)
    ang = tok[None, :] * freq[:, None]
    p = np.concatenate([np.sin(ang), np.cos(ang)], 0)
    hi = p.astype(np.float16)
    lo = (p - hi.astype(np.float64)).astype(np.float16)
    pk = np.stack([hi, lo])
    r, s = np.meshgrid(np.arange(P), np.arange(P), indexing="ij")
    gt, lt, eq = ((np.where(m, 0.0, NEG)) for m in (r > s, r < s, r == s))
    mask = np.concatenate([gt] * 4 + [lt] + [eq] * 4, 1).astype(np.float32)
    ident = np.eye(P, dtype=np.float32)
    before = (r < s).astype(np.float32)
    order = np.tile(np.arange(E, 0, -1, dtype=np.float32), (P, NT))
    return {"c_rot": rot, "c_pk": pk, "c_mask": mask, "c_ident": ident, "c_before": before, "c_order": order}


def load_sinusoids(eng, d, keys, sem):
    for part3, half in ((0, 0), (1, 1), (2, 0)):
        eng.dma_start(keys[32 * part3 + DK:32 * part3 + 2 * DK],
                      d["c_pk"][half:half + 1].rearrange("a r n -> r a n").to_broadcast([DK, QUAD, S])).then_inc(sem, 16)


def stage_project(nc, d, g, ops):
    with ExitStack() as ctx:
        def sb(name, shape, dt):
            return ctx.enter_context(nc.sbuf_tensor(name, shape, dt))

        def sem(name):
            return ctx.enter_context(nc.semaphore(name))

        rot = sb("rot", [P, 4, S], F32)
        wq = sb("wq", [P, CT, C], F32)
        wqs = sb("wqs", [P, CT, C], F32)
        wk = sb("wk", [P, CT, C], F32)
        wv = sb("wv", [P, CT, C], F32)
        bias = sb("bias", [P, 3, CT], F32)
        xT = sb("xT", [P, 2, CT, CH], F32)
        stg = sb("stg", [P, 2, 8, CH], F16)
        vst = sb("vst", [P, 2, 2, H, 32], F32)
        prod = sb("prod", [P, 2, 4, CH], F32)
        turned = sb("turned", [P, 2, 2, CH], F32)
        pq = ctx.enter_context(nc.psum_tensor("pq", [P, 2, 3, CH], F32))
        pv = ctx.enter_context(nc.psum_tensor("pv", [P, 2, 2, C], F32))

        const_in = sem("a_const_in")
        x_in = [sem(f"a_x_in{i}") for i in range(2)]
        vst_ready = sem("a_vst_ready")
        qk_ready = sem("a_qk_ready")
        v_ready = sem("a_v_ready")
        first_hi = sem("a_first_hi")
        rot_prod = sem("a_rot_prod")
        rot_sum = sem("a_rot_sum")
        rot_hi = sem("a_rot_hi")
        dve_done = sem("a_dve_done")
        pool_done = sem("a_pool_done")
        v_copied = sem("a_v_copied")
        stored = [sem(f"a_stored{i}") for i in range(2)]
        v_stored = [sem(f"a_v_stored{i}") for i in range(2)]
        rot_in = [sem(f"a_rot_in{i}") for i in range(NCH)]
        ops_in = sem("a_ops_in")
        ops_set = sem("a_ops_set")
        misc = sem("a_misc")
        NCONST = 5
        OUT = 3 * 16
        VOUT = 2 * 16

        block = ctx.enter_context(nc.Block())

        @block.sync
        def _(sp):
            sp.dma_start(xT[:, 0], d["xT"][0]).then_inc(x_in[0], 16)
            for t, s in ((wq, "Wq"), (wqs, "Wqs"), (wk, "Wk"), (wv, "Wv")):
                sp.dma_start(t[:, :, :], d[s].rearrange("(t p) n -> p t n", p=P)).then_inc(const_in, 16)
            sp.dma_start(bias[:, :, :], d["uv"]).then_inc(const_in, 16)
            for ch in range(NCH):
                cols = slice(ch * CH, (ch + 1) * CH)
                sp.dma_start(rot[:, :, cols], d["c_rot"][:, :, cols]).then_inc(rot_in[ch], 16)
            with sp.Fori(0, B) as b:
                for ch in range(NCH):
                    sp.wait_ge(v_ready, b * 8 + 2 * ch + 1)
                    nxt = b * 4 + (ch + 1) if ch < NCH - 1 else (b * 4 + 4) % 8
                    sp.dma_start(xT[:, (ch + 1) % 2], d["xT"][bass.ds(nxt, 1)].rearrange("a p t n -> p (a t) n")
                                 ).then_inc(x_in[(ch + 1) % 2], 16)
                    for ht in range(CT):
                        st = b * 8 + (2 * ch + ht)
                        row = b * C + ht * P
                        sp.wait_ge(dve_done, st + 1 + 2)
                        sp.wait_ge(pool_done, st + 1 + 2)
                        q = g["qs"].rearrange("k r n -> r k n")
                        sp.dma_start(q[bass.ds(row, P), 0:4, ch * CH + 1:(ch + 1) * CH + 1],
                                     stg[:, ht, 0:4, :]).then_inc(stored[ht], 16)
                        o = 1 if ch == 0 else 0
                        sp.dma_start(q[bass.ds(row, P), 4:6, ch * CH + o:(ch + 1) * CH],
                                     stg[:, ht, 4:6, o:]).then_inc(stored[ht], 16)
                        k = g["ks"].rearrange("k r n -> r k n")
                        sp.dma_start(k[bass.ds(row, P), :, ch * CH:(ch + 1) * CH],
                                     stg[:, ht, 6:8, :]).then_inc(stored[ht], 16)
                        sp.wait_ge(v_copied, st + 1 + 2)
                        for i in range(2):
                            tok = ch * CH + (2 * ht + i) * P
                            for_quads = g["vs"].rearrange("(a t) n -> t a n", t=S)
                            sp.dma_start(for_quads[tok:tok + P, bass.ds(b * NQ, NQ), :],
                                         vst[:, ht, i].rearrange("p (a c) n -> p a (c n)", a=NQ)
                                         ).then_inc(v_stored[ht], 16)
            for s in stored:
                sp.wait_ge(s, OUT * (B * NCH + 1))
            with nc.allow_non_contiguous_dma(reason="one column"):
                q = g["qs"]
                for dst, src in ((0, 0), (1, 1), (2, 2), (3, 3), (4, 2), (5, 3)):
                    sp.dma_start(q[dst, :, 0:1], q[src, :, S:S + 1]).then_inc(misc, 16)
            sp.wait_ge(misc, 6 * 16)
            for s in v_stored:
                sp.wait_ge(s, VOUT * (B * NCH + 1))
            sp.wait_ge(x_in[0], 16 * (B * NCH // 2 + 1))

        @block.tensor
        def _(pe):
            pe.wait_ge(const_in, 16 * NCONST)
            with pe.Fori(0, B) as b:
                for ch in range(NCH):
                    xp = ch % 2
                    pe.wait_ge(x_in[xp], b * 32 + 16 * (ch // 2 + 1))
                    for ht in range(CT):
                        st = b * 8 + (2 * ch + ht)
                        pe.wait_ge(dve_done, st - 1 + 2)
                        pe.wait_ge(first_hi, 2 * (st - 1) + 4)
                        for n, w in enumerate((wq, wqs, wk)):
                            for ct in range(CT):
                                last = nc.tensor.matmul(pq[:, ht, n, :], w[:, ct, ht * P:(ht + 1) * P],
                                                        xT[:, xp, ct, :], start=(ct == 0), stop=(ct == CT - 1))
                        last.then_inc(qk_ready, 1)
                        pe.wait_ge(v_copied, st - 1 + 2)
                        for i in range(2):
                            for ct in range(CT):
                                t = 2 * ht + i
                                last = nc.tensor.matmul(pv[:, ht, i, :], xT[:, xp, ct, t * P:(t + 1) * P],
                                                        wv[:, ct, :], start=(ct == 0), stop=(ct == CT - 1))
                        last.then_inc(v_ready, 1)

        @block.scalar
        def _(act):
            act.dma_start(ops["ident"][:, :], d["c_ident"]).then_inc(ops_in, 16)
            act.dma_start(ops["maskf"][:, :], d["c_mask"]).then_inc(ops_in, 16)
            load_sinusoids(act, d, ops["kexp"], ops_in)
            act.wait_ge(const_in, 16 * NCONST)
            act.wait_ge(vst_ready, 2)
            act.sem_inc(first_hi, 4)
            act.sem_inc(v_copied, 2)
            with act.Fori(0, B) as b:
                for ch in range(NCH):
                    for ht in range(CT):
                        st = b * 8 + (2 * ch + ht)
                        use = b * 4 + ch
                        act.wait_ge(qk_ready, st + 1)
                        act.wait_ge(stored[ht], OUT * use + OUT)
                        nc.scalar.activation(stg[:, ht, 0, :], pq[:, ht, 0, :], ACT.Identity, bias=bias[:, 0, ht:ht + 1]
                                             ).then_inc(first_hi, 1)
                        nc.scalar.activation(stg[:, ht, 6, :], pq[:, ht, 2, :], ACT.Copy).then_inc(first_hi, 1)
                        act.wait_ge(v_ready, st + 1)
                        act.wait_ge(v_stored[ht], VOUT * use + VOUT)
                        nc.scalar.activation(vst[:, ht, :, :, 0:DK],
                                             pv[:, ht].rearrange("p i (h d) -> p i h d", h=H), ACT.Copy
                                             ).then_inc(v_copied, 1)
                        for n in range(2):
                            act.wait_ge(rot_sum, 2 * st + (n + 1))
                            nc.scalar.activation(stg[:, ht, 2 + 2 * n, :], turned[:, ht, n, :], ACT.Copy
                                                 ).then_inc(rot_hi, 1)

        @block.vector
        def _(dve):
            nc.vector.memset(vst[:, :, :, :, :], 0.0).then_inc(vst_ready, 1)
            dve.wait_ge(vst_ready, 1)
            nc.vector.memset(vst[:, :, :, :, DK:DK + 1], 1.0).then_inc(vst_ready, 1)
            dve.sem_inc(dve_done, 2)
            dve.wait_ge(const_in, 16 * NCONST)
            with dve.Fori(0, B) as b:
                for ch in range(NCH):
                    for ht in range(CT):
                        st = b * 8 + (2 * ch + ht)
                        use = b * 4 + ch
                        cols = slice(ch * CH, (ch + 1) * CH)
                        if ht == 0:
                            dve.wait_ge(rot_in[ch], 16)
                        dve.wait_ge(qk_ready, st + 1)
                        dve.wait_ge(pool_done, st - 1 + 2)
                        for n in (1, 3, 0, 2):
                            if n == 0:
                                dve.wait_ge(first_hi, 2 * st + 1 + 4)
                            nc.vector.scalar_tensor_tensor(
                                out=prod[:, ht, n, :], in0=pq[:, ht, n % 2, :], scalar=bias[:, 1 + n % 2, ht:ht + 1],
                                in1=rot[:, n, cols], op0=ALU.add, op1=ALU.mult).then_inc(rot_prod, 1)
                        dve.wait_ge(first_hi, 2 * st + 2 + 4)
                        dve.wait_ge(stored[ht], OUT * use + OUT)
                        nc.vector.scalar_tensor_tensor(
                            out=stg[:, ht, 1, :], in0=pq[:, ht, 0, :], scalar=bias[:, 0, ht:ht + 1],
                            in1=stg[:, ht, 0, :], op0=ALU.add, op1=ALU.subtract)
                        nc.vector.tensor_tensor(stg[:, ht, 7, :], pq[:, ht, 2, :], stg[:, ht, 6, :], ALU.subtract
                                                ).then_inc(dve_done, 1)

        @block.gpsimd
        def _(pool):
            pool.sem_inc(pool_done, 2)
            for s in stored:
                pool.sem_inc(s, OUT)
            for s in v_stored:
                pool.sem_inc(s, VOUT)
            nc.gpsimd.memset(ops["kexp"][ONE_ROW:ONE_ROW + 1], 1.0).then_inc(ops_set, 1)
            for c in range(NCH):
                nc.gpsimd.memset(ops["qop"][0:NSPLIT, c, SUP], 0.0).then_inc(ops_set, 1)
            pool.wait_ge(ops_set, 1 + NCH)
            pool.wait_ge(ops_in, 16 * 5)
            nc.gpsimd.tensor_copy(ops["mask"][:, :], ops["maskf"][:, :]).then_inc(ops_set, 1)
            nc.gpsimd.tensor_copy(ops["identb"][:, :], ops["ident"][:, :]).then_inc(ops_set, 1)
            with pool.Fori(0, B) as b:
                for ch in range(NCH):
                    for ht in range(CT):
                        st = b * 8 + (2 * ch + ht)
                        for n in range(2):
                            pool.wait_ge(rot_prod, 4 * st + (n + 3))
                            nc.gpsimd.tensor_tensor(turned[:, ht, n, :], prod[:, ht, 2 * n, :],
                                                    prod[:, ht, 2 * n + 1, :], ALU.add).then_inc(rot_sum, 1)
                        for n in range(2):
                            pool.wait_ge(rot_hi, 2 * st + (n + 1))
                            last = nc.gpsimd.tensor_tensor(stg[:, ht, 3 + 2 * n, :], turned[:, ht, n, :],
                                                           stg[:, ht, 2 + 2 * n, :], ALU.subtract)
                        last.then_inc(pool_done, 1)
            pool.wait_ge(ops_set, 3 + NCH)


def stage_attention(nc, d, g, ops, heads_out):
    with ExitStack() as ctx:
        def sb(name, shape, dt):
            return ctx.enter_context(nc.sbuf_tensor(name, shape, dt))

        def sem(name):
            return ctx.enter_context(nc.semaphore(name))

        NMAX = QUAD * QT * 5
        SLOTS = NMAX + 2
        STEPS = KT + 2
        TILES = 2 * STEPS
        NM = 3
        LEAD, TURN_LAG, OUT_AT = 25, 5, 3
        assert len(range(NMAX)) + 2 == SLOTS and (NMAX + LEAD) % NM == (SLOTS - 1) % NM
        NP = 4

        kmax = sb("kmax", [P, QUAD, S], F16)
        kexp, ident, identb, mask, qop = (ops[k] for k in ("kexp", "ident", "identb", "mask", "qop"))
        vals = sb("vals", [P, KT, QUAD, 32], F32)
        prob = sb("prob", [P, NP, 2, CH], F32)
        zero = sb("zero", [P, 4 * C], F32)
        part = sb("part", [P, QUAD * QT, 5], F32)
        nmax = sb("nmax", [P, QUAD * QT], F32)
        nmaxT = sb("nmaxT", [QUAD * QT, 2, P], F16)
        summed = sb("summed", [P, CH], F32)
        rsum = sb("rsum", [P, QT, QUAD], F32)
        sc_ps = ctx.enter_context(nc.psum_tensor("sc_ps", [P, 2, 2, CH], F32))
        mx_ps = ctx.enter_context(nc.psum_tensor("mx_ps", [P, NM, CH], F32))
        acc = ctx.enter_context(nc.psum_tensor("acc", [P, CH], F32))

        filled = sem("b_filled")
        kmax_set = sem("b_kmax_set")
        zeroed = sem("b_zeroed")
        zeros_out = sem("b_zeros_out")
        q_in = [sem(f"b_q_in{i}") for i in range(NCH)]
        m_in = [sem(f"b_m_in{i}") for i in range(NCH)]
        kmax_in = [sem(f"b_kmax_in{i}") for i in range(QUAD)]
        kexp_in = [sem(f"b_kexp_in{i}") for i in range(4)]
        scores = sem("b_scores")
        exped = sem("b_exped")
        pv_done = sem("b_pv_done")
        evacuated = sem("b_evacuated")
        slot_full = sem("b_slot_full")
        slot_free = sem("b_slot_free")
        max_done = sem("b_max_done")
        own = sem("b_own")

        NQDMA = 3 * 6 - 3
        q_total = [NQDMA + (3 if c == 0 else 0) for c in range(NCH)]

        block = ctx.enter_context(nc.Block())

        def entries(n_next, n_after):
            seq = [(1, k) for k in range(LEAD, NMAX)] if n_next else []
            if n_next:
                ahead = [(2, k) for k in range(LEAD)] if n_after else []
                seq += ahead[:TURN_LAG] + ["maxima"] + ahead[TURN_LAG:]
            seq.insert(OUT_AT if n_next else 0, "output")
            return seq

        BODY = entries(True, True)
        BEFORE = [(1, k) for k in range(NMAX)] + [(2, k) for k in range(TURN_LAG)] + ["maxima"] + [
            (2, k) for k in range(TURN_LAG, LEAD)]

        def number(n, pos, last):
            if last == "before":
                return pos
            if last and n == NIT * NCH - 1:
                return len(BEFORE) + SLOTS * (n - 1) + len(entries(True, False)) + pos
            return len(BEFORE) + SLOTS * n + pos

        def body_entries(c, last):
            return entries(not (last and c == NCH - 1), not (last and c >= NCH - 2))

        def load_kmax(eng, it, h):
            for part3, half in ((0, 0), (1, 1), (2, 0)):
                eng.dma_start(kmax[32 * part3:32 * part3 + DK, h], g["ks"][half, bass.ds(it * 4 * DK + h * DK, DK)]
                             ).then_inc(kmax_in[h], 16)

        def load_kexp(eng, it, s):
            cols = slice(s * CH, (s + 1) * CH)
            for part3, half in ((0, 0), (1, 1), (2, 0)):
                src = g["ks"][half, bass.ds(it * 4 * DK, 4 * DK), cols]
                eng.dma_start(kexp[32 * part3:32 * part3 + DK, :, cols], src.rearrange("(h r) n -> r h n", h=QUAD)
                             ).then_inc(kexp_in[s], 16)
            eng.dma_start(vals[:, 4 * s:4 * s + 4].rearrange("p k h d -> p k (h d)"),
                         g["vs"][bass.ds(it * S + s * CH, CH)].rearrange("(k p) n -> p k n", p=P)
                         ).then_inc(kexp_in[s], 16)

        @block.sync
        def _(sp):
            def load_q(it, c):
                row = it * 4 * DK
                k = 0
                for cls in range(3):
                    for part3, half in ((0, 0), (1, 0), (2, 1)):
                        base = 32 * part3
                        src = g["qs"][half, bass.ds(row, 4 * DK), c * CH:(c + 1) * CH]
                        sp.dma_start(qop[base:base + DK, c, cls], src.rearrange("(h r) n -> r h n", h=QUAD)
                                     ).then_inc(q_in[c], 16)
                        kind = 2 * (1 if cls == LOW else 2) + half
                        if cls != SUP:
                            src = g["qs"][kind, bass.ds(row, 4 * DK), c * CH:(c + 1) * CH]
                            sp.dma_start(qop[base + DK:base + 2 * DK, c, cls], src.rearrange("(h r) n -> r h n", h=QUAD)
                                         ).then_inc(q_in[c], 16)
                        elif c == 0:
                            src = g["qs"][2 + half, bass.ds(row, 4 * DK), 0:1]
                            with nc.allow_non_contiguous_dma(reason="place 0 alone"):
                                sp.dma_start(qop[base + DK:base + 2 * DK, c, cls, :, 0:1],
                                             src.rearrange("(h r) n -> r h n", h=QUAD)).then_inc(q_in[c], 16)

            def send_max(c, turned):
                sp.wait_ge(slot_free, turned + 1 + NM)
                for cls in range(3):
                    sp.dma_start(qop[ONE_ROW:ONE_ROW + 1, c, cls].rearrange("o h (q n) -> o (h q) n", q=QT),
                                 nmaxT[:, c % 2, :]).then_inc(m_in[c], 16)

            for c in range(3):
                load_q(0, c)
            send_max(0, BEFORE.index("maxima"))

            def turn(it, last):
                for c in range(NCH):
                    n = it * NCH + c
                    seq = body_entries(c, last)
                    if c < 1 or not last:
                        sp.wait_ge(evacuated, n + 2)
                        load_q(it + (c + 3) // NCH, (c + 3) % NCH)
                    if c == 2 and not last:
                        for h in (1, 2, 3):
                            sp.wait_ge(slot_full, number(n, seq.index((1, (h + 1) * QT * 5 - 1)), last) + 1)
                            load_kmax(sp, it + 1, h)
                    if c == 3 and not last:
                        for s in range(3):
                            sp.wait_ge(pv_done, n * STEPS + 4 * s + 4 + 2)
                            load_kexp(sp, it + 1, s)
                    if "maxima" in seq:
                        send_max((c + 1) % NCH, number(n, seq.index("maxima"), last))
                    if c == 1 and not last:
                        sp.wait_ge(slot_full, number(n, seq.index((2, QT * 5 - 1)), last) + 1)
                        load_kmax(sp, it + 1, 0)
                    if c == 3 and not last:
                        sp.wait_ge(pv_done, n * STEPS + STEPS + 2)
                        load_kexp(sp, it + 1, 3)

            with sp.Fori(0, NIT - 1) as it:
                turn(it, False)
            turn(NIT - 1, True)

        @block.tensor
        def _(pe):
            def max_tile(c, i, k, bank):
                h, qt = divmod(i, QT)
                T = c * QT + qt
                q = lambda cls: qop[0:NSPLIT, c, cls, h, qt * P:(qt + 1) * P]
                if k < 4:
                    others = [t for t in range(KT) if t != T][4 * k:4 * k + 4]
                    col = 0
                    while others:
                        cls = LOW if others[0] < T else HIGH
                        run = [others.pop(0)]
                        while others and others[0] == run[-1] + 1 and (LOW if others[0] < T else HIGH) == cls:
                            run.append(others.pop(0))
                        width = len(run) * P
                        last = nc.tensor.matmul(bank[:, col:col + width], q(cls), kmax[0:NSPLIT, h, run[0] * P:run[0] * P + width],
                                                start=True, stop=True, skip_group_check=True)
                        col += width
                else:
                    for n, cls in enumerate((LOW, HIGH, SUP)):
                        nc.tensor.matmul(bank[:, n * P:(n + 1) * P], q(cls), kmax[0:NSPLIT, h, T * P:(T + 1) * P],
                                         start=(n == 0), stop=False, skip_group_check=True)
                    last = nc.tensor.matmul(bank[:, 0:3 * P], identb[:, :], mask[:, 3 * P:6 * P],
                                            start=False, stop=True, skip_group_check=True)
                last.then_inc(slot_full, 1)

            def score_tile(c, t, pair, buf):
                for j in range(2):
                    h = 2 * pair + j
                    out = sc_ps[:, buf, j, :]
                    q = lambda cls, a, b: qop[0:BIG_ROWS, c, cls, h, a:b]
                    k = lambda kt: kexp[0:BIG_ROWS, h, kt * P:(kt + 1) * P]
                    if t < KT:
                        split = min(max(t - c * QT, 0), QT) * P
                        if t >= (c + 1) * QT:
                            split = CH
                        on_diag = c * QT <= t < (c + 1) * QT
                        if split:
                            last = nc.tensor.matmul(out[:, 0:split], k(t), q(HIGH, 0, split), start=True,
                                                    stop=True, skip_group_check=True)
                        if split < CH:
                            last = nc.tensor.matmul(out[:, split:CH], k(t), q(LOW, split, CH), start=True,
                                                    stop=not on_diag, skip_group_check=True)
                        if on_diag:
                            last = nc.tensor.matmul(out[:, split:split + P], identb[:, :], mask[:, 4 * P:5 * P],
                                                    start=False, stop=True, skip_group_check=True)
                    else:
                        cls, m = (HIGH, 0) if t == KT else (SUP, 5)
                        for n in range(QT):
                            nc.tensor.matmul(out[:, n * P:(n + 1) * P], k(c * QT + n), q(cls, n * P, (n + 1) * P),
                                             start=(n == 0), stop=False, skip_group_check=True)
                        last = nc.tensor.matmul(out[:, :], identb[:, :], mask[:, m * P:(m + 4) * P],
                                                start=False, stop=True, skip_group_check=True)
                last.then_inc(scores, 1)

            def values(c, t):
                for n in ([None] if t < KT else range(QT)):
                    for h in range(QUAD):
                        kt = t if t < KT else c * QT + n
                        cols = slice(0, CH) if t < KT else slice(n * P, (n + 1) * P)
                        last = nc.tensor.matmul(acc[32 * h:32 * h + 32, cols], vals[:, kt, h, :],
                                                prob[:, (2 * t + h // 2) % NP, h % 2, cols],
                                                start=(t == 0), stop=(t == STEPS - 1), skip_group_check=True)
                last.then_inc(pv_done, 1)

            def take_bank(n, pos, last):
                strict = pos == 0 and last != "before"
                pe.wait_ge(slot_free, number(n, pos, last) + (NM if strict else 1))
                return mx_ps[:, pos % NM, :]

            def needs_q(it, c):
                pe.wait_ge(q_in[c], (it + 1) * 16 * q_total[c])

            def emit(it, c, n, pos, entry, last):
                if entry == "maxima":
                    pe.wait_ge(max_done, n + 2)
                    bank = take_bank(n, pos, last)
                    nc.tensor.transpose(bank[0:QUAD * QT, 0:P], nmax[:, :], ident[:, :]).then_inc(slot_full, 1)
                elif entry == "output":
                    pe.wait_ge(evacuated, n + 2)
                    pe.wait_ge(filled, 1)
                    bank = take_bank(n, pos, last)
                    for qt in range(QT):
                        mm = nc.tensor.transpose(bank[:, qt * P:(qt + 1) * P], summed[:, qt * P:(qt + 1) * P], ident[:, :])
                    mm.then_inc(slot_full, 1)
                else:
                    off, k = entry
                    nit, nc_ = it + (c + off) // NCH, (c + off) % NCH
                    if k == 0:
                        needs_q(nit, nc_)
                    if nc_ == 0 and k % (QT * 5) == 0:
                        pe.wait_ge(kmax_in[k // (QT * 5)], (nit + 1) * 16 * 3)
                    max_tile(nc_, k // 5, k % 5, take_bank(n, pos, last))

            def first_scores(it, c, n):
                pe.wait_ge(m_in[c], (it + 1) * 16 * 3)
                pe.wait_ge(kexp_in[0], (it + 1) * 16 * 4)
                for pair in range(2):
                    pe.wait_ge(exped, n * TILES + pair + 1)
                    score_tile(c, 0, pair, pair)

            pe.wait_ge(kmax_set, 16 * 3)
            for pos, entry in enumerate(BEFORE):
                emit(-1, NCH - 1, -1, pos, entry, "before")
            first_scores(0, 0, 0)

            def turn(it, last):
                for c in range(NCH):
                    n = it * NCH + c
                    nit, nc_ = (it, c + 1) if c < NCH - 1 else (it + 1, 0)
                    more = not (last and c == NCH - 1)
                    seq = body_entries(c, last)
                    done = [0]

                    def pace(t, part):
                        due = min(len(seq), SLOTS * (3 * (t - 1) + part) // (3 * STEPS))
                        if not more:
                            due = len(seq) if t >= 2 else 0
                        while done[0] < due:
                            if seq[done[0]] == "output" and (t, part) < (1, 3):
                                return
                            emit(it, c, n, done[0], seq[done[0]], last)
                            done[0] += 1

                    for t in range(1, STEPS + 1):
                        if t < STEPS:
                            if t < KT and t % 4 == 0:
                                pe.wait_ge(kexp_in[t // 4], (it + 1) * 16 * 4)
                            for pair in range(2):
                                pe.wait_ge(exped, n * TILES + (2 * t + pair) - 2 + 1 + 2)
                                score_tile(c, t, pair, pair)
                                pace(t, pair + 1)
                        elif more:
                            first_scores(nit, nc_, n + 1)
                            pace(t, 2)
                        if t == 1:
                            pe.wait_ge(evacuated, n + 2)
                        pe.wait_ge(exped, n * TILES + 2 * t + 2)
                        values(c, t - 1)
                        pace(t, 3)

            with pe.Fori(0, NIT - 1) as it:
                turn(it, False)
            turn(NIT - 1, True)
            pe.wait_ge(evacuated, NIT * NCH + 2)
            pe.wait_ge(slot_free, number(NIT * NCH - 1, 1, True) + NM)
            for qt in range(QT):
                mm = nc.tensor.transpose(mx_ps[:, 0, qt * P:(qt + 1) * P], summed[:, qt * P:(qt + 1) * P], ident[:, :])
            mm.then_inc(slot_full, 1)

        @block.scalar
        def _(act):
            act.sem_inc(exped, 2)
            act.sem_inc(evacuated, 2)
            load_kmax(act, 0, 0)
            load_sinusoids(act, d, kmax, kmax_set)
            act.wait_ge(q_in[0], 16 * q_total[0])
            for h in range(1, QUAD):
                load_kmax(act, 0, h)
            for s in range(4):
                load_kexp(act, 0, s)

            def exp_step(c, n, t):
                for pair in range(2):
                    act.wait_ge(scores, n * TILES + 2 * t + pair + 1)
                    if pair == 0:
                        act.wait_ge(pv_done, n * STEPS + t - 1 + 2)
                    nc.scalar.activation(prob[:, (2 * t + pair) % NP, :, :], sc_ps[:, pair, :, :], ACT.Exp, scale=SCALE
                                         ).then_inc(exped, 1)

            exp_step(0, 0, 0)

            def turn(it, last):
                for c in range(NCH):
                    n = it * NCH + c
                    for t in range(1, STEPS):
                        exp_step(c, n, t)
                    if not (last and c == NCH - 1):
                        exp_step((c + 1) % NCH, n + 1, 0)
                    act.wait_ge(pv_done, (n + 1) * STEPS + 2)
                    seq = body_entries(c, last)
                    act.wait_ge(slot_full, number(n, seq.index("output"), last) + 1)
                    nc.scalar.activation(summed[:, :], acc[:, :], ACT.Copy).then_inc(evacuated, 1)

            with act.Fori(0, NIT - 1) as it:
                turn(it, False)
            turn(NIT - 1, True)

        @block.vector
        def _(dve):
            dve.sem_inc(slot_free, NM)
            nc.vector.memset(summed[:, :], 1.0).then_inc(filled, 1)

            def divide_output(it, c, bank_no, num):
                links = it * NCH + c + 1
                turn_, c_ = (it + 1, c - 1) if c else (it, NCH - 1)
                dve.wait_ge(slot_full, num + 1)
                bank = mx_ps[:, bank_no, :].rearrange("p (a h d) -> p a h d", a=QT, d=32)
                nc.vector.reciprocal(rsum[:, :, :], bank[:, :, :, DK]).then_inc(own, 1)
                dve.wait_ge(own, links)
                nc.vector.tensor_tensor(
                    heads_out[:, c_, :, bass.ds(turn_, 1), :].rearrange("p a o (h d) -> p a (o h) d", d=DK),
                    bank[:, :, :, 0:DK], rsum[:, :, :].unsqueeze(3).to_broadcast([P, QT, QUAD, DK]), ALU.mult
                    ).then_inc(slot_free, 1)

            def drain(it, c, n, seq, last):
                for pos, entry in enumerate(seq):
                    num = number(n, pos, last)
                    if entry == "output":
                        divide_output(it, c, pos % NM, num)
                        continue
                    dve.wait_ge(slot_full, num + 1)
                    if entry == "maxima":
                        nc.vector.tensor_copy(nmaxT[:, (c + 1) % 2, :], mx_ps[0:QUAD * QT, pos % NM, 0:P]
                                              ).then_inc(slot_free, 1)
                        continue
                    off, k = entry
                    if entry == (2, 0):
                        dve.wait_ge(max_done, n + 2)
                    width = CH if k % 5 < 3 else 3 * P
                    nc.vector.reduce_max(part[:, k // 5, k % 5:k % 5 + 1], mx_ps[:, pos % NM, 0:width], AX
                                         ).then_inc(slot_free, 1)
                    if entry == (1, NMAX - 1):
                        dve.wait_ge(slot_free, num + 1 + NM)
                        nc.vector.tensor_reduce(nmax[:, :], part[:, :, :], AX, ALU.max, negate=True).then_inc(max_done, 1)

            drain(-1, NCH - 1, -1, BEFORE, "before")

            def turn(it, last):
                for c in range(NCH):
                    drain(it, c, it * NCH + c, body_entries(c, last), last)

            with dve.Fori(0, NIT - 1) as it:
                turn(it, False)
            turn(NIT - 1, True)
            divide_output(NIT, 0, 0, number(NIT * NCH - 1, 1, True))

        @block.gpsimd
        def _(pool):
            pool.sem_inc(pv_done, 2)
            nc.gpsimd.memset(zero[:, :], 0.0).then_inc(zeroed, 1)
            pool.wait_ge(zeroed, 1)
            pool.wait_ge(evacuated, 1 + 2)
            zeros = 0
            for t, r0 in ((g["xs"], 0), (g["ys"], NTOK * 2)):
                for r in range(r0, t.shape[0], P * 4):
                    pool.dma_start(t[r:r + P * 4].rearrange("(p a) n -> p (a n)", p=P), zero[:, :]).then_inc(zeros_out, 16)
                    zeros += 1
            pool.wait_ge(zeros_out, 16 * zeros)


def place_rows(c):
    if c:
        return [((0, P), (0, QT), c * CH - 1)]
    return [((0, 1), (0, 1), S - 1), ((1, P), (0, 1), 0), ((0, P), (1, QT), P - 1)]


def rows_of(t, run, start):
    (a, z), (q0, q1), _ = run
    n = (z - a) * (q1 - q0)
    return t[bass.ds(start, n)].rearrange("(q p) n -> p q n", q=q1 - q0)


def stage_norm(nc, d, g, heads_out, x1, logits):
    with ExitStack() as ctx:
        def sb(name, shape, dt):
            return ctx.enter_context(nc.sbuf_tensor(name, shape, dt))

        def sem(name):
            return ctx.enter_context(nc.semaphore(name))

        GROUPS = B * NCH
        LAG = 2
        wo = sb("wo", [P, CT, C], F32)
        rw = sb("rw", [P, CT, E], F32)
        bo = sb("bo", [P, C], F32)
        ident = sb("identc", [P, P], F32)
        xres = sb("xres", [P, 2, QT, C], F32)
        xbias = sb("xbias", [P, 2, QT, C], F32)
        headsT = sb("headsT", [P, 2, QT, CT, P], F32)
        res = sb("res", [P, 2, QT, C], F32)
        stats = sb("stats", [P, 2, QT, 6], F32)
        agg = sb("agg", [P, 2, QT, 2], F32)
        dev = sb("dev", [P, 2, QT], F32)
        rstd = sb("rstd", [P, 2, QT], F32)
        xnormT = sb("xnormT", [P, 2, QT, CT, P], F32)
        t_ps = ctx.enter_context(nc.psum_tensor("t_ps", [P, QT, CT, P], F32))
        y_ps = ctx.enter_context(nc.psum_tensor("y_ps", [P, QT, C], F32))
        n_ps = ctx.enter_context(nc.psum_tensor("n_ps", [P, QT, CT, P], F32))
        l_ps = ctx.enter_context(nc.psum_tensor("l_ps", [P, CH], F32))

        const_in = sem("c_const_in")
        x_in = [sem(f"c_x_in{i}") for i in range(2)]
        biased = sem("c_biased")
        headsT_ps = sem("c_headsT_ps")
        headsT_sb = sem("c_headsT_sb")
        projected = sem("c_projected")
        residual = sem("c_residual")
        own = sem("c_own")
        spread = sem("c_spread")
        rooted = sem("c_rooted")
        normed = sem("c_normed")
        xT_ps = sem("c_xT_ps")
        xT_sb = sem("c_xT_sb")
        routed = sem("c_routed")
        logged = sem("c_logged")

        block = ctx.enter_context(nc.Block())

        @block.sync
        def _(sp):
            sp.dma_start(ident[:, :], d["c_ident"]).then_inc(const_in, 16)
            sp.dma_start(wo[:, :, :], d["Wo"].rearrange("(t p) n -> p t n", p=P)).then_inc(const_in, 16)
            sp.dma_start(bo[:, :], d["bo"].to_broadcast([P, C])).then_inc(const_in, 16)
            sp.dma_start(rw[:, :, :], d["rw"].rearrange("(t p) n -> p t n", p=P)).then_inc(const_in, 16)
            for m in range(GROUPS):
                b, c = divmod(m, NCH)
                if m >= 2:
                    sp.wait_ge(biased, m - 1)
                for run in place_rows(c):
                    (a, z), (q0, q1), row = run
                    sp.dma_start(xres[a:z, m % 2, q0:q1], rows_of(d["x"], run, b * S + row)).then_inc(x_in[m % 2], 16)

        @block.gpsimd
        def _(pool):
            pool.wait_ge(const_in, 64)
            for m in range(GROUPS):
                loads = sum(len(place_rows(k % NCH)) for k in range(m + 1) if k % 2 == m % 2)
                pool.wait_ge(x_in[m % 2], 16 * loads)
                if m >= 2:
                    pool.wait_ge(residual, m - 1)
                nc.gpsimd.tensor_tensor(xbias[:, m % 2], xres[:, m % 2],
                                        bo[:, :].unsqueeze(1).to_broadcast([P, QT, C]), ALU.add).then_inc(biased, 1)

        @block.tensor
        def _(pe):
            pe.wait_ge(const_in, 64)
            for m in range(GROUPS + LAG):
                r = m - LAG
                if m < GROUPS:
                    b, c = divmod(m, NCH)
                    if m >= 1:
                        pe.wait_ge(headsT_sb, m)
                    for qt in range(QT):
                        for ct in range(CT):
                            at = (1 + b * NQ + 2 * ct)
                            two = heads_out[:, c, qt, at:at + 2, :].rearrange("p a n -> p (a n)")
                            last = nc.tensor.transpose(t_ps[:, qt, ct, :], two, ident[:, :])
                    last.then_inc(headsT_ps, 1)
                if r >= 0:
                    pe.wait_ge(normed, r + 1)
                    if r >= 1:
                        pe.wait_ge(xT_sb, r)
                    for qt in range(QT):
                        for ct in range(CT):
                            last = nc.tensor.transpose(n_ps[:, qt, ct, :], x1[:, r * QT + qt, ct * P:(ct + 1) * P], ident[:, :])
                    last.then_inc(xT_ps, 1)
                if m < GROUPS:
                    pe.wait_ge(headsT_sb, m + 1)
                    if m >= 1:
                        pe.wait_ge(residual, m)
                    for qt in range(QT):
                        for ct in range(CT):
                            last = nc.tensor.matmul(y_ps[:, qt, :], headsT[:, m % 2, qt, ct, :], wo[:, ct, :],
                                                    start=(ct == 0), stop=(ct == CT - 1))
                    last.then_inc(projected, 1)
                if r >= 0:
                    pe.wait_ge(xT_sb, r + 1)
                    for qt in range(QT):
                        for ct in range(CT):
                            at = (r * QT + qt) * E
                            last = nc.tensor.matmul(l_ps[:, at:at + E], xnormT[:, r % 2, qt, ct, :], rw[:, ct, :],
                                                    start=(ct == 0), stop=(ct == CT - 1))
                    last.then_inc(routed, 1)

        @block.scalar
        def _(act):
            for m in range(GROUPS + LAG):
                if m < GROUPS:
                    act.wait_ge(headsT_ps, m + 1)
                    if m >= 2:
                        act.wait_ge(projected, m - 1)
                    nc.scalar.activation(headsT[:, m % 2], t_ps[:, :, :, :], ACT.Copy).then_inc(headsT_sb, 1)
                if 1 <= m <= GROUPS:
                    act.wait_ge(spread, m)
                    nc.scalar.activation(dev[:, (m - 1) % 2, :], agg[:, (m - 1) % 2, :, 1], ACT.Sqrt).then_inc(rooted, 1)
                r = m - LAG
                if r >= 0:
                    act.wait_ge(xT_ps, r + 1)
                    if r >= 2:
                        act.wait_ge(routed, r - 1)
                    nc.scalar.activation(xnormT[:, r % 2], n_ps[:, :, :, :], ACT.Copy).then_inc(xT_sb, 1)

        @block.vector
        def _(dve):
            for m in range(GROUPS):
                par = m % 2
                dve.wait_ge(projected, m + 1)
                dve.wait_ge(biased, m + 1)
                nc.vector.tensor_tensor(res[:, par], y_ps[:, :, :], xbias[:, par], ALU.add).then_inc(residual, 1)
                dve.wait_ge(residual, m + 1)
                for qt in range(QT):
                    last = nc.vector.bn_stats(stats[:, par, qt, :], res[:, par, qt, :])
                last.then_inc(own, 1)
                dve.wait_ge(own, 3 * m + 1)
                for qt in range(QT):
                    last = nc.vector.bn_aggr(agg[:, par, qt, :], stats[:, par, qt, :])
                last.then_inc(own, 1)
                dve.wait_ge(own, 3 * m + 2)
                nc.vector.tensor_scalar(agg[:, par, :, 1], agg[:, par, :, 1], EPS, None, ALU.add).then_inc(spread, 1)
                dve.wait_ge(rooted, m + 1)
                nc.vector.reciprocal(rstd[:, par, :], dev[:, par, :]).then_inc(own, 1)
                dve.wait_ge(own, 3 * m + 3)
                for qt in range(QT):
                    last = nc.vector.tensor_scalar(x1[:, m * QT + qt, :], res[:, par, qt, :], agg[:, par, qt, 0:1],
                                                   rstd[:, par, qt:qt + 1], ALU.subtract, ALU.mult)
                last.then_inc(normed, 1)
            dve.wait_ge(routed, GROUPS)
            nc.vector.tensor_copy(logits[:, :, :].rearrange("p t e -> p (t e)"), l_ps[:, 0:NT * E]).then_inc(logged, 1)
            dve.wait_ge(logged, 1)


def load_weights(eng, d, w, e, par):
    for n, name in enumerate(("wg", "w1")):
        eng.dma_start(w["raw"][:, par, n].rearrange("p (t f) -> p t f", t=CT),
                      d[name][bass.ds(e, 1)].rearrange("a (t p) f -> p (a t) f", p=P)).then_inc(w["in"][par], 16)
    eng.dma_start(w["raw"][:, par, 2].rearrange("p (t n) -> p t n", t=FT),
                  d["w2"][bass.ds(e, 1)].rearrange("a (t p) n -> p (a t) n", p=P)).then_inc(w["in"][par], 16)


def stage_route(nc, d, g, w, x1, logits, gates, slots, bounds):
    with ExitStack() as ctx:
        def sb(name, shape, dt):
            return ctx.enter_context(nc.sbuf_tensor(name, shape, dt))

        def sem(name):
            return ctx.enter_context(nc.semaphore(name))

        full = [P, NT, E]
        order = sb("order", full, F32)
        before = sb("before", [P, P], F32)
        ones = sb("ones", [P, P], F32)
        probs = sb("probs", full, F32)
        expd = sb("expd", full, F32)
        work = sb("work", full, F32)
        chosen = sb("chosen", [P, 2, NT, E], F32)
        both = sb("both", full, F32)
        rank = sb("rank", full, F32)
        total = sb("total", full, F32)
        run = sb("run", [P, 2, NT, E], F32)
        row = sb("row", [P, NT], F32)
        slotf = sb("slotf", [P, NT], F32)
        need = sb("need", [P, E], F32)
        needi = sb("needi", [P, E], I32)
        upto = sb("upto", [P, 2, E], F32)
        r_ps = ctx.enter_context(nc.psum_tensor("r_ps", [P, 2, NT * E], F32))

        const_in = sem("d_const_in")
        own = sem("d_own")
        shifted = sem("d_shifted")
        exped = sem("d_exped")
        hot = sem("d_hot")
        counted = sem("d_counted")
        placed = sem("d_placed")
        sent = sem("d_sent")
        block = ctx.enter_context(nc.Block())

        @block.sync
        def _(sp):
            sp.dma_start(order[:, :, :].rearrange("p t e -> p (t e)"), d["c_order"]).then_inc(const_in, 16)
            sp.dma_start(before[:, :], d["c_before"]).then_inc(const_in, 16)

        @block.scalar
        def _(act):
            load_weights(act, d, w, 0, 0)
            load_weights(act, d, w, 1, 1)
            act.wait_ge(shifted, 1)
            nc.scalar.activation(expd[:, :, :], work[:, :, :], ACT.Exp).then_inc(exped, 1)
            act.wait_ge(w["in"][0], 48)
            for n in range(3):
                last = nc.scalar.activation(w["half"][:, 0, n, 0, :], w["raw"][:, 0, n, :], ACT.Copy)
            last.then_inc(w["high"], 1)

        @block.tensor
        def _(pe):
            pe.wait_ge(hot, 1)
            rhs = both[:, :, :].rearrange("p t e -> p (t e)")
            nc.tensor.matmul(r_ps[:, 0, :], before[:, :], rhs, start=True, stop=True)
            nc.tensor.matmul(r_ps[:, 1, :], ones[:, :], rhs, start=True, stop=True).then_inc(counted, 1)

        @block.vector
        def _(dve):
            links = [0]

            def link(ins):
                links[0] += 1
                ins.then_inc(own, 1)
                dve.wait_ge(own, links[0])

            def wide(ap):
                return ap.unsqueeze(2).to_broadcast(full)

            V = nc.vector
            link(V.memset(ones[:, :], 1.0))
            link(V.reduce_max(row[:, :], logits[:, :, :], AX))
            V.tensor_tensor(work[:, :, :], logits[:, :, :], wide(row[:, :]), ALU.subtract).then_inc(shifted, 1)
            dve.wait_ge(exped, 1)
            link(V.reduce_sum(row[:, :], expd[:, :, :], AX))
            link(V.reciprocal(row[:, :], row[:, :]))
            link(V.tensor_tensor(probs[:, :, :], expd[:, :, :], wide(row[:, :]), ALU.mult))
            dve.wait_ge(const_in, 32)
            for k in range(2):
                link(V.reduce_max(gates[:, k, :], probs[:, :, :], AX))
                link(V.tensor_tensor(work[:, :, :], probs[:, :, :], wide(gates[:, k, :]), ALU.is_equal))
                link(V.tensor_tensor(work[:, :, :], work[:, :, :], order[:, :, :], ALU.mult))
                link(V.reduce_max(row[:, :], work[:, :, :], AX))
                link(V.tensor_tensor(chosen[:, k], work[:, :, :], wide(row[:, :]), ALU.is_equal))
                if k == 0:
                    link(V.scalar_tensor_tensor(out=probs[:, :, :], in0=chosen[:, 0], scalar=-2.0, in1=probs[:, :, :],
                                                op0=ALU.mult, op1=ALU.add))
            V.tensor_tensor(both[:, :, :], chosen[:, 0], chosen[:, 1], ALU.add).then_inc(hot, 1)
            dve.wait_ge(counted, 1)
            link(V.tensor_copy(rank[:, :, :].rearrange("p t e -> p (t e)"), r_ps[:, 0, :]))
            link(V.tensor_copy(total[:, :, :].rearrange("p t e -> p (t e)"), r_ps[:, 1, :]))
            link(V.tensor_copy(run[:, 0], total[:, :, :]))
            a, step = 0, 1
            while step < NT:
                link(V.tensor_copy(run[:, 1 - a, 0:step], run[:, a, 0:step]))
                link(V.tensor_tensor(run[:, 1 - a, step:], run[:, a, step:], run[:, a, 0:NT - step], ALU.add))
                a, step = 1 - a, 2 * step
            link(V.tensor_scalar(need[:, :], run[:, a, NT - 1], float(BLK - 1), None, ALU.add))
            link(V.tensor_copy(needi[:, :], need[:, :]))
            link(V.tensor_single_scalar(needi[:, :], needi[:, :], BLK.bit_length() - 1, ALU.arith_shift_right))
            link(V.tensor_copy(need[:, :], needi[:, :]))
            link(V.tensor_scalar(need[:, :], need[:, :], 1.0, None, ALU.max))
            link(V.tensor_copy(upto[:, 0], need[:, :]))
            u, step = 0, 1
            while step < E:
                link(V.tensor_copy(upto[:, 1 - u, 0:step], upto[:, u, 0:step]))
                link(V.tensor_tensor(upto[:, 1 - u, step:], upto[:, u, step:], upto[:, u, 0:E - step], ALU.add))
                u, step = 1 - u, 2 * step
            link(V.tensor_tensor(need[:, :], upto[:, u], need[:, :], ALU.subtract))
            link(V.tensor_copy(bounds[:, 0:E], need[:, :]))
            link(V.tensor_copy(bounds[:, E:2 * E], upto[:, u]))
            link(V.tensor_tensor(rank[:, :, :], rank[:, :, :], total[:, :, :], ALU.subtract))
            link(V.tensor_tensor(rank[:, :, :], rank[:, :, :], run[:, a], ALU.add))
            link(V.scalar_tensor_tensor(out=rank[:, :, :], in0=need[:, :].unsqueeze(1).to_broadcast(full),
                                        scalar=float(BLK), in1=rank[:, :, :], op0=ALU.mult, op1=ALU.add))
            for k in range(2):
                link(V.tensor_tensor(work[:, :, :], rank[:, :, :], chosen[:, k], ALU.mult))
                link(V.reduce_sum(slotf[:, :], work[:, :, :], AX))
                V.tensor_copy(slots[:, k, :], slotf[:, :]).then_inc(placed, 1)
                dve.wait_ge(placed, k + 1)
            dve.wait_ge(w["high"], 1)
            for n in range(3):
                last = V.tensor_tensor(w["half"][:, 0, n, 1, :], w["raw"][:, 0, n, :], w["half"][:, 0, n, 0, :], ALU.subtract)
            last.then_inc(w["low"], 1)

        @block.gpsimd
        def _(pool):
            for k in range(2):
                pool.wait_ge(placed, k + 1)
                for t in range(NT):
                    pool.indirect_dma_start(out=g["xs"], out_offset=bass.IndirectOffsetOnAxis(ap=slots[:, k, t:t + 1], axis=0),
                                            in_=x1[:, t, :], in_offset=None).then_inc(sent, 16)
            pool.wait_ge(sent, 16 * 2 * NT)


def stage_experts(nc, d, g, w, bounds):
    with ExitStack() as ctx:
        def sb(name, shape, dt):
            return ctx.enter_context(nc.sbuf_tensor(name, shape, dt))

        def sem(name):
            return ctx.enter_context(nc.semaphore(name))

        raw, wh, w_in, w_high, w_low = w["raw"], w["half"], w["in"], w["high"], w["low"]
        ball = sb("ball", [P, 2, E, FT], F32)
        bcur = sb("bcur", [P, 2, 2, FT], F32)
        b2 = sb("b2", [P, E, C], F32)
        ident = sb("idente", [P, P], F32)
        xin = sb("xin", [P, 2, C], F32)
        xh = sb("xh", [P, 2, CT, BLK], F16)
        act_out = sb("act_out", [P, 4, BLK], F32)
        hid = sb("hid", [P, 4, BLK], F32)
        hh = sb("hh", [P, FT, 2, BLK], F16)
        yout = sb("yout", [P, 2, C], F32)
        gu = ctx.enter_context(nc.psum_tensor("gu", [P, 4, 2, BLK], F32))
        y_ps = ctx.enter_context(nc.psum_tensor("ye_ps", [P, 2, C], F32))
        x_ps = ctx.enter_context(nc.psum_tensor("xe_ps", [P, CT, BLK], F32))

        const_in = sem("e_const_in")
        x_in = sem("e_x_in")
        x_turned = sem("e_x_turned")
        x_high = sem("e_x_high")
        x_low = sem("e_x_low")
        gu_ready = sem("e_gu_ready")
        gated = sem("e_gated")
        hidden = sem("e_hidden")
        h_high = sem("e_h_high")
        h_low = sem("e_h_low")
        down = sem("e_down")
        y_ready = sem("e_y_ready")
        y_out = sem("e_y_out")
        biases = sem("e_biases")
        passed = sem("e_passed")
        passed_w = sem("e_passed_w")
        PARTS = ((0, 0), (0, 1), (1, 0))

        block = ctx.enter_context(nc.Block())

        def span(eng, e):
            lo = eng.value_load(bounds[0:1, bass.ds(e, 1)], min_val=0, max_val=NBLK - 1)
            hi = eng.value_load(bounds[0:1, bass.ds(e + E, 1)], min_val=1, max_val=NBLK)
            return lo, hi

        @block.sync
        def _(sp):
            def load_x(blk):
                sp.dma_start(xin[:, :, :], g["xs"][bass.ds(blk * BLK, BLK)].rearrange("(i p) n -> p i n", p=P)
                             ).then_inc(x_in, 16)

            sp.dma_start(ident[:, :], d["c_ident"]).then_inc(const_in, 16)
            load_x(0)
            sp.dma_start(ball[:, 0], d["bg"]).then_inc(const_in, 16)
            sp.dma_start(ball[:, 1], d["b1"]).then_inc(const_in, 16)
            sp.dma_start(b2[:, :, :].rearrange("p e n -> p (e n)"), d["b2"].to_broadcast([P, E * C])).then_inc(const_in, 16)
            sp.wait_ge(x_turned, 1)
            load_x(1)
            with sp.Fori(0, E // 2) as pair:
                for par in range(2):
                    lo, hi = span(sp, pair * 2 + par)
                    with sp.Fori(lo, hi) as blk:
                        sp.wait_ge(x_turned, blk + 2)
                        load_x(blk + 2)
                        sp.wait_ge(y_ready, blk + 1 + 1)
                        sp.dma_start(g["ys"][bass.ds(blk * BLK, BLK)].rearrange("(i p) n -> p i n", p=P), yout[:, :, :]
                                     ).then_inc(y_out, 16)
            _, total = span(sp, E - 1)
            sp.wait_ge(y_out, total * 16 + 16)
            sp.sem_inc(passed, 1)
            sp.wait_ge(x_in, total * 16 + 32)
            sp.sem_inc(passed, 1)

        @block.tensor
        def _(pe):
            def turn_x(blk):
                pe.wait_ge(x_in, blk * 16 + 16)
                pe.wait_ge(x_low, blk + 1)
                for i in range(2):
                    for ct in range(CT):
                        last = nc.tensor.transpose(x_ps[:, ct, i * P:(i + 1) * P], xin[:, i, ct * P:(ct + 1) * P], ident[:, :])
                last.then_inc(x_turned, 1)

            def gate_up(blk, f, par):
                if f == 0:
                    pe.wait_ge(x_low, blk + 2)
                pe.wait_ge(hidden, blk * FT + f + 1)
                for n in range(2):
                    for ct in range(CT):
                        for k, (wp, xp) in enumerate(PARTS):
                            at = ct * F + f * P
                            last = nc.tensor.matmul(gu[:, f % 4, n, :], wh[:, par, n, wp, at:at + P], xh[:, xp, ct, :],
                                                    start=(ct == 0 and k == 0), stop=(ct == CT - 1 and k == 2),
                                                    skip_group_check=True)
                last.then_inc(gu_ready, 1)

            def down_product(blk, f, par):
                pe.wait_ge(h_low, blk * FT + f + 1)
                if f == 0:
                    pe.wait_ge(y_ready, blk + 1)
                for i in range(2):
                    for k, (wp, hp) in enumerate(PARTS):
                        last = nc.tensor.matmul(y_ps[:, i, :], hh[:, f, hp, i * P:(i + 1) * P],
                                                wh[:, par, 2, wp, f * C:(f + 1) * C],
                                                start=(f == 0 and i == 0 and k == 0), stop=(f == FT - 1 and k == 2),
                                                skip_group_check=True)
                last.then_inc(down, 1)

            pe.wait_ge(const_in, 64)
            turn_x(0)
            with pe.Fori(0, E // 2) as pair:
                for par in range(2):
                    lo, hi = span(pe, pair * 2 + par)
                    pe.wait_ge(w_low, pair * 2 + (par + 1))
                    pe.sem_inc(passed, 1)
                    with pe.Fori(lo, hi) as blk:
                        for f in range(FT):
                            gate_up(blk, f, par)
                            if f >= 2:
                                down_product(blk, f - 2, par)
                        turn_x(blk + 1)
                        down_product(blk, FT - 2, par)
                        down_product(blk, FT - 1, par)

        @block.scalar
        def _(act):
            def turned_high(blk):
                act.wait_ge(x_turned, blk + 1)
                nc.scalar.activation(xh[:, 0], x_ps[:, :, :], ACT.Copy).then_inc(x_high, 1)

            turned_high(0)
            with act.Fori(0, E // 2) as pair:
                for par in range(2):
                    e = pair * 2 + par
                    lo, hi = span(act, e)
                    act.wait_ge(w_low, e + 1)
                    load_weights(act, d, w, (e + 2) % E, par)
                    act.wait_ge(biases, e + 1)
                    with act.Fori(lo, hi) as blk:
                        for f in range(FT + 1):
                            if f < FT:
                                act.wait_ge(gu_ready, blk * FT + f + 1)
                                nc.scalar.activation(act_out[:, f % 4, :], gu[:, f % 4, 0, :], ACT.Gelu,
                                                     bias=bcur[:, par, 0, f:f + 1]).then_inc(gated, 1)
                            if f >= 1:
                                act.wait_ge(hidden, blk * FT + (f - 1) + 1 + 4)
                                act.wait_ge(down, blk * FT + (f - 1) + 1)
                                nc.scalar.activation(hh[:, f - 1, 0, :], hid[:, (f - 1) % 4, :], ACT.Copy).then_inc(h_high, 1)
                        turned_high(blk + 1)
            for par in range(2):
                act.wait_ge(w_in[par], 48 * (E // 2 + 1))

        @block.gpsimd
        def _(pool):
            with pool.Fori(0, E // 2) as pair:
                for par in range(2):
                    e = pair * 2 + par
                    lo, _ = span(pool, e)
                    pool.wait_ge(down, lo * FT + 8)
                    pool.wait_ge(w_in[1 - par], (pair + (1 + par)) * 48)
                    pool.sem_inc(passed_w, 1)
                    for n in range(3):
                        last = nc.gpsimd.tensor_copy(wh[:, 1 - par, n, 0, :], raw[:, 1 - par, n, :])
                    last.then_inc(w_high, 1)
                    pool.wait_ge(w_high, e + 2)
                    for n in range(3):
                        last = nc.gpsimd.tensor_tensor(wh[:, 1 - par, n, 1, :], raw[:, 1 - par, n, :],
                                                       wh[:, 1 - par, n, 0, :], ALU.subtract)
                    last.then_inc(w_low, 1)

        @block.vector
        def _(dve):
            def turned_low(blk):
                dve.wait_ge(x_high, blk + 1)
                nc.vector.tensor_tensor(xh[:, 1], x_ps[:, :, :], xh[:, 0], ALU.subtract).then_inc(x_low, 1)

            dve.sem_inc(x_low, 1)
            dve.sem_inc(hidden, 4)
            dve.sem_inc(down, 8)
            dve.sem_inc(y_ready, 1)
            dve.sem_inc(y_out, 16)
            dve.wait_ge(const_in, 64)
            turned_low(0)
            with dve.Fori(0, E // 2) as pair:
                for par in range(2):
                    e = pair * 2 + par
                    lo, hi = span(dve, e)
                    nc.vector.tensor_copy(bcur[:, par], ball[:, :, bass.ds(e, 1), :].rearrange("p k a f -> p k (a f)")
                                          ).then_inc(biases, 1)
                    dve.wait_ge(biases, e + 1)
                    dve.sem_inc(passed, 1)
                    with dve.Fori(lo, hi) as blk:
                        for f in range(FT + 1):
                            if f < FT:
                                dve.wait_ge(gated, blk * FT + f + 1)
                                nc.vector.scalar_tensor_tensor(
                                    out=hid[:, f % 4, :], in0=gu[:, f % 4, 1, :], scalar=bcur[:, par, 1, f:f + 1],
                                    in1=act_out[:, f % 4, :], op0=ALU.add, op1=ALU.mult).then_inc(hidden, 1)
                            if f >= 1:
                                dve.wait_ge(h_high, blk * FT + (f - 1) + 1)
                                nc.vector.tensor_tensor(hh[:, f - 1, 1, :], hid[:, (f - 1) % 4, :], hh[:, f - 1, 0, :],
                                                        ALU.subtract).then_inc(h_low, 1)
                        turned_low(blk + 1)
                        dve.wait_ge(down, blk * FT + FT + 8)
                        dve.wait_ge(y_out, blk * 16 + 16)
                        nc.vector.tensor_tensor(yout[:, :, :], y_ps[:, :, :],
                                                b2[:, bass.ds(e, 1), :].to_broadcast([P, 2, C]), ALU.add).then_inc(y_ready, 1)


def stage_combine(nc, d, g, x1, gates, slots, out):
    with ExitStack() as ctx:
        def sb(name, shape, dt):
            return ctx.enter_context(nc.sbuf_tensor(name, shape, dt))

        def sem(name):
            return ctx.enter_context(nc.semaphore(name))

        ya = sb("ya", [P, NT, C], F32)
        yb = sb("yb", [P, NT, C], F32)
        stats = sb("fstats", [P, NT, 6], F32)
        agg = sb("fagg", [P, NT, 2], F32)
        dev = sb("fdev", [P, NT], F32)
        rstd = sb("frstd", [P, NT], F32)
        got = [sem(f"f_got{i}") for i in range(B * NCH)]
        own = sem("f_own")
        spread = sem("f_spread")
        rooted = sem("f_rooted")
        normed = sem("f_normed")
        out_done = sem("f_out_done")
        block = ctx.enter_context(nc.Block())

        @block.gpsimd
        def _(pool):
            for t in range(NT):
                for k, y in enumerate((ya, yb)):
                    pool.indirect_dma_start(out=y[:, t, :], out_offset=None, in_=g["ys"],
                                            in_offset=bass.IndirectOffsetOnAxis(ap=slots[:, k, t:t + 1], axis=0)
                                            ).then_inc(got[t // QT], 16)

        @block.vector
        def _(dve):
            for m in range(B * NCH):
                tiles = range(m * QT, (m + 1) * QT)
                some = slice(m * QT, (m + 1) * QT)
                dve.wait_ge(got[m], 16 * 2 * QT)
                for k, (a, b) in enumerate(((ya, x1), (yb, ya))):
                    for t in tiles:
                        last = nc.vector.scalar_tensor_tensor(out=(ya if k == 0 else yb)[:, t, :], in0=a[:, t, :],
                                                              scalar=gates[:, k, t:t + 1], in1=b[:, t, :],
                                                              op0=ALU.mult, op1=ALU.add)
                    last.then_inc(own, 1)
                    dve.wait_ge(own, 5 * m + k + 1)
                for t in tiles:
                    last = nc.vector.bn_stats(stats[:, t, :], yb[:, t, :])
                last.then_inc(own, 1)
                dve.wait_ge(own, 5 * m + 3)
                for t in tiles:
                    last = nc.vector.bn_aggr(agg[:, t, :], stats[:, t, :])
                last.then_inc(own, 1)
                dve.wait_ge(own, 5 * m + 4)
                nc.vector.tensor_scalar(agg[:, some, 1], agg[:, some, 1], EPS, None, ALU.add).then_inc(spread, 1)
                dve.wait_ge(rooted, m + 1)
                nc.vector.reciprocal(rstd[:, some], dev[:, some]).then_inc(own, 1)
                dve.wait_ge(own, 5 * m + 5)
                for t in tiles:
                    last = nc.vector.tensor_scalar(ya[:, t, :], yb[:, t, :], agg[:, t, 0:1], rstd[:, t:t + 1],
                                                   ALU.subtract, ALU.mult)
                last.then_inc(normed, 1)

        @block.scalar
        def _(act):
            for m in range(B * NCH):
                some = slice(m * QT, (m + 1) * QT)
                act.wait_ge(spread, m + 1)
                nc.scalar.activation(dev[:, some], agg[:, some, 1], ACT.Sqrt).then_inc(rooted, 1)

        @block.sync
        def _(sp):
            n = 0
            for m in range(B * NCH):
                b, c = divmod(m, NCH)
                sp.wait_ge(normed, m + 1)
                for run in place_rows(c):
                    (a, z), (q0, q1), row = run
                    sp.dma_start(rows_of(out, run, b * S + row), ya[a:z, m * QT + q0:m * QT + q1, :]).then_inc(out_done, 16)
                    n += 1
            sp.wait_ge(out_done, 16 * n)


def build(nc, d, out):
    g = scratch(nc)
    with ExitStack() as ctx:
        def sb(name, shape, dt):
            return ctx.enter_context(nc.sbuf_tensor(name, shape, dt))

        x1 = sb("x1", [P, NT, C], F32)
        logits = sb("logits", [P, NT, E], F32)
        gates = sb("gates", [P, 2, NT], F32)
        slots = sb("slots", [P, 2, NT], U32)
        bounds = sb("bounds", [P, 2 * E], I32)
        with ExitStack() as inner:
            def isb(name, shape, dt):
                return inner.enter_context(nc.sbuf_tensor(name, shape, dt))

            ops = {
                "kexp": isb("kexp", [P, QUAD, S], F16),
                "qop": isb("qop", [P, NCH, 3, QUAD, CH], F16),
                "ident": isb("ident", [P, P], F32), "identb": isb("identb", [P, P], BF16),
                "maskf": isb("maskf", [P, 9 * P], F32), "mask": isb("mask", [P, 9 * P], BF16),
            }
            stage_project(nc, d, g, ops)
            with nc.sbuf_tensor("heads_out", [P, NCH, QT, NIT + 1, QUAD * DK], F32) as heads_out:
                stage_attention(nc, d, g, ops, heads_out)
                stage_norm(nc, d, g, heads_out, x1, logits)
        with ExitStack() as inner:
            w = {
                "raw": inner.enter_context(nc.sbuf_tensor("raw", [P, 2, 3, CT * F], F32)),
                "half": inner.enter_context(nc.sbuf_tensor("half", [P, 2, 3, 2, CT * F], F16)),
                "in": [inner.enter_context(nc.semaphore(f"w_in{i}")) for i in range(2)],
                "high": inner.enter_context(nc.semaphore("w_high")),
                "low": inner.enter_context(nc.semaphore("w_low")),
            }
            stage_route(nc, d, g, w, x1, logits, gates, slots, bounds)
            stage_experts(nc, d, g, w, bounds)
        stage_combine(nc, d, g, x1, gates, slots, out)


def layouts(i):
    swap = np.arange(C).reshape(H, 2, DK // 2)[:, ::-1].reshape(C)
    x = np.ascontiguousarray(i["L0_attn_x"]).reshape(NTOK, C)
    cols = lambda a: a.reshape(CT, P).T
    u, v = i["L0_attn_u"].reshape(C), i["L0_attn_v"].reshape(C)
    out = {
        "x": x,
        "xT": x.reshape(B * NCH, CH, CT, P).transpose(0, 3, 2, 1),
        "Wq": i["L0_attn_Wq"], "Wqs": i["L0_attn_Wq"][:, swap], "Wk": i["L0_attn_Wk"], "Wv": i["L0_attn_Wv"],
        "Wo": i["L0_attn_Wo"], "bo": i["L0_attn_bo"].reshape(1, C),
        "uv": np.stack([cols(u), cols(v), cols(v[swap])], 1),
        "rw": i["L0_ffn_router_w"].T,
        "w1": i["L0_ffn_w1_w"].transpose(0, 2, 1), "wg": i["L0_ffn_wg_w"].transpose(0, 2, 1),
        "w2": i["L0_ffn_w2_w"].transpose(0, 2, 1),
        "b1": i["L0_ffn_w1_b"].reshape(E, FT, P).transpose(2, 0, 1), "bg": i["L0_ffn_wg_b"].reshape(E, FT, P).transpose(2, 0, 1),
        "b2": i["L0_ffn_w2_b"].reshape(1, E * C),
    }
    out.update(constants())
    return {k: np.ascontiguousarray(a) for k, a in out.items()}


def scratch(nc, kind="Internal"):
    shapes = {"qs": ((6, B * C, W), F16), "ks": ((2, B * C, S), F16), "vs": ((B * NQ * S, P), F32),
              "xs": (((NBLK + 2) * BLK, C), F32), "ys": ((NBLK * BLK, C), F32)}
    return {k: nc.dram_tensor(f"scratch_{k}", s, dt, kind=kind).ap() for k, (s, dt) in shapes.items()}


def kernel(**inputs):
    import concourse.bacc as bacc
    from concourse.bass_utils import run_bass_kernel_spmd

    nc = bacc.Bacc("TRN2", target_bir_lowering=False, num_devices=1)
    arrays = {f"in_{k}": a for k, a in layouts({k: np.asarray(a) for k, a in inputs.items()}).items()}
    d = {k[3:]: nc.dram_tensor(k, a.shape, mybir.dt.from_np(a.dtype), kind="ExternalInput").ap() for k, a in arrays.items()}
    out = nc.dram_tensor("out", (NTOK, C), F32, kind="ExternalOutput").ap()
    build(nc, d, out)
    r = run_bass_kernel_spmd(nc, [arrays], core_ids=[0])
    return r.results[0]["out"].reshape(B, S, C)
```

```python
from contextlib import ExitStack

import numpy as np

import concourse.bass as bass
from concourse import mybir

F32 = mybir.dt.float32
F16 = mybir.dt.float16
BF16 = mybir.dt.bfloat16
I32 = mybir.dt.int32
U32 = mybir.dt.uint32
ALU = mybir.AluOpType
ACT = mybir.ActivationFunctionType
AX = mybir.AxisListType.X

P = 128
B, S, C, H = 2, 2048, 256, 16
DK = C // H
CT = C // P
E, F = 8, 1024
FT = F // P
CH = 512
NCH = S // CH
QT = CH // P
KT = S // P
QUAD = 4
NQ = H // QUAD
NIT = B * NQ
NTOK = B * S
NT = NTOK // P
W = S + 8
BLK = 256
NBLK = NTOK * 2 // BLK + E
SCALE = 1.0 / float(DK) ** 0.5
NEG = -1.0e30
EPS = 1e-5
NSPLIT = 3 * 2 * DK
ONE_ROW = NSPLIT
BIG_ROWS = NSPLIT + 1
HALVES = ((0, 0), (0, 1), (1, 0))
LOW, HIGH, SUP = range(3)


def constants():
    half = DK // 2
    expo = np.arange(0, DK, 2, dtype=np.float32) / np.float32(DK)
    freq = (np.float32(1.0) / np.power(np.float32(10000.0), expo).astype(np.float32)).astype(np.float64)
    tok = np.arange(S, dtype=np.float64)
    rot = np.zeros((P, 4, S), np.float32)
    for r in range(P):
        d = r % DK
        w = freq[d % half]
        for k, base in ((0, 0.0), (2, float(S))):
            ang = (tok + base) * w
            own = -np.cos(ang) if d < half else np.cos(ang)
            rot[r, k] = own
            rot[r, k + 1] = np.sin(ang)
    ang = tok[None, :] * freq[:, None]
    p = np.concatenate([np.sin(ang), np.cos(ang)], 0)
    hi = p.astype(np.float16)
    lo = (p - hi.astype(np.float64)).astype(np.float16)
    pk = np.stack([hi, lo])
    r, s = np.meshgrid(np.arange(P), np.arange(P), indexing="ij")
    gt, lt, eq = ((np.where(m, 0.0, NEG)) for m in (r > s, r < s, r == s))
    mask = np.concatenate([gt, lt, eq], 1).astype(np.float32)
    ident = np.eye(P, dtype=np.float32)
    before = (r < s).astype(np.float32)
    order = np.tile(np.arange(E, 0, -1, dtype=np.float32), (P, NT))
    return {"c_rot": rot, "c_pk": pk, "c_mask": mask, "c_ident": ident, "c_before": before, "c_order": order}


def load_sinusoids(eng, d, keys, sem):
    for part3, half in ((0, 0), (1, 1), (2, 0)):
        eng.dma_start(keys[32 * part3 + DK:32 * part3 + 2 * DK],
                      d["c_pk"][half:half + 1].rearrange("a r n -> r a n").to_broadcast([DK, QUAD, S])).then_inc(sem, 16)


def stage_project(nc, d, g, ops):
    with ExitStack() as ctx:
        def sb(name, shape, dt):
            return ctx.enter_context(nc.sbuf_tensor(name, shape, dt))

        def sem(name):
            return ctx.enter_context(nc.semaphore(name))

        rot = sb("rot", [P, 4, S], F32)
        wh = sb("wh_a", [P, 4, 2, CT * C], F16)
        bias = sb("bias", [P, 3, CT], F32)
        xT = sb("xT", [P, CT, CH], F32)
        xh = sb("xh_a", [P, 2, 2, CT, CH], F16)
        stg = sb("stg", [P, 2, 8, CH], F16)
        vst = sb("vst", [P, 2, 2, H, 32], F32)
        prod = sb("prod", [P, 2, 4, CH], F32)
        turned = sb("turned", [P, 2, 2, CH], F32)
        pq = ctx.enter_context(nc.psum_tensor("pq", [P, 2, 3, CH], F32))
        pv = ctx.enter_context(nc.psum_tensor("pv", [P, 2, 2, C], F32))

        const_in = sem("a_const_in")
        x_in = sem("a_x_in")
        w_high = sem("a_w_high")
        w_low = sem("a_w_low")
        x_high = sem("a_x_high")
        x_low = sem("a_x_low")
        vst_ready = sem("a_vst_ready")
        qk_ready = sem("a_qk_ready")
        v_ready = sem("a_v_ready")
        first_hi = sem("a_first_hi")
        rot_prod = sem("a_rot_prod")
        rot_sum = sem("a_rot_sum")
        rot_hi = sem("a_rot_hi")
        dve_done = sem("a_dve_done")
        pool_done = sem("a_pool_done")
        v_copied = sem("a_v_copied")
        stored = [sem(f"a_stored{i}") for i in range(2)]
        v_stored = [sem(f"a_v_stored{i}") for i in range(2)]
        rot_in = [sem(f"a_rot_in{i}") for i in range(NCH)]
        ops_in = sem("a_ops_in")
        ops_set = sem("a_ops_set")
        place0_in = sem("a_place0_in")
        NCONST = 5
        OUT = 3 * 16
        VOUT = 2 * 16

        raw_w = prod[:, 0]
        block = ctx.enter_context(nc.Block())

        @block.sync
        def _(sp):
            for n, s in enumerate(("Wq", "Wqs", "Wk", "Wv")):
                sp.dma_start(raw_w[:, n].rearrange("p (t n) -> p t n", t=CT), d[s].rearrange("(t p) n -> p t n", p=P)
                             ).then_inc(const_in, 16)
            sp.dma_start(xT[:, :, :], d["xT"][0]).then_inc(x_in, 16)
            sp.dma_start(bias[:, :, :], d["uv"]).then_inc(const_in, 16)
            for ch in range(NCH):
                cols = slice(ch * CH, (ch + 1) * CH)
                sp.dma_start(rot[:, :, cols], d["c_rot"][:, :, cols]).then_inc(rot_in[ch], 16)
            sp.wait_ge(x_low, 1)
            sp.dma_start(xT[:, :, :], d["xT"][1]).then_inc(x_in, 16)
            with sp.Fori(0, B) as b:
                for ch in range(NCH):
                    sp.wait_ge(x_low, b * NCH + (ch + 2))
                    nxt = b * 4 + (ch + 2) if ch < NCH - 2 else (b * 4 + (ch + 2)) % 8
                    sp.dma_start(xT[:, :, :], d["xT"][bass.ds(nxt, 1)].rearrange("a p t n -> p (a t) n")
                                 ).then_inc(x_in, 16)
                    for ht in range(CT):
                        st = b * 8 + (2 * ch + ht)
                        row = b * C + ht * P
                        sp.wait_ge(dve_done, st + 1 + 2)
                        sp.wait_ge(pool_done, st + 1 + 2)
                        q = g["qs"].rearrange("k r n -> r k n")
                        sp.dma_start(q[bass.ds(row, P), 0:4, ch * CH + 1:(ch + 1) * CH + 1],
                                     stg[:, ht, 0:4, :]).then_inc(stored[ht], 16)
                        o = 1 if ch == 0 else 0
                        sp.dma_start(q[bass.ds(row, P), 4:6, ch * CH + o:(ch + 1) * CH],
                                     stg[:, ht, 4:6, o:]).then_inc(stored[ht], 16)
                        k = g["ks"].rearrange("k r n -> r k n")
                        sp.dma_start(k[bass.ds(row, P), :, ch * CH:(ch + 1) * CH],
                                     stg[:, ht, 6:8, :]).then_inc(stored[ht], 16)
                        sp.wait_ge(v_copied, st + 1 + 2)
                        for i in range(2):
                            tok = ch * CH + (2 * ht + i) * P
                            for_quads = g["vs"].rearrange("(a t) n -> t a n", t=S)
                            sp.dma_start(for_quads[tok:tok + P, bass.ds(b * NQ, NQ), :],
                                         vst[:, ht, i].rearrange("p (a c) n -> p a (c n)", a=NQ)
                                         ).then_inc(v_stored[ht], 16)
            for s in stored:
                sp.wait_ge(s, OUT * (B * NCH + 1))
            with nc.allow_non_contiguous_dma(reason="one column"):
                q = g["qs"]
                for dst, src in ((0, 0), (1, 1), (2, 2), (3, 3), (4, 2), (5, 3)):
                    sp.dma_start(q[dst, :, 0:1], q[src, :, S:S + 1]).then_inc(place0_in, 16)
            sp.wait_ge(place0_in, 6 * 16)
            for s in v_stored:
                sp.wait_ge(s, VOUT * (B * NCH + 1))
            sp.wait_ge(x_in, 16 * (B * NCH + 2))

        @block.tensor
        def _(pe):
            pe.wait_ge(w_low, 1)
            with pe.Fori(0, B) as b:
                for ch in range(NCH):
                    xp = ch % 2
                    pe.wait_ge(x_low, b * NCH + (ch + 1))
                    for ht in range(CT):
                        st = b * 8 + (2 * ch + ht)
                        pe.wait_ge(dve_done, st - 1 + 2)
                        pe.wait_ge(first_hi, 2 * (st - 1) + 4)
                        for n in range(3):
                            for ct in range(CT):
                                for k, (wp, dp) in enumerate(HALVES):
                                    at = ct * C + ht * P
                                    last = nc.tensor.matmul(pq[:, ht, n, :], wh[:, n, wp, at:at + P], xh[:, xp, dp, ct, :],
                                                            start=(ct == 0 and k == 0), stop=(ct == CT - 1 and k == 2))
                        last.then_inc(qk_ready, 1)
                        pe.wait_ge(v_copied, st - 1 + 2)
                        for i in range(2):
                            for ct in range(CT):
                                t = 2 * ht + i
                                for k, (wp, dp) in enumerate(HALVES):
                                    last = nc.tensor.matmul(pv[:, ht, i, :], xh[:, xp, dp, ct, t * P:(t + 1) * P],
                                                            wh[:, 3, wp, ct * C:(ct + 1) * C],
                                                            start=(ct == 0 and k == 0), stop=(ct == CT - 1 and k == 2))
                        last.then_inc(v_ready, 1)

        @block.scalar
        def _(act):
            act.dma_start(ops["ident"][:, :], d["c_ident"]).then_inc(ops_in, 16)
            act.dma_start(ops["mask"][:, :], d["c_mask"]).then_inc(ops_in, 16)
            load_sinusoids(act, d, ops["kexp"], ops_in)
            act.wait_ge(const_in, 16 * NCONST)
            nc.scalar.activation(wh[:, :, 0, :], raw_w, ACT.Copy).then_inc(w_high, 1)

            def high_x(g, par):
                act.wait_ge(x_in, 16 * g + 16)
                nc.scalar.activation(xh[:, par, 0], xT[:, :, :], ACT.Copy).then_inc(x_high, 1)

            high_x(0, 0)
            act.wait_ge(vst_ready, 2)
            act.sem_inc(first_hi, 4)
            act.sem_inc(v_copied, 2)
            with act.Fori(0, B) as b:
                for ch in range(NCH):
                    for ht in range(CT):
                        st = b * 8 + (2 * ch + ht)
                        use = b * 4 + ch
                        act.wait_ge(qk_ready, st + 1)
                        act.wait_ge(stored[ht], OUT * use + OUT)
                        nc.scalar.activation(stg[:, ht, 0, :], pq[:, ht, 0, :], ACT.Identity, bias=bias[:, 0, ht:ht + 1]
                                             ).then_inc(first_hi, 1)
                        nc.scalar.activation(stg[:, ht, 6, :], pq[:, ht, 2, :], ACT.Copy).then_inc(first_hi, 1)
                        act.wait_ge(v_ready, st + 1)
                        act.wait_ge(v_stored[ht], VOUT * use + VOUT)
                        nc.scalar.activation(vst[:, ht, :, :, 0:DK],
                                             pv[:, ht].rearrange("p i (h d) -> p i h d", h=H), ACT.Copy
                                             ).then_inc(v_copied, 1)
                        if ht == 0:
                            high_x(b * NCH + (ch + 1), (ch + 1) % 2)
                        for n in range(2):
                            act.wait_ge(rot_sum, 2 * st + (n + 1))
                            nc.scalar.activation(stg[:, ht, 2 + 2 * n, :], turned[:, ht, n, :], ACT.Copy
                                                 ).then_inc(rot_hi, 1)

        @block.vector
        def _(dve):
            nc.vector.memset(vst[:, :, :, :, :], 0.0).then_inc(vst_ready, 1)
            dve.wait_ge(vst_ready, 1)
            nc.vector.memset(vst[:, :, :, :, DK:DK + 1], 1.0).then_inc(vst_ready, 1)
            dve.sem_inc(dve_done, 2)
            dve.wait_ge(w_high, 1)
            nc.vector.tensor_tensor(wh[:, :, 1, :], raw_w, wh[:, :, 0, :], ALU.subtract).then_inc(w_low, 1)

            def low_x(g, par):
                dve.wait_ge(x_high, g + 1)
                nc.vector.tensor_tensor(xh[:, par, 1], xT[:, :, :], xh[:, par, 0], ALU.subtract).then_inc(x_low, 1)

            low_x(0, 0)
            dve.wait_ge(w_low, 1)
            with dve.Fori(0, B) as b:
                for ch in range(NCH):
                    for ht in range(CT):
                        st = b * 8 + (2 * ch + ht)
                        use = b * 4 + ch
                        cols = slice(ch * CH, (ch + 1) * CH)
                        if ht == 0:
                            dve.wait_ge(rot_in[ch], 16)
                        dve.wait_ge(qk_ready, st + 1)
                        dve.wait_ge(pool_done, st - 1 + 2)
                        for n in (1, 3, 0, 2):
                            if n == 0:
                                dve.wait_ge(first_hi, 2 * st + 1 + 4)
                            nc.vector.scalar_tensor_tensor(
                                out=prod[:, ht, n, :], in0=pq[:, ht, n % 2, :], scalar=bias[:, 1 + n % 2, ht:ht + 1],
                                in1=rot[:, n, cols], op0=ALU.add, op1=ALU.mult).then_inc(rot_prod, 1)
                        dve.wait_ge(first_hi, 2 * st + 2 + 4)
                        dve.wait_ge(stored[ht], OUT * use + OUT)
                        nc.vector.scalar_tensor_tensor(
                            out=stg[:, ht, 1, :], in0=pq[:, ht, 0, :], scalar=bias[:, 0, ht:ht + 1],
                            in1=stg[:, ht, 0, :], op0=ALU.add, op1=ALU.subtract)
                        nc.vector.tensor_tensor(stg[:, ht, 7, :], pq[:, ht, 2, :], stg[:, ht, 6, :], ALU.subtract
                                                ).then_inc(dve_done, 1)
                        if ht == 0:
                            low_x(b * NCH + (ch + 1), (ch + 1) % 2)

        @block.gpsimd
        def _(pool):
            pool.sem_inc(pool_done, 2)
            for s in stored:
                pool.sem_inc(s, OUT)
            for s in v_stored:
                pool.sem_inc(s, VOUT)
            nc.gpsimd.memset(ops["kexp"][ONE_ROW:ONE_ROW + 1], 1.0).then_inc(ops_set, 1)
            for c in range(NCH):
                nc.gpsimd.memset(ops["qop"][0:NSPLIT, c, SUP], 0.0).then_inc(ops_set, 1)
            pool.wait_ge(ops_set, 1 + NCH)
            with pool.Fori(0, B) as b:
                for ch in range(NCH):
                    for ht in range(CT):
                        st = b * 8 + (2 * ch + ht)
                        for n in range(2):
                            pool.wait_ge(rot_prod, 4 * st + (n + 3))
                            nc.gpsimd.tensor_tensor(turned[:, ht, n, :], prod[:, ht, 2 * n, :],
                                                    prod[:, ht, 2 * n + 1, :], ALU.add).then_inc(rot_sum, 1)
                        for n in range(2):
                            pool.wait_ge(rot_hi, 2 * st + (n + 1))
                            last = nc.gpsimd.tensor_tensor(stg[:, ht, 3 + 2 * n, :], turned[:, ht, n, :],
                                                           stg[:, ht, 2 + 2 * n, :], ALU.subtract)
                        last.then_inc(pool_done, 1)
            pool.wait_ge(ops_in, 16 * 5)


def stage_attention(nc, d, g, ops, heads_out):
    with ExitStack() as ctx:
        def sb(name, shape, dt):
            return ctx.enter_context(nc.sbuf_tensor(name, shape, dt))

        def sem(name):
            return ctx.enter_context(nc.semaphore(name))

        NMAX = QUAD * QT * 5
        SLOTS = NMAX + 2
        STEPS = KT + 2
        PARTS = 2
        KEPT = 2 * PARTS + 2 * QT
        DIAG = STEPS - QT
        TILES = 2 * STEPS
        NM = 3
        LEAD, TURN_LAG, OUT_AT = 25, 5, 4
        assert (NMAX + LEAD) % NM == (SLOTS - 1) % NM
        NP = 4

        kmax = sb("kmax", [P, QUAD, S], F16)
        kexp, ident, mask, qop = (ops[k] for k in ("kexp", "ident", "mask", "qop"))
        vals = sb("vals", [P, KT, QUAD, 32], F32)
        prob = sb("prob", [P, NP, 2, CH], F32)
        joint = sb("joint", [P, 2, 2, 2, CH], F32)
        zero = sb("zero", [P, 4 * C], F32)
        masked = sb("masked", [P, 3 * P], F32)
        part = sb("part", [P, QUAD * QT, 5], F32)
        nmax = sb("nmax", [P, QUAD * QT], F32)
        nmaxT = sb("nmaxT", [QUAD * QT, 2, P], F16)
        summed = sb("summed", [P, CH], F32)
        rsum = sb("rsum", [P, QT, QUAD], F32)
        sc_ps = ctx.enter_context(nc.psum_tensor("sc_ps", [P, 2, 2, CH], F32))
        mx_ps = ctx.enter_context(nc.psum_tensor("mx_ps", [P, NM, CH], F32))
        acc = ctx.enter_context(nc.psum_tensor("acc", [P, CH], F32))

        filled = sem("b_filled")
        kmax_set = sem("b_kmax_set")
        zeroed = sem("b_zeroed")
        zeros_out = sem("b_zeros_out")
        q_in = [sem(f"b_q_in{i}") for i in range(NCH)]
        m_in = [sem(f"b_m_in{i}") for i in range(NCH)]
        kmax_in = [sem(f"b_kmax_in{i}") for i in range(QUAD)]
        kexp_in = [sem(f"b_kexp_in{i}") for i in range(4)]
        scores = sem("b_scores")
        exped = sem("b_exped")
        pv_done = sem("b_pv_done")
        parted = sem("b_parted")
        kept = sem("b_kept")
        passed = sem("b_passed")
        passed_v = sem("b_passed_v")
        joined = sem("b_joined")
        evacuated = sem("b_evacuated")
        slot_full = sem("b_slot_full")
        slot_free = sem("b_slot_free")
        max_done = sem("b_max_done")
        own = sem("b_own")

        NQDMA = 3 * 6 - 3
        q_total = [NQDMA + (3 if c == 0 else 0) for c in range(NCH)]

        block = ctx.enter_context(nc.Block())

        def entries(n_next, n_after):
            seq = [(1, k) for k in range(LEAD, NMAX)] if n_next else []
            if n_next:
                ahead = [(2, k) for k in range(LEAD)] if n_after else []
                seq += ahead[:TURN_LAG] + ["maxima"] + ahead[TURN_LAG:]
            seq.insert(OUT_AT if n_next else 0, "output")
            return seq

        BEFORE = [(1, k) for k in range(NMAX)] + [(2, k) for k in range(TURN_LAG)] + ["maxima"] + [
            (2, k) for k in range(TURN_LAG, LEAD)]

        def number(n, pos, last):
            if last == "before":
                return pos
            if last and n == NIT * NCH - 1:
                return len(BEFORE) + SLOTS * (n - 1) + len(entries(True, False)) + pos
            return len(BEFORE) + SLOTS * n + pos

        def key_block(c, step):
            off = [t for t in range(KT) if not c * QT <= t < (c + 1) * QT]
            return None if step < PARTS else (off + list(range(c * QT, (c + 1) * QT)))[step - PARTS]

        def body_entries(c, last):
            return entries(not (last and c == NCH - 1), not (last and c >= NCH - 2))

        def load_kmax(eng, it, h):
            for part3, half in ((0, 0), (1, 1), (2, 0)):
                eng.dma_start(kmax[32 * part3:32 * part3 + DK, h], g["ks"][half, bass.ds(it * 4 * DK + h * DK, DK)]
                              ).then_inc(kmax_in[h], 16)

        def load_kexp(eng, it, s):
            cols = slice(s * CH, (s + 1) * CH)
            for part3, half in ((0, 0), (1, 1), (2, 0)):
                src = g["ks"][half, bass.ds(it * 4 * DK, 4 * DK), cols]
                eng.dma_start(kexp[32 * part3:32 * part3 + DK, :, cols], src.rearrange("(h r) n -> r h n", h=QUAD)
                             ).then_inc(kexp_in[s], 16)
            eng.dma_start(vals[:, 4 * s:4 * s + 4].rearrange("p k h d -> p k (h d)"),
                         g["vs"][bass.ds(it * S + s * CH, CH)].rearrange("(k p) n -> p k n", p=P)
                         ).then_inc(kexp_in[s], 16)

        @block.sync
        def _(sp):
            def load_q(it, c):
                row = it * 4 * DK
                for cls in range(3):
                    for part3, half in ((0, 0), (1, 0), (2, 1)):
                        base = 32 * part3
                        src = g["qs"][half, bass.ds(row, 4 * DK), c * CH:(c + 1) * CH]
                        sp.dma_start(qop[base:base + DK, c, cls], src.rearrange("(h r) n -> r h n", h=QUAD)
                                     ).then_inc(q_in[c], 16)
                        kind = 2 * (1 if cls == LOW else 2) + half
                        if cls != SUP:
                            src = g["qs"][kind, bass.ds(row, 4 * DK), c * CH:(c + 1) * CH]
                            sp.dma_start(qop[base + DK:base + 2 * DK, c, cls], src.rearrange("(h r) n -> r h n", h=QUAD)
                                         ).then_inc(q_in[c], 16)
                        elif c == 0:
                            src = g["qs"][2 + half, bass.ds(row, 4 * DK), 0:1]
                            with nc.allow_non_contiguous_dma(reason="place 0 alone"):
                                sp.dma_start(qop[base + DK:base + 2 * DK, c, cls, :, 0:1],
                                             src.rearrange("(h r) n -> r h n", h=QUAD)).then_inc(q_in[c], 16)

            def send_max(c, turned):
                sp.wait_ge(slot_free, turned + 1 + NM)
                for cls in range(3):
                    sp.dma_start(qop[ONE_ROW:ONE_ROW + 1, c, cls].rearrange("o h (q n) -> o (h q) n", q=QT),
                                 nmaxT[:, c % 2, :]).then_inc(m_in[c], 16)

            for c in range(3):
                load_q(0, c)
            send_max(0, BEFORE.index("maxima"))

            def turn(it, last):
                for c in range(NCH):
                    n = it * NCH + c
                    seq = body_entries(c, last)
                    if c < 1 or not last:
                        sp.wait_ge(evacuated, n + 2)
                        load_q(it + (c + 3) // NCH, (c + 3) % NCH)
                    if c == 2 and not last:
                        for h in (1, 2, 3):
                            sp.wait_ge(slot_full, number(n, seq.index((1, (h + 1) * QT * 5 - 1)), last) + 1)
                            load_kmax(sp, it + 1, h)
                    if c == 3 and not last:
                        for s in range(3):
                            sp.wait_ge(pv_done, n * KT + 4 * s + 4 + 2)
                            load_kexp(sp, it + 1, s)
                    if "maxima" in seq:
                        send_max((c + 1) % NCH, number(n, seq.index("maxima"), last))
                    if c == 1 and not last:
                        sp.wait_ge(slot_full, number(n, seq.index((2, QT * 5 - 1)), last) + 1)
                        load_kmax(sp, it + 1, 0)
                    if c == 3 and not last:
                        sp.wait_ge(pv_done, n * KT + KT + 2)
                        load_kexp(sp, it + 1, 3)

            with sp.Fori(0, NIT - 1) as it:
                turn(it, False)
            turn(NIT - 1, True)

        @block.tensor
        def _(pe):
            def max_tile(c, i, k, bank):
                h, qt = divmod(i, QT)
                T = c * QT + qt
                q = lambda cls: qop[0:NSPLIT, c, cls, h, qt * P:(qt + 1) * P]
                if k < 4:
                    others = [t for t in range(KT) if t != T][4 * k:4 * k + 4]
                    col = 0
                    while others:
                        cls = LOW if others[0] < T else HIGH
                        run = [others.pop(0)]
                        while others and others[0] == run[-1] + 1 and (LOW if others[0] < T else HIGH) == cls:
                            run.append(others.pop(0))
                        width = len(run) * P
                        last = nc.tensor.matmul(bank[:, col:col + width], q(cls), kmax[0:NSPLIT, h, run[0] * P:run[0] * P + width],
                                                start=True, stop=True, skip_group_check=True)
                        col += width
                else:
                    for n, cls in enumerate((LOW, HIGH, SUP)):
                        last = nc.tensor.matmul(bank[:, n * P:(n + 1) * P], q(cls), kmax[0:NSPLIT, h, T * P:(T + 1) * P],
                                                start=(n == 0), stop=(n == 2), skip_group_check=True)
                last.then_inc(slot_full, 1)

            def score_tile(c, step, pair, buf):
                t = key_block(c, step)
                for j in range(2):
                    h = 2 * pair + j
                    out = sc_ps[:, buf, j, :]
                    q = lambda cls, a, b: qop[0:BIG_ROWS, c, cls, h, a:b]
                    k = lambda kt: kexp[0:BIG_ROWS, h, kt * P:(kt + 1) * P]
                    if step >= PARTS:
                        split = min(max(t - c * QT, 0), QT) * P
                        if t >= (c + 1) * QT:
                            split = CH
                        if split:
                            last = nc.tensor.matmul(out[:, 0:split], k(t), q(HIGH, 0, split), start=True,
                                                    stop=True, skip_group_check=True)
                        if split < CH:
                            last = nc.tensor.matmul(out[:, split:CH], k(t), q(LOW, split, CH), start=True,
                                                    stop=True, skip_group_check=True)
                    else:
                        cls = HIGH if step == 0 else SUP
                        for n in range(QT):
                            last = nc.tensor.matmul(out[:, n * P:(n + 1) * P], k(c * QT + n), q(cls, n * P, (n + 1) * P),
                                                    start=(n == 0), stop=(n == QT - 1), skip_group_check=True)
                last.then_inc(scores, 1)

            def values(c, step):
                for h in range(QUAD):
                    last = nc.tensor.matmul(acc[32 * h:32 * h + 32, :], vals[:, key_block(c, step), h, :],
                                            prob[:, (2 * step + h // 2) % NP, h % 2, :],
                                            start=(step == PARTS), stop=(step == STEPS - 1), skip_group_check=True)
                last.then_inc(pv_done, 1)

            def take_bank(n, pos, last):
                strict = pos == 0 and last != "before"
                pe.wait_ge(slot_free, number(n, pos, last) + (NM if strict else 1))
                return mx_ps[:, pos % NM, :]

            def needs_q(it, c):
                pe.wait_ge(q_in[c], (it + 1) * 16 * q_total[c])

            def emit(it, c, n, pos, entry, last):
                if entry == "maxima":
                    pe.wait_ge(max_done, n + 2)
                    bank = take_bank(n, pos, last)
                    nc.tensor.transpose(bank[0:QUAD * QT, 0:P], nmax[:, :], ident[:, :]).then_inc(slot_full, 1)
                elif entry == "output":
                    pe.wait_ge(evacuated, n + 2)
                    pe.wait_ge(filled, 1)
                    bank = take_bank(n, pos, last)
                    for qt in range(QT):
                        mm = nc.tensor.transpose(bank[:, qt * P:(qt + 1) * P], summed[:, qt * P:(qt + 1) * P], ident[:, :])
                    mm.then_inc(slot_full, 1)
                else:
                    off, k = entry
                    nit, nc_ = it + (c + off) // NCH, (c + off) % NCH
                    if k == 0:
                        needs_q(nit, nc_)
                    if nc_ == 0 and k % (QT * 5) == 0:
                        pe.wait_ge(kmax_in[k // (QT * 5)], (nit + 1) * 16 * 3)
                    max_tile(nc_, k // 5, k % 5, take_bank(n, pos, last))

            def first_scores(it, c, n):
                pe.wait_ge(m_in[c], (it + 1) * 16 * 3)
                if c == 0:
                    pe.wait_ge(kexp_in[0], (it + 1) * 16 * 4)
                for pair in range(2):
                    pe.wait_ge(exped, n * TILES + pair + 1)
                    score_tile(c, 0, pair, pair)

            pe.wait_ge(kmax_set, 16 * 3)
            for pos, entry in enumerate(BEFORE):
                emit(-1, NCH - 1, -1, pos, entry, "before")
            first_scores(0, 0, 0)

            WEIGHTS = []
            for t in range(1, STEPS + 1):
                WEIGHTS += 2 * [8 if t < STEPS else 4] + [10 if t <= PARTS else 16 if t < STEPS else 0]

            def turn(it, last):
                for c in range(NCH):
                    n = it * NCH + c
                    nit, nc_ = (it, c + 1) if c < NCH - 1 else (it + 1, 0)
                    more = not (last and c == NCH - 1)
                    seq = body_entries(c, last)
                    done = [0]

                    def pace(t, part):
                        due = min(len(seq), SLOTS * sum(WEIGHTS[:3 * (t - 1) + part]) // sum(WEIGHTS))
                        if not more:
                            due = len(seq) if t >= 2 else 0
                        while done[0] < due:
                            if seq[done[0]] == "output" and (t, part) < (1, 3):
                                return
                            emit(it, c, n, done[0], seq[done[0]], last)
                            done[0] += 1

                    for t in range(1, STEPS + 1):
                        if t < STEPS:
                            kt = key_block(c, t)
                            if c == 0 and t >= PARTS and kt % 4 == 0 and kt:
                                pe.wait_ge(kexp_in[kt // 4], (it + 1) * 16 * 4)
                            for pair in range(2):
                                pe.wait_ge(exped, n * TILES + (2 * t + pair) - 2 + 1 + 2)
                                score_tile(c, t, pair, pair)
                                pace(t, pair + 1)
                        elif more:
                            first_scores(nit, nc_, n + 1)
                            pace(t, 2)
                        if t == PARTS + 1:
                            pe.wait_ge(evacuated, n + 2)
                        if t > DIAG:
                            pe.wait_ge(joined, (n * QT + (t - DIAG)) * 2 + 2)
                        else:
                            pe.wait_ge(exped, n * TILES + 2 * t + 2)
                        if t > PARTS:
                            values(c, t - 1)
                        pace(t, 3)

            with pe.Fori(0, NIT - 1) as it:
                turn(it, False)
            turn(NIT - 1, True)
            pe.wait_ge(evacuated, NIT * NCH + 2)
            pe.wait_ge(slot_free, number(NIT * NCH - 1, 1, True) + NM)
            for qt in range(QT):
                mm = nc.tensor.transpose(mx_ps[:, 0, qt * P:(qt + 1) * P], summed[:, qt * P:(qt + 1) * P], ident[:, :])
            mm.then_inc(slot_full, 1)

        @block.scalar
        def _(act):
            act.sem_inc(exped, 2)
            load_kmax(act, 0, 0)
            load_sinusoids(act, d, kmax, kmax_set)
            act.wait_ge(q_in[0], 16 * q_total[0])
            for h in range(1, QUAD):
                load_kmax(act, 0, h)
            for s in range(4):
                load_kexp(act, 0, s)

            def exp_step(c, n, t):
                for pair in range(2):
                    act.wait_ge(scores, n * TILES + 2 * t + pair + 1)
                    if t < PARTS:
                        into = joint[:, (c + t) % 2, pair]
                        if pair == 0 and t == 0:
                            act.wait_ge(parted, n * 2 + 2)
                        elif pair == 0:
                            act.wait_ge(joined, n * QT * 2 + 2)
                    else:
                        into = prob[:, (2 * t + pair) % NP]
                        if pair == 0:
                            act.wait_ge(pv_done, n * KT + t - 1)
                    nc.scalar.activation(into, sc_ps[:, pair, :, :], ACT.Exp, scale=SCALE).then_inc(exped, 1)

            for t in range(PARTS):
                exp_step(0, 0, t)

            def turn(it, last):
                for c in range(NCH):
                    n = it * NCH + c
                    for t in range(PARTS, STEPS):
                        exp_step(c, n, t)
                    if not (last and c == NCH - 1):
                        for t in range(PARTS):
                            exp_step((c + 1) % NCH, n + 1, t)

            with act.Fori(0, NIT - 1) as it:
                turn(it, False)
            turn(NIT - 1, True)

        @block.vector
        def _(dve):
            dve.sem_inc(slot_free, NM)
            dve.sem_inc(evacuated, 2)
            nc.vector.memset(summed[:, :], 1.0).then_inc(filled, 1)

            def divide_output(it, c, bank_no, num):
                links = it * NCH + c + 1
                turn_, c_ = (it + 1, c - 1) if c else (it, NCH - 1)
                dve.wait_ge(slot_full, num + 1)
                bank = mx_ps[:, bank_no, :].rearrange("p (a h d) -> p a h d", a=QT, d=32)
                nc.vector.reciprocal(rsum[:, :, :], bank[:, :, :, DK]).then_inc(own, 1)
                dve.wait_ge(own, links)
                nc.vector.tensor_tensor(
                    heads_out[:, c_, :, bass.ds(turn_, 1), :].rearrange("p a o (h d) -> p a (o h) d", d=DK),
                    bank[:, :, :, 0:DK], rsum[:, :, :].unsqueeze(3).to_broadcast([P, QT, QUAD, DK]), ALU.mult
                    ).then_inc(slot_free, 1)

            def drain(it, c, n, seq, last):
                for pos, entry in enumerate(seq):
                    num = number(n, pos, last)
                    if entry == "output":
                        divide_output(it, c, pos % NM, num)
                        continue
                    dve.wait_ge(slot_full, num + 1)
                    if entry == "maxima":
                        nc.vector.tensor_copy(nmaxT[:, (c + 1) % 2, :], mx_ps[0:QUAD * QT, pos % NM, 0:P]
                                              ).then_inc(slot_free, 1)
                        continue
                    off, k = entry
                    if entry == (2, 0):
                        dve.wait_ge(max_done, n + 2)
                    into = part[:, k // 5, k % 5:k % 5 + 1]
                    if k % 5 < 4:
                        width = CH if k % 5 < 3 else 3 * P
                        nc.vector.reduce_max(into, mx_ps[:, pos % NM, 0:width], AX).then_inc(slot_free, 1)
                    else:
                        dve.sem_inc(passed_v, 1)
                        nc.vector.tensor_tensor_reduce(
                            out=masked[:, :], in0=mx_ps[:, pos % NM, 0:3 * P], in1=mask[:, :], scale=1.0, scalar=2 * NEG,
                            op0=ALU.add, op1=ALU.max, accum_out=into).then_inc(slot_free, 1)
                    if entry == (1, NMAX - 1):
                        dve.wait_ge(slot_free, num + 1 + NM)
                        nc.vector.tensor_reduce(nmax[:, :], part[:, :, :], AX, ALU.max, negate=True).then_inc(max_done, 1)

            drain(-1, NCH - 1, -1, BEFORE, "before")

            def turn(it, last):
                for c in range(NCH):
                    n = it * NCH + c
                    drain(it, c, n, body_entries(c, last), last)
                    dve.wait_ge(pv_done, (n + 1) * KT + 2)
                    nc.vector.tensor_copy(summed[:, :], acc[:, :]).then_inc(evacuated, 1)

            with dve.Fori(0, NIT - 1) as it:
                turn(it, False)
            turn(NIT - 1, True)
            divide_output(NIT, 0, 0, number(NIT * NCH - 1, 1, True))

        @block.gpsimd
        def _(pool):
            pool.sem_inc(pv_done, 2)
            pool.sem_inc(parted, 2)
            pool.sem_inc(joined, 2)
            nc.gpsimd.memset(zero[:, :], 0.0).then_inc(zeroed, 1)
            pool.wait_ge(zeroed, 1)
            pool.wait_ge(kexp_in[3], 16 * 4)
            zeros = 0
            for t, r0 in ((g["xs"], 0), (g["ys"], NTOK * 2)):
                for r in range(r0, t.shape[0], P * 4):
                    pool.dma_start(t[r:r + P * 4].rearrange("(p a) n -> p (a n)", p=P), zero[:, :]).then_inc(zeros_out, 16)
                    zeros += 1
            def keep(tile, sign, op):
                blocks = [[0, k] for k in tile.shape[1:-1]]
                return nc.gpsimd.affine_select(out=tile, in_=tile, pattern=blocks + [[-sign, P]], compare_op=op, fill=0.0,
                                               base=0, channel_multiplier=sign)

            def join(c, n):
                high, sup = joint[:, c % 2], joint[:, 1 - c % 2]
                square = lambda t: t.rearrange("p j (q n) -> p j q n", n=P)
                for pair in range(2):
                    pool.wait_ge(exped, n * TILES + pair + 1 + 2)
                    pool.sem_inc(passed, 1)
                    keep(square(high[:, pair]), 1, ALU.is_gt).then_inc(kept, 1)
                for pair in range(2):
                    pool.wait_ge(exped, n * TILES + 2 + pair + 1 + 2)
                    pool.sem_inc(passed, 1)
                    keep(square(sup[:, pair]), 1, ALU.is_equal).then_inc(kept, 1)
                for pair in range(2):
                    pool.wait_ge(kept, n * KEPT + 3 + pair)
                    nc.gpsimd.tensor_tensor(high[:, pair], high[:, pair], sup[:, pair], ALU.add).then_inc(parted, 1)
                pool.wait_ge(parted, n * 2 + 2 + 2)
                for k in range(QT):
                    cols = slice(k * P, (k + 1) * P)
                    for pair in range(2):
                        into = prob[:, (2 * (DIAG + k) + pair) % NP, :, cols]
                        pool.wait_ge(exped, n * TILES + 2 * (DIAG + k) + pair + 1 + 2)
                        pool.sem_inc(passed, 1)
                        keep(into, -1, ALU.is_gt).then_inc(kept, 1)
                        pool.wait_ge(kept, n * KEPT + 4 + 2 * k + pair + 1)
                        nc.gpsimd.tensor_tensor(into, into, high[:, pair, :, cols], ALU.add).then_inc(joined, 1)

            with pool.Fori(0, NIT) as it:
                for c in range(NCH):
                    join(c, it * NCH + c)
            pool.wait_ge(zeros_out, 16 * zeros)


def place_rows(c):
    if c:
        return [((0, P), (0, QT), c * CH - 1)]
    return [((0, 1), (0, 1), S - 1), ((1, P), (0, 1), 0), ((0, P), (1, QT), P - 1)]


def rows_of(t, run, start):
    (a, z), (q0, q1), _ = run
    n = (z - a) * (q1 - q0)
    return t[bass.ds(start, n)].rearrange("(q p) n -> p q n", q=q1 - q0)


def stage_norm(nc, d, g, heads_out, x1, logits):
    with ExitStack() as ctx:
        def sb(name, shape, dt):
            return ctx.enter_context(nc.sbuf_tensor(name, shape, dt))

        def sem(name):
            return ctx.enter_context(nc.semaphore(name))

        GROUPS = B * NCH
        LAG = 2
        wo = sb("wo", [P, CT, C], F32)
        rw = sb("rw", [P, CT, E], F32)
        bo = sb("bo", [P, C], F32)
        ident = sb("identc", [P, P], F32)
        xres = sb("xres", [P, 2, QT, C], F32)
        xbias = sb("xbias", [P, 2, QT, C], F32)
        headsT = sb("headsT", [P, 2, QT, CT, P], F32)
        res = sb("res", [P, 2, QT, C], F32)
        stats = sb("stats", [P, 2, QT, 6], F32)
        agg = sb("agg", [P, 2, QT, 2], F32)
        dev = sb("dev", [P, 2, QT], F32)
        rstd = sb("rstd", [P, 2, QT], F32)
        xnormT = sb("xnormT", [P, 2, QT, CT, P], F32)
        t_ps = ctx.enter_context(nc.psum_tensor("t_ps", [P, QT, CT, P], F32))
        y_ps = ctx.enter_context(nc.psum_tensor("y_ps", [P, QT, C], F32))
        n_ps = ctx.enter_context(nc.psum_tensor("n_ps", [P, QT, CT, P], F32))
        l_ps = ctx.enter_context(nc.psum_tensor("l_ps", [P, CH], F32))

        const_in = sem("c_const_in")
        x_in = [sem(f"c_x_in{i}") for i in range(2)]
        biased = sem("c_biased")
        headsT_ps = sem("c_headsT_ps")
        headsT_sb = sem("c_headsT_sb")
        projected = sem("c_projected")
        residual = sem("c_residual")
        own = sem("c_own")
        spread = sem("c_spread")
        rooted = sem("c_rooted")
        normed = sem("c_normed")
        xT_ps = sem("c_xT_ps")
        xT_sb = sem("c_xT_sb")
        routed = sem("c_routed")
        logged = sem("c_logged")

        block = ctx.enter_context(nc.Block())

        @block.sync
        def _(sp):
            sp.dma_start(ident[:, :], d["c_ident"]).then_inc(const_in, 16)
            sp.dma_start(wo[:, :, :], d["Wo"].rearrange("(t p) n -> p t n", p=P)).then_inc(const_in, 16)
            sp.dma_start(bo[:, :], d["bo"].to_broadcast([P, C])).then_inc(const_in, 16)
            sp.dma_start(rw[:, :, :], d["rw"].rearrange("(t p) n -> p t n", p=P)).then_inc(const_in, 16)
            for m in range(GROUPS):
                b, c = divmod(m, NCH)
                if m >= 2:
                    sp.wait_ge(biased, m - 1)
                for run in place_rows(c):
                    (a, z), (q0, q1), row = run
                    sp.dma_start(xres[a:z, m % 2, q0:q1], rows_of(d["x"], run, b * S + row)).then_inc(x_in[m % 2], 16)

        @block.gpsimd
        def _(pool):
            pool.wait_ge(const_in, 64)
            for m in range(GROUPS):
                loads = sum(len(place_rows(k % NCH)) for k in range(m + 1) if k % 2 == m % 2)
                pool.wait_ge(x_in[m % 2], 16 * loads)
                if m >= 2:
                    pool.wait_ge(residual, m - 1)
                nc.gpsimd.tensor_tensor(xbias[:, m % 2], xres[:, m % 2],
                                        bo[:, :].unsqueeze(1).to_broadcast([P, QT, C]), ALU.add).then_inc(biased, 1)

        @block.tensor
        def _(pe):
            pe.wait_ge(const_in, 64)
            for m in range(GROUPS + LAG):
                r = m - LAG
                if m < GROUPS:
                    b, c = divmod(m, NCH)
                    if m >= 1:
                        pe.wait_ge(headsT_sb, m)
                    for qt in range(QT):
                        for ct in range(CT):
                            at = (1 + b * NQ + 2 * ct)
                            two = heads_out[:, c, qt, at:at + 2, :].rearrange("p a n -> p (a n)")
                            last = nc.tensor.transpose(t_ps[:, qt, ct, :], two, ident[:, :])
                    last.then_inc(headsT_ps, 1)
                if r >= 0:
                    pe.wait_ge(normed, r + 1)
                    if r >= 1:
                        pe.wait_ge(xT_sb, r)
                    for qt in range(QT):
                        for ct in range(CT):
                            last = nc.tensor.transpose(n_ps[:, qt, ct, :], x1[:, r * QT + qt, ct * P:(ct + 1) * P], ident[:, :])
                    last.then_inc(xT_ps, 1)
                if m < GROUPS:
                    pe.wait_ge(headsT_sb, m + 1)
                    if m >= 1:
                        pe.wait_ge(residual, m)
                    for qt in range(QT):
                        for ct in range(CT):
                            last = nc.tensor.matmul(y_ps[:, qt, :], headsT[:, m % 2, qt, ct, :], wo[:, ct, :],
                                                    start=(ct == 0), stop=(ct == CT - 1))
                    last.then_inc(projected, 1)
                if r >= 0:
                    pe.wait_ge(xT_sb, r + 1)
                    for qt in range(QT):
                        for ct in range(CT):
                            at = (r * QT + qt) * E
                            last = nc.tensor.matmul(l_ps[:, at:at + E], xnormT[:, r % 2, qt, ct, :], rw[:, ct, :],
                                                    start=(ct == 0), stop=(ct == CT - 1))
                    last.then_inc(routed, 1)

        @block.scalar
        def _(act):
            for m in range(GROUPS + LAG):
                if m < GROUPS:
                    act.wait_ge(headsT_ps, m + 1)
                    if m >= 2:
                        act.wait_ge(projected, m - 1)
                    nc.scalar.activation(headsT[:, m % 2], t_ps[:, :, :, :], ACT.Copy).then_inc(headsT_sb, 1)
                if 1 <= m <= GROUPS:
                    act.wait_ge(spread, m)
                    nc.scalar.activation(dev[:, (m - 1) % 2, :], agg[:, (m - 1) % 2, :, 1], ACT.Sqrt).then_inc(rooted, 1)
                r = m - LAG
                if r >= 0:
                    act.wait_ge(xT_ps, r + 1)
                    if r >= 2:
                        act.wait_ge(routed, r - 1)
                    nc.scalar.activation(xnormT[:, r % 2], n_ps[:, :, :, :], ACT.Copy).then_inc(xT_sb, 1)

        @block.vector
        def _(dve):
            for m in range(GROUPS):
                par = m % 2
                dve.wait_ge(projected, m + 1)
                dve.wait_ge(biased, m + 1)
                nc.vector.tensor_tensor(res[:, par], y_ps[:, :, :], xbias[:, par], ALU.add).then_inc(residual, 1)
                dve.wait_ge(residual, m + 1)
                for qt in range(QT):
                    last = nc.vector.bn_stats(stats[:, par, qt, :], res[:, par, qt, :])
                last.then_inc(own, 1)
                dve.wait_ge(own, 3 * m + 1)
                for qt in range(QT):
                    last = nc.vector.bn_aggr(agg[:, par, qt, :], stats[:, par, qt, :])
                last.then_inc(own, 1)
                dve.wait_ge(own, 3 * m + 2)
                nc.vector.tensor_scalar(agg[:, par, :, 1], agg[:, par, :, 1], EPS, None, ALU.add).then_inc(spread, 1)
                dve.wait_ge(rooted, m + 1)
                nc.vector.reciprocal(rstd[:, par, :], dev[:, par, :]).then_inc(own, 1)
                dve.wait_ge(own, 3 * m + 3)
                for qt in range(QT):
                    last = nc.vector.tensor_scalar(x1[:, m * QT + qt, :], res[:, par, qt, :], agg[:, par, qt, 0:1],
                                                   rstd[:, par, qt:qt + 1], ALU.subtract, ALU.mult)
                last.then_inc(normed, 1)
            dve.wait_ge(routed, GROUPS)
            nc.vector.tensor_copy(logits[:, :, :].rearrange("p t e -> p (t e)"), l_ps[:, 0:NT * E]).then_inc(logged, 1)
            dve.wait_ge(logged, 1)


def load_weights(eng, d, w, e, par):
    for n, name in enumerate(("wg", "w1")):
        eng.dma_start(w["raw"][:, par, n].rearrange("p (t f) -> p t f", t=CT),
                      d[name][bass.ds(e, 1)].rearrange("a (t p) f -> p (a t) f", p=P)).then_inc(w["in"][par], 16)
    eng.dma_start(w["raw"][:, par, 2].rearrange("p (t n) -> p t n", t=FT),
                  d["w2"][bass.ds(e, 1)].rearrange("a (t p) n -> p (a t) n", p=P)).then_inc(w["in"][par], 16)


def stage_route(nc, d, g, w, x1, logits, gates, slots, bounds):
    with ExitStack() as ctx:
        def sb(name, shape, dt):
            return ctx.enter_context(nc.sbuf_tensor(name, shape, dt))

        def sem(name):
            return ctx.enter_context(nc.semaphore(name))

        full = [P, NT, E]
        order = sb("order", full, F32)
        before = sb("before", [P, P], F32)
        ones = sb("ones", [P, P], F32)
        probs = sb("probs", full, F32)
        expd = sb("expd", full, F32)
        work = sb("work", full, F32)
        chosen = sb("chosen", [P, 2, NT, E], F32)
        both = sb("both", full, F32)
        rank = sb("rank", full, F32)
        total = sb("total", full, F32)
        run = sb("run", [P, 2, NT, E], F32)
        row = sb("row", [P, NT], F32)
        slotf = sb("slotf", [P, NT], F32)
        need = sb("need", [P, E], F32)
        needi = sb("needi", [P, E], I32)
        upto = sb("upto", [P, 2, E], F32)
        r_ps = ctx.enter_context(nc.psum_tensor("r_ps", [P, 2, NT * E], F32))

        const_in = sem("d_const_in")
        own = sem("d_own")
        shifted = sem("d_shifted")
        exped = sem("d_exped")
        hot = sem("d_hot")
        counted = sem("d_counted")
        placed = sem("d_placed")
        sent = sem("d_sent")
        block = ctx.enter_context(nc.Block())

        @block.sync
        def _(sp):
            sp.dma_start(order[:, :, :].rearrange("p t e -> p (t e)"), d["c_order"]).then_inc(const_in, 16)
            sp.dma_start(before[:, :], d["c_before"]).then_inc(const_in, 16)

        @block.scalar
        def _(act):
            load_weights(act, d, w, 0, 0)
            load_weights(act, d, w, 1, 1)
            act.wait_ge(shifted, 1)
            nc.scalar.activation(expd[:, :, :], work[:, :, :], ACT.Exp).then_inc(exped, 1)
            act.wait_ge(w["in"][0], 48)
            for n in range(3):
                last = nc.scalar.activation(w["half"][:, 0, n, 0, :], w["raw"][:, 0, n, :], ACT.Copy)
            last.then_inc(w["high"], 1)

        @block.tensor
        def _(pe):
            pe.wait_ge(hot, 1)
            rhs = both[:, :, :].rearrange("p t e -> p (t e)")
            nc.tensor.matmul(r_ps[:, 0, :], before[:, :], rhs, start=True, stop=True)
            nc.tensor.matmul(r_ps[:, 1, :], ones[:, :], rhs, start=True, stop=True).then_inc(counted, 1)

        @block.vector
        def _(dve):
            links = [0]

            def aside(ins):
                links[0] += 1
                ins.then_inc(own, 1)

            def link(ins):
                aside(ins)
                dve.wait_ge(own, links[0])

            def wide(ap):
                return ap.unsqueeze(2).to_broadcast(full)

            V = nc.vector
            aside(V.memset(ones[:, :], 1.0))
            link(V.reduce_max(row[:, :], logits[:, :, :], AX))
            V.tensor_tensor(work[:, :, :], logits[:, :, :], wide(row[:, :]), ALU.subtract).then_inc(shifted, 1)
            dve.wait_ge(exped, 1)
            link(V.reduce_sum(row[:, :], expd[:, :, :], AX))
            link(V.reciprocal(row[:, :], row[:, :]))
            link(V.tensor_tensor(probs[:, :, :], expd[:, :, :], wide(row[:, :]), ALU.mult))
            dve.wait_ge(const_in, 32)
            for k in range(2):
                link(V.reduce_max(gates[:, k, :], probs[:, :, :], AX))
                link(V.tensor_tensor(work[:, :, :], probs[:, :, :], wide(gates[:, k, :]), ALU.is_equal))
                link(V.tensor_tensor(work[:, :, :], work[:, :, :], order[:, :, :], ALU.mult))
                link(V.reduce_max(row[:, :], work[:, :, :], AX))
                link(V.tensor_tensor(chosen[:, k], work[:, :, :], wide(row[:, :]), ALU.is_equal))
                if k == 0:
                    link(V.scalar_tensor_tensor(out=probs[:, :, :], in0=chosen[:, 0], scalar=-2.0, in1=probs[:, :, :],
                                                op0=ALU.mult, op1=ALU.add))
            V.tensor_tensor(both[:, :, :], chosen[:, 0], chosen[:, 1], ALU.add).then_inc(hot, 1)
            dve.wait_ge(counted, 1)
            aside(V.tensor_copy(rank[:, :, :].rearrange("p t e -> p (t e)"), r_ps[:, 0, :]))
            aside(V.tensor_copy(total[:, :, :].rearrange("p t e -> p (t e)"), r_ps[:, 1, :]))
            link(V.tensor_copy(run[:, 0].rearrange("p t e -> p (t e)"), r_ps[:, 1, :]))
            a, step = 0, 1
            while step < NT:
                aside(V.tensor_copy(run[:, 1 - a, 0:step], run[:, a, 0:step]))
                link(V.tensor_tensor(run[:, 1 - a, step:], run[:, a, step:], run[:, a, 0:NT - step], ALU.add))
                a, step = 1 - a, 2 * step
            aside(V.tensor_tensor(rank[:, :, :], rank[:, :, :], total[:, :, :], ALU.subtract))
            link(V.tensor_scalar(need[:, :], run[:, a, NT - 1], float(BLK - 1), None, ALU.add))
            aside(V.tensor_tensor(rank[:, :, :], rank[:, :, :], run[:, a], ALU.add))
            link(V.tensor_copy(needi[:, :], need[:, :]))
            link(V.tensor_single_scalar(needi[:, :], needi[:, :], BLK.bit_length() - 1, ALU.arith_shift_right))
            link(V.tensor_copy(need[:, :], needi[:, :]))
            link(V.tensor_scalar(need[:, :], need[:, :], 1.0, None, ALU.max))
            link(V.tensor_copy(upto[:, 0], need[:, :]))
            u, step = 0, 1
            while step < E:
                aside(V.tensor_copy(upto[:, 1 - u, 0:step], upto[:, u, 0:step]))
                link(V.tensor_tensor(upto[:, 1 - u, step:], upto[:, u, step:], upto[:, u, 0:E - step], ALU.add))
                u, step = 1 - u, 2 * step
            link(V.tensor_tensor(need[:, :], upto[:, u], need[:, :], ALU.subtract))
            aside(V.tensor_copy(bounds[:, 0:E], need[:, :]))
            aside(V.tensor_copy(bounds[:, E:2 * E], upto[:, u]))
            link(V.scalar_tensor_tensor(out=rank[:, :, :], in0=need[:, :].unsqueeze(1).to_broadcast(full),
                                        scalar=float(BLK), in1=rank[:, :, :], op0=ALU.mult, op1=ALU.add))
            for k in range(2):
                link(V.tensor_tensor(work[:, :, :], rank[:, :, :], chosen[:, k], ALU.mult))
                link(V.reduce_sum(slotf[:, :], work[:, :, :], AX))
                V.tensor_copy(slots[:, k, :], slotf[:, :]).then_inc(placed, 1)
                dve.wait_ge(placed, k + 1)
            dve.wait_ge(w["high"], 1)
            for n in range(3):
                last = V.tensor_tensor(w["half"][:, 0, n, 1, :], w["raw"][:, 0, n, :], w["half"][:, 0, n, 0, :], ALU.subtract)
            last.then_inc(w["low"], 1)

        @block.gpsimd
        def _(pool):
            for k in range(2):
                pool.wait_ge(placed, k + 1)
                for t in range(NT):
                    pool.indirect_dma_start(out=g["xs"], out_offset=bass.IndirectOffsetOnAxis(ap=slots[:, k, t:t + 1], axis=0),
                                            in_=x1[:, t, :], in_offset=None).then_inc(sent, 16)
            pool.wait_ge(sent, 16 * 2 * NT)


def stage_experts(nc, d, g, w, bounds):
    with ExitStack() as ctx:
        def sb(name, shape, dt):
            return ctx.enter_context(nc.sbuf_tensor(name, shape, dt))

        def sem(name):
            return ctx.enter_context(nc.semaphore(name))

        raw, wh, w_in, w_high, w_low = w["raw"], w["half"], w["in"], w["high"], w["low"]
        ball = sb("ball", [P, 2, E, FT], F32)
        bcur = sb("bcur", [P, 2, 2, FT], F32)
        b2 = sb("b2", [P, E, C], F32)
        ident = sb("idente", [P, P], F32)
        xin = sb("xin", [P, 2, C], F32)
        xh = sb("xh", [P, 2, CT, BLK], F16)
        act_out = sb("act_out", [P, 4, BLK], F32)
        hid = sb("hid", [P, 4, BLK], F32)
        hh = sb("hh", [P, FT, 2, BLK], F16)
        yout = sb("yout", [P, 2, C], F32)
        gu = ctx.enter_context(nc.psum_tensor("gu", [P, 4, 2, BLK], F32))
        y_ps = ctx.enter_context(nc.psum_tensor("ye_ps", [P, 2, C], F32))
        x_ps = ctx.enter_context(nc.psum_tensor("xe_ps", [P, CT, BLK], F32))

        const_in = sem("e_const_in")
        x_in = sem("e_x_in")
        x_turned = sem("e_x_turned")
        x_high = sem("e_x_high")
        x_low = sem("e_x_low")
        gu_ready = sem("e_gu_ready")
        gated = sem("e_gated")
        hidden = sem("e_hidden")
        h_high = sem("e_h_high")
        h_low = sem("e_h_low")
        down = sem("e_down")
        y_ready = sem("e_y_ready")
        y_out = sem("e_y_out")
        biases = sem("e_biases")
        passed = sem("e_passed")
        passed_w = sem("e_passed_w")

        block = ctx.enter_context(nc.Block())

        def span(eng, e):
            lo = eng.value_load(bounds[0:1, bass.ds(e, 1)], min_val=0, max_val=NBLK - 1)
            hi = eng.value_load(bounds[0:1, bass.ds(e + E, 1)], min_val=1, max_val=NBLK)
            return lo, hi

        @block.sync
        def _(sp):
            def load_x(blk):
                sp.dma_start(xin[:, :, :], g["xs"][bass.ds(blk * BLK, BLK)].rearrange("(i p) n -> p i n", p=P)
                             ).then_inc(x_in, 16)

            sp.dma_start(ident[:, :], d["c_ident"]).then_inc(const_in, 16)
            load_x(0)
            sp.dma_start(ball[:, 0], d["bg"]).then_inc(const_in, 16)
            sp.dma_start(ball[:, 1], d["b1"]).then_inc(const_in, 16)
            sp.dma_start(b2[:, :, :].rearrange("p e n -> p (e n)"), d["b2"].to_broadcast([P, E * C])).then_inc(const_in, 16)
            sp.wait_ge(x_turned, 1)
            load_x(1)
            with sp.Fori(0, E // 2) as pair:
                for par in range(2):
                    lo, hi = span(sp, pair * 2 + par)
                    with sp.Fori(lo, hi) as blk:
                        sp.wait_ge(x_turned, blk + 2)
                        load_x(blk + 2)
                        sp.wait_ge(y_ready, blk + 1 + 1)
                        sp.dma_start(g["ys"][bass.ds(blk * BLK, BLK)].rearrange("(i p) n -> p i n", p=P), yout[:, :, :]
                                     ).then_inc(y_out, 16)
            _, total = span(sp, E - 1)
            sp.wait_ge(y_out, total * 16 + 16)
            sp.sem_inc(passed, 1)
            sp.wait_ge(x_in, total * 16 + 32)
            sp.sem_inc(passed, 1)

        @block.tensor
        def _(pe):
            def turn_x(blk):
                pe.wait_ge(x_in, blk * 16 + 16)
                pe.wait_ge(x_low, blk + 1)
                for i in range(2):
                    for ct in range(CT):
                        last = nc.tensor.transpose(x_ps[:, ct, i * P:(i + 1) * P], xin[:, i, ct * P:(ct + 1) * P], ident[:, :])
                last.then_inc(x_turned, 1)

            def gate_up(blk, f, par):
                if f == 0:
                    pe.wait_ge(x_low, blk + 2)
                pe.wait_ge(hidden, blk * FT + f + 1)
                for n in range(2):
                    for ct in range(CT):
                        for k, (wp, xp) in enumerate(HALVES):
                            at = ct * F + f * P
                            last = nc.tensor.matmul(gu[:, f % 4, n, :], wh[:, par, n, wp, at:at + P], xh[:, xp, ct, :],
                                                    start=(ct == 0 and k == 0), stop=(ct == CT - 1 and k == 2),
                                                    skip_group_check=True)
                last.then_inc(gu_ready, 1)

            def down_product(blk, f, par):
                pe.wait_ge(h_low, blk * FT + f + 1)
                if f == 0:
                    pe.wait_ge(y_ready, blk + 1)
                for i in range(2):
                    for k, (wp, hp) in enumerate(HALVES):
                        last = nc.tensor.matmul(y_ps[:, i, :], hh[:, f, hp, i * P:(i + 1) * P],
                                                wh[:, par, 2, wp, f * C:(f + 1) * C],
                                                start=(f == 0 and i == 0 and k == 0), stop=(f == FT - 1 and k == 2),
                                                skip_group_check=True)
                last.then_inc(down, 1)

            pe.wait_ge(const_in, 64)
            turn_x(0)
            with pe.Fori(0, E // 2) as pair:
                for par in range(2):
                    lo, hi = span(pe, pair * 2 + par)
                    pe.wait_ge(w_low, pair * 2 + (par + 1))
                    pe.sem_inc(passed, 1)
                    with pe.Fori(lo, hi) as blk:
                        for f in range(FT):
                            gate_up(blk, f, par)
                            if f >= 2:
                                down_product(blk, f - 2, par)
                        turn_x(blk + 1)
                        down_product(blk, FT - 2, par)
                        down_product(blk, FT - 1, par)

        @block.scalar
        def _(act):
            def turned_high(blk):
                act.wait_ge(x_turned, blk + 1)
                nc.scalar.activation(xh[:, 0], x_ps[:, :, :], ACT.Copy).then_inc(x_high, 1)

            turned_high(0)
            with act.Fori(0, E // 2) as pair:
                for par in range(2):
                    e = pair * 2 + par
                    lo, hi = span(act, e)
                    act.wait_ge(w_low, e + 1)
                    load_weights(act, d, w, (e + 2) % E, par)
                    act.wait_ge(biases, e + 1)
                    with act.Fori(lo, hi) as blk:
                        for f in range(FT + 1):
                            if f < FT:
                                act.wait_ge(gu_ready, blk * FT + f + 1)
                                nc.scalar.activation(act_out[:, f % 4, :], gu[:, f % 4, 0, :], ACT.Gelu,
                                                     bias=bcur[:, par, 0, f:f + 1]).then_inc(gated, 1)
                            if f >= 1:
                                act.wait_ge(hidden, blk * FT + (f - 1) + 1 + 4)
                                act.wait_ge(down, blk * FT + (f - 1) + 1)
                                nc.scalar.activation(hh[:, f - 1, 0, :], hid[:, (f - 1) % 4, :], ACT.Copy).then_inc(h_high, 1)
                        turned_high(blk + 1)
            for par in range(2):
                act.wait_ge(w_in[par], 48 * (E // 2 + 1))

        @block.gpsimd
        def _(pool):
            with pool.Fori(0, E // 2) as pair:
                for par in range(2):
                    e = pair * 2 + par
                    lo, _ = span(pool, e)
                    pool.wait_ge(down, lo * FT + 8)
                    pool.wait_ge(w_in[1 - par], (pair + (1 + par)) * 48)
                    pool.sem_inc(passed_w, 1)
                    for n in range(3):
                        last = nc.gpsimd.tensor_copy(wh[:, 1 - par, n, 0, :], raw[:, 1 - par, n, :])
                    last.then_inc(w_high, 1)
                    pool.wait_ge(w_high, e + 2)
                    for n in range(3):
                        last = nc.gpsimd.tensor_tensor(wh[:, 1 - par, n, 1, :], raw[:, 1 - par, n, :],
                                                       wh[:, 1 - par, n, 0, :], ALU.subtract)
                    last.then_inc(w_low, 1)

        @block.vector
        def _(dve):
            def turned_low(blk):
                dve.wait_ge(x_high, blk + 1)
                nc.vector.tensor_tensor(xh[:, 1], x_ps[:, :, :], xh[:, 0], ALU.subtract).then_inc(x_low, 1)

            dve.sem_inc(x_low, 1)
            dve.sem_inc(hidden, 4)
            dve.sem_inc(down, 8)
            dve.sem_inc(y_ready, 1)
            dve.sem_inc(y_out, 16)
            dve.wait_ge(const_in, 64)
            turned_low(0)
            with dve.Fori(0, E // 2) as pair:
                for par in range(2):
                    e = pair * 2 + par
                    lo, hi = span(dve, e)
                    nc.vector.tensor_copy(bcur[:, par], ball[:, :, bass.ds(e, 1), :].rearrange("p k a f -> p k (a f)")
                                          ).then_inc(biases, 1)
                    dve.wait_ge(biases, e + 1)
                    dve.sem_inc(passed, 1)
                    with dve.Fori(lo, hi) as blk:
                        for f in range(FT + 1):
                            if f < FT:
                                dve.wait_ge(gated, blk * FT + f + 1)
                                nc.vector.scalar_tensor_tensor(
                                    out=hid[:, f % 4, :], in0=gu[:, f % 4, 1, :], scalar=bcur[:, par, 1, f:f + 1],
                                    in1=act_out[:, f % 4, :], op0=ALU.add, op1=ALU.mult).then_inc(hidden, 1)
                            if f >= 1:
                                dve.wait_ge(h_high, blk * FT + (f - 1) + 1)
                                nc.vector.tensor_tensor(hh[:, f - 1, 1, :], hid[:, (f - 1) % 4, :], hh[:, f - 1, 0, :],
                                                        ALU.subtract).then_inc(h_low, 1)
                        turned_low(blk + 1)
                        dve.wait_ge(down, blk * FT + FT + 8)
                        dve.wait_ge(y_out, blk * 16 + 16)
                        nc.vector.tensor_tensor(yout[:, :, :], y_ps[:, :, :],
                                                b2[:, bass.ds(e, 1), :].to_broadcast([P, 2, C]), ALU.add).then_inc(y_ready, 1)


def stage_combine(nc, d, g, x1, gates, slots, out):
    with ExitStack() as ctx:
        def sb(name, shape, dt):
            return ctx.enter_context(nc.sbuf_tensor(name, shape, dt))

        def sem(name):
            return ctx.enter_context(nc.semaphore(name))

        ya = sb("ya", [P, NT, C], F32)
        yb = sb("yb", [P, NT, C], F32)
        stats = sb("fstats", [P, NT, 6], F32)
        agg = sb("fagg", [P, NT, 2], F32)
        dev = sb("fdev", [P, NT], F32)
        rstd = sb("frstd", [P, NT], F32)
        got = [sem(f"f_got{i}") for i in range(B * NCH)]
        own = sem("f_own")
        spread = sem("f_spread")
        rooted = sem("f_rooted")
        normed = sem("f_normed")
        out_done = sem("f_out_done")
        block = ctx.enter_context(nc.Block())

        @block.gpsimd
        def _(pool):
            for t in range(NT):
                for k, y in enumerate((ya, yb)):
                    pool.indirect_dma_start(out=y[:, t, :], out_offset=None, in_=g["ys"],
                                            in_offset=bass.IndirectOffsetOnAxis(ap=slots[:, k, t:t + 1], axis=0)
                                            ).then_inc(got[t // QT], 16)

        @block.vector
        def _(dve):
            for m in range(B * NCH):
                tiles = range(m * QT, (m + 1) * QT)
                some = slice(m * QT, (m + 1) * QT)
                dve.wait_ge(got[m], 16 * 2 * QT)
                for k, (a, b) in enumerate(((ya, x1), (yb, ya))):
                    for t in tiles:
                        last = nc.vector.scalar_tensor_tensor(out=(ya if k == 0 else yb)[:, t, :], in0=a[:, t, :],
                                                              scalar=gates[:, k, t:t + 1], in1=b[:, t, :],
                                                              op0=ALU.mult, op1=ALU.add)
                    last.then_inc(own, 1)
                    dve.wait_ge(own, 5 * m + k + 1)
                for t in tiles:
                    last = nc.vector.bn_stats(stats[:, t, :], yb[:, t, :])
                last.then_inc(own, 1)
                dve.wait_ge(own, 5 * m + 3)
                for t in tiles:
                    last = nc.vector.bn_aggr(agg[:, t, :], stats[:, t, :])
                last.then_inc(own, 1)
                dve.wait_ge(own, 5 * m + 4)
                nc.vector.tensor_scalar(agg[:, some, 1], agg[:, some, 1], EPS, None, ALU.add).then_inc(spread, 1)
                dve.wait_ge(rooted, m + 1)
                nc.vector.reciprocal(rstd[:, some], dev[:, some]).then_inc(own, 1)
                dve.wait_ge(own, 5 * m + 5)
                for t in tiles:
                    last = nc.vector.tensor_scalar(ya[:, t, :], yb[:, t, :], agg[:, t, 0:1], rstd[:, t:t + 1],
                                                   ALU.subtract, ALU.mult)
                last.then_inc(normed, 1)

        @block.scalar
        def _(act):
            for m in range(B * NCH):
                some = slice(m * QT, (m + 1) * QT)
                act.wait_ge(spread, m + 1)
                nc.scalar.activation(dev[:, some], agg[:, some, 1], ACT.Sqrt).then_inc(rooted, 1)

        @block.sync
        def _(sp):
            n = 0
            for m in range(B * NCH):
                b, c = divmod(m, NCH)
                sp.wait_ge(normed, m + 1)
                for run in place_rows(c):
                    (a, z), (q0, q1), row = run
                    sp.dma_start(rows_of(out, run, b * S + row), ya[a:z, m * QT + q0:m * QT + q1, :]).then_inc(out_done, 16)
                    n += 1
            sp.wait_ge(out_done, 16 * n)


def build(nc, d, out):
    g = scratch(nc)
    with ExitStack() as ctx:
        def sb(name, shape, dt):
            return ctx.enter_context(nc.sbuf_tensor(name, shape, dt))

        x1 = sb("x1", [P, NT, C], F32)
        logits = sb("logits", [P, NT, E], F32)
        gates = sb("gates", [P, 2, NT], F32)
        slots = sb("slots", [P, 2, NT], U32)
        bounds = sb("bounds", [P, 2 * E], I32)
        with ExitStack() as inner:
            def isb(name, shape, dt):
                return inner.enter_context(nc.sbuf_tensor(name, shape, dt))

            ops = {
                "kexp": isb("kexp", [P, QUAD, S], F16),
                "qop": isb("qop", [P, NCH, 3, QUAD, CH], F16),
                "ident": isb("ident", [P, P], F32), "mask": isb("mask", [P, 3 * P], F32),
            }
            stage_project(nc, d, g, ops)
            with nc.sbuf_tensor("heads_out", [P, NCH, QT, NIT + 1, QUAD * DK], F32) as heads_out:
                stage_attention(nc, d, g, ops, heads_out)
                stage_norm(nc, d, g, heads_out, x1, logits)
        with ExitStack() as inner:
            w = {
                "raw": inner.enter_context(nc.sbuf_tensor("raw", [P, 2, 3, CT * F], F32)),
                "half": inner.enter_context(nc.sbuf_tensor("half", [P, 2, 3, 2, CT * F], F16)),
                "in": [inner.enter_context(nc.semaphore(f"w_in{i}")) for i in range(2)],
                "high": inner.enter_context(nc.semaphore("w_high")),
                "low": inner.enter_context(nc.semaphore("w_low")),
            }
            stage_route(nc, d, g, w, x1, logits, gates, slots, bounds)
            stage_experts(nc, d, g, w, bounds)
        stage_combine(nc, d, g, x1, gates, slots, out)


def layouts(i):
    swap = np.arange(C).reshape(H, 2, DK // 2)[:, ::-1].reshape(C)
    x = np.ascontiguousarray(i["L0_attn_x"]).reshape(NTOK, C)
    cols = lambda a: a.reshape(CT, P).T
    u, v = i["L0_attn_u"].reshape(C), i["L0_attn_v"].reshape(C)
    out = {
        "x": x,
        "xT": x.reshape(B * NCH, CH, CT, P).transpose(0, 3, 2, 1),
        "Wq": i["L0_attn_Wq"], "Wqs": i["L0_attn_Wq"][:, swap], "Wk": i["L0_attn_Wk"], "Wv": i["L0_attn_Wv"],
        "Wo": i["L0_attn_Wo"], "bo": i["L0_attn_bo"].reshape(1, C),
        "uv": np.stack([cols(u), cols(v), cols(v[swap])], 1),
        "rw": i["L0_ffn_router_w"].T,
        "w1": i["L0_ffn_w1_w"].transpose(0, 2, 1), "wg": i["L0_ffn_wg_w"].transpose(0, 2, 1),
        "w2": i["L0_ffn_w2_w"].transpose(0, 2, 1),
        "b1": i["L0_ffn_w1_b"].reshape(E, FT, P).transpose(2, 0, 1), "bg": i["L0_ffn_wg_b"].reshape(E, FT, P).transpose(2, 0, 1),
        "b2": i["L0_ffn_w2_b"].reshape(1, E * C),
    }
    out.update(constants())
    return {k: np.ascontiguousarray(a) for k, a in out.items()}


def scratch(nc, kind="Internal"):
    shapes = {"qs": ((6, B * C, W), F16), "ks": ((2, B * C, S), F16), "vs": ((B * NQ * S, P), F32),
              "xs": (((NBLK + 2) * BLK, C), F32), "ys": ((NBLK * BLK, C), F32)}
    return {k: nc.dram_tensor(f"scratch_{k}", s, dt, kind=kind).ap() for k, (s, dt) in shapes.items()}


def kernel(**inputs):
    import concourse.bacc as bacc
    from concourse.bass_utils import run_bass_kernel_spmd

    nc = bacc.Bacc("TRN2", target_bir_lowering=False, num_devices=1)
    arrays = {f"in_{k}": a for k, a in layouts({k: np.asarray(a) for k, a in inputs.items()}).items()}
    d = {k[3:]: nc.dram_tensor(k, a.shape, mybir.dt.from_np(a.dtype), kind="ExternalInput").ap() for k, a in arrays.items()}
    out = nc.dram_tensor("out", (NTOK, C), F32, kind="ExternalOutput").ap()
    build(nc, d, out)
    r = run_bass_kernel_spmd(nc, [arrays], core_ids=[0])
    return r.results[0]["out"].reshape(B, S, C)
```
